# Optimizing a Trainium2 kernel written in Bass

```python
import numpy as np
import jax
import jax.numpy as jnp

def _softmax(x, axis=-1):
    return jax.nn.softmax(x, axis=axis)

def _gelu(x):
    return jax.nn.gelu(x, approximate=True)

def _silu(x):
    return jax.nn.silu(x)

def _sigmoid(x):
    return jax.nn.sigmoid(x)

def _layernorm(x, axis=-1, eps=1e-05):
    m = jnp.mean(x, axis=axis, keepdims=True)
    v = jnp.var(x, axis=axis, keepdims=True)
    return (x - m) / jnp.sqrt(v + eps)

def _scatter_add(tgt, idx, src, axis=0):
    return tgt.at[idx].add(src)

def _segment_sum(src, seg, n):
    return jax.ops.segment_sum(src, seg, n)
kernel_name = 'mk_gnn_preln_d2_gnn_r8_1206c7'

def setup_inputs(seed: int=0):
    np.random.seed(seed)
    _w = jnp.asarray

    def _rec_inputs():
        import jax
        import jax.numpy as jnp
        _gk = jax.random.key(seed)
        x = -0.0003713 + 1 * jax.random.normal(jax.random.fold_in(_gk, 1), (12500, 256), jnp.float32)
        src = jax.random.randint(jax.random.fold_in(_gk, 2), (200000,), 0, 12500, jnp.int32)
        dst = jax.random.randint(jax.random.fold_in(_gk, 3), (200000,), 0, 12500, jnp.int32)
        _o = jnp.argsort(dst, stable=True)
        src = src[_o]
        dst = dst[_o]
        edge_attr_16 = -0.000153872 + 1.00011 * jax.random.normal(jax.random.fold_in(_gk, 12), (200000, 16), jnp.float32)
        edge_attr_4 = 0.0007022 + 0.999661 * jax.random.normal(jax.random.fold_in(_gk, 13), (200000, 4), jnp.float32)
        return (x, src, dst, edge_attr_16, edge_attr_4)
    x, src, dst, edge_attr_16, edge_attr_4 = _rec_inputs()

    def _L0_gnn_setup():
        import jax, jax.numpy as jnp
        import numpy as np
        N, E, C, R, HID = (6250, 62500, 64, 16, 64)
        key = jax.random.key(seed)
        ks = jax.random.split(key, 24)
        g = lambda k, shape, s=1.0: jax.random.normal(k, shape, dtype=jnp.float32) * s
        cs = C ** (-0.5)
        inp = {'h': g(ks[0], (N, 4 * C)), 'edge_index': jax.random.randint(ks[1], (2, E), 0, N), 'edge_sh': g(ks[2], (E, 4)), 'edge_rbf': g(ks[3], (E, R)), 'W_up0': g(ks[4], (C, C), cs), 'W_up1': g(ks[5], (C, C), cs), 'M1': g(ks[6], (R, HID), R ** (-0.5)), 'M2': g(ks[7], (HID, HID), HID ** (-0.5)), 'M3': g(ks[8], (HID, HID), HID ** (-0.5)), 'M4': g(ks[9], (HID, 4 * C), HID ** (-0.5)), 'W_lin0': g(ks[10], (C, C), cs), 'W_lin1': g(ks[11], (C, C), cs), 'Wsc0': g(ks[12], (C, C), cs), 'Wsc1': g(ks[13], (C, C), cs), 'Wc0': g(ks[14], (C, 5)), 'Wc1': g(ks[15], (C, 4)), 'WB0': g(ks[16], (C, C), cs), 'WB1': g(ks[17], (C, C), cs), 'gamma0': jnp.ones((C,), jnp.float32), 'beta0': jnp.zeros((C,), jnp.float32), 'gamma1': jnp.ones((C,), jnp.float32)}
        return inp
    _L0_gnn_all = _L0_gnn_setup()
    _L0_gnn_in = {k: v for k, v in _L0_gnn_all.items() if k in ('W_up0', 'W_up1', 'M1', 'M2', 'M3', 'M4', 'W_lin0', 'W_lin1', 'Wsc0', 'Wsc1', 'Wc0', 'Wc1', 'WB0', 'WB1', 'gamma0', 'beta0', 'gamma1')}
    del _L0_gnn_all

    def _L1_gnn_setup():
        import jax, jax.numpy as jnp
        import numpy as np
        N_NODES = 6250
        N_EDGES = 100000
        IN_FEATS = 256
        OUT_FEATS = 64
        HEADS = 4
        NEG_SLOPE = 0.2
        W_SCALE = 0.05

        def gat_layer(h, src, dst, W, al, ar, b):
            H, F = al.shape
            n = h.shape[0]
            feat = (h @ W).reshape(n, H, F)
            el = jnp.sum(feat * al[None], axis=-1)
            er = jnp.sum(feat * ar[None], axis=-1)
            e = jax.nn.leaky_relu(el[src] + er[dst], NEG_SLOPE)
            m = jax.ops.segment_max(e, dst, num_segments=n)
            ex = jnp.exp(e - m[dst])
            denom = jax.ops.segment_sum(ex, dst, num_segments=n)
            a = ex / denom[dst]
            msg = feat[src] * a[:, :, None]
            out = jax.ops.segment_sum(msg, dst, num_segments=n)
            out = out + b.reshape(1, H, F)
            out = jax.nn.elu(out)
            return out.reshape(n, H * F)
        key = jax.random.key(seed)
        ks = jax.random.split(key, 12)
        h = jax.random.normal(ks[0], (N_NODES, IN_FEATS), dtype=jnp.float32)
        src = jax.random.randint(ks[1], (N_EDGES,), 0, N_NODES, dtype=jnp.int32)
        dst = jax.random.randint(ks[2], (N_EDGES,), 0, N_NODES, dtype=jnp.int32)
        W1 = jax.random.normal(ks[3], (IN_FEATS, HEADS * OUT_FEATS), dtype=jnp.float32) * W_SCALE
        al1 = jax.random.normal(ks[4], (HEADS, OUT_FEATS), dtype=jnp.float32) * W_SCALE
        ar1 = jax.random.normal(ks[5], (HEADS, OUT_FEATS), dtype=jnp.float32) * W_SCALE
        b1 = jnp.zeros((HEADS * OUT_FEATS,), dtype=jnp.float32)
        W2 = jax.random.normal(ks[6], (HEADS * OUT_FEATS, HEADS * OUT_FEATS), dtype=jnp.float32) * W_SCALE
        al2 = jax.random.normal(ks[7], (HEADS, OUT_FEATS), dtype=jnp.float32) * W_SCALE
        ar2 = jax.random.normal(ks[8], (HEADS, OUT_FEATS), dtype=jnp.float32) * W_SCALE
        b2 = jnp.zeros((HEADS * OUT_FEATS,), dtype=jnp.float32)
        return {'h': h, 'src': src, 'dst': dst, 'W1': W1, 'al1': al1, 'ar1': ar1, 'b1': b1, 'W2': W2, 'al2': al2, 'ar2': ar2, 'b2': b2}
    _L1_gnn_all = _L1_gnn_setup()
    _L1_gnn_in = {k: v for k, v in _L1_gnn_all.items() if k in ('W1', 'al1', 'ar1', 'b1', 'W2', 'al2', 'ar2', 'b2')}
    del _L1_gnn_all
    return {'x': x, 'src': src, 'dst': dst, 'edge_attr_16': edge_attr_16, 'edge_attr_4': edge_attr_4, 'L0_gnn_W_up0': _L0_gnn_in['W_up0'], 'L0_gnn_W_up1': _L0_gnn_in['W_up1'], 'L0_gnn_M1': _L0_gnn_in['M1'], 'L0_gnn_M2': _L0_gnn_in['M2'], 'L0_gnn_M3': _L0_gnn_in['M3'], 'L0_gnn_M4': _L0_gnn_in['M4'], 'L0_gnn_W_lin0': _L0_gnn_in['W_lin0'], 'L0_gnn_W_lin1': _L0_gnn_in['W_lin1'], 'L0_gnn_Wsc0': _L0_gnn_in['Wsc0'], 'L0_gnn_Wsc1': _L0_gnn_in['Wsc1'], 'L0_gnn_Wc0': _L0_gnn_in['Wc0'], 'L0_gnn_Wc1': _L0_gnn_in['Wc1'], 'L0_gnn_WB0': _L0_gnn_in['WB0'], 'L0_gnn_WB1': _L0_gnn_in['WB1'], 'L0_gnn_gamma0': _L0_gnn_in['gamma0'], 'L0_gnn_beta0': _L0_gnn_in['beta0'], 'L0_gnn_gamma1': _L0_gnn_in['gamma1'], 'L1_gnn_W1': _L1_gnn_in['W1'], 'L1_gnn_al1': _L1_gnn_in['al1'], 'L1_gnn_ar1': _L1_gnn_in['ar1'], 'L1_gnn_b1': _L1_gnn_in['b1'], 'L1_gnn_W2': _L1_gnn_in['W2'], 'L1_gnn_al2': _L1_gnn_in['al2'], 'L1_gnn_ar2': _L1_gnn_in['ar2'], 'L1_gnn_b2': _L1_gnn_in['b2']}

def reference(x, src, dst, edge_attr_16, edge_attr_4, L0_gnn_W_up0, L0_gnn_W_up1, L0_gnn_M1, L0_gnn_M2, L0_gnn_M3, L0_gnn_M4, L0_gnn_W_lin0, L0_gnn_W_lin1, L0_gnn_Wsc0, L0_gnn_Wsc1, L0_gnn_Wc0, L0_gnn_Wc1, L0_gnn_WB0, L0_gnn_WB1, L0_gnn_gamma0, L0_gnn_beta0, L0_gnn_gamma1, L1_gnn_W1, L1_gnn_al1, L1_gnn_ar1, L1_gnn_b1, L1_gnn_W2, L1_gnn_al2, L1_gnn_ar2, L1_gnn_b2):
    import jax
    import jax.numpy as jnp

    def _L0_gnn_ref(h, edge_index, edge_sh, edge_rbf, W_up0, W_up1, M1, M2, M3, M4, W_lin0, W_lin1, Wsc0, Wsc1, Wc0, Wc1, WB0, WB1, gamma0, beta0, gamma1):
        import jax, jax.numpy as jnp
        import numpy as np
        N, E, C, R, HID = (6250, 62500, 64, 16, 64)
        n = h.shape[0]
        h0 = h[:, :C]
        h1 = h[:, C:].reshape(n, C, 3)
        up0 = h0 @ W_up0
        up1 = jnp.einsum('ncx,cd->ndx', h1, W_up1)
        r = jax.nn.silu(edge_rbf @ M1)
        r = jax.nn.silu(r @ M2)
        r = jax.nn.silu(r @ M3)
        tpw = (r @ M4).reshape(-1, 4, C)
        snd, rcv = (edge_index[0], edge_index[1])
        x0 = up0[snd]
        x1 = up1[snd]
        sh0 = edge_sh[:, 0]
        sh1 = edge_sh[:, 1:]
        inv3 = 1.0 / jnp.sqrt(jnp.float32(3.0))
        m0e = tpw[:, 0] * x0 * sh0[:, None] + tpw[:, 3] * jnp.einsum('ecx,ex->ec', x1, sh1) * inv3
        m1e = tpw[:, 1][:, :, None] * x0[:, :, None] * sh1[:, None, :] + tpw[:, 2][:, :, None] * x1 * sh0[:, None, None]
        msg0 = jax.ops.segment_sum(m0e, rcv, num_segments=n)
        msg1 = jax.ops.segment_sum(m1e, rcv, num_segments=n)
        A0 = msg0 @ W_lin0
        A1 = jnp.einsum('ncx,cd->ndx', msg1, W_lin1)
        sc0 = h0 @ Wsc0
        sc1 = jnp.einsum('ncx,cd->ndx', h1, Wsc1)
        vv = jnp.sum(A1 * A1, -1)
        B0 = Wc0[:, 0] * A0 + Wc0[:, 1] * A0 * A0 + Wc0[:, 2] * vv + Wc0[:, 3] * A0 ** 3 + Wc0[:, 4] * A0 * vv
        B1 = (Wc1[:, 0] + Wc1[:, 1] * A0 + Wc1[:, 2] * A0 * A0 + Wc1[:, 3] * vv)[..., None] * A1
        o0 = B0 @ WB0 + sc0
        o1 = jnp.einsum('ncx,cd->ndx', B1, WB1) + sc1
        eps = jnp.float32(1e-05)
        mu = jnp.mean(o0, 0)
        xc = o0 - mu
        var = jnp.mean(xc * xc, 0)
        n0 = xc * jax.lax.rsqrt(var + eps) * gamma0 + beta0
        nrm1 = jnp.mean(jnp.sum(o1 * o1, -1) / 3.0, 0)
        n1 = o1 * (jax.lax.rsqrt(nrm1 + eps) * gamma1)[None, :, None]
        return jnp.concatenate([n0, n1.reshape(n, 3 * C)], -1)

    def _L1_gnn_ref(h, src, dst, W1, al1, ar1, b1, W2, al2, ar2, b2):
        import jax, jax.numpy as jnp
        import numpy as np
        N_NODES = 6250
        N_EDGES = 100000
        IN_FEATS = 256
        OUT_FEATS = 64
        HEADS = 4
        NEG_SLOPE = 0.2
        W_SCALE = 0.05

        def gat_layer(h, src, dst, W, al, ar, b):
            H, F = al.shape
            n = h.shape[0]
            feat = (h @ W).reshape(n, H, F)
            el = jnp.sum(feat * al[None], axis=-1)
            er = jnp.sum(feat * ar[None], axis=-1)
            e = jax.nn.leaky_relu(el[src] + er[dst], NEG_SLOPE)
            m = jax.ops.segment_max(e, dst, num_segments=n)
            ex = jnp.exp(e - m[dst])
            denom = jax.ops.segment_sum(ex, dst, num_segments=n)
            a = ex / denom[dst]
            msg = feat[src] * a[:, :, None]
            out = jax.ops.segment_sum(msg, dst, num_segments=n)
            out = out + b.reshape(1, H, F)
            out = jax.nn.elu(out)
            return out.reshape(n, H * F)
        h = gat_layer(h, src, dst, W1, al1, ar1, b1)
        h = gat_layer(h, src, dst, W2, al2, ar2, b2)
        return h
    edge_index = jnp.stack([src, dst])
    h = jnp.maximum(_layernorm(x, axis=-1), 0.0)
    x = x + _L0_gnn_ref(h, edge_index, edge_attr_4, edge_attr_16, L0_gnn_W_up0, L0_gnn_W_up1, L0_gnn_M1, L0_gnn_M2, L0_gnn_M3, L0_gnn_M4, L0_gnn_W_lin0, L0_gnn_W_lin1, L0_gnn_Wsc0, L0_gnn_Wsc1, L0_gnn_Wc0, L0_gnn_Wc1, L0_gnn_WB0, L0_gnn_WB1, L0_gnn_gamma0, L0_gnn_beta0, L0_gnn_gamma1)
    h = jnp.maximum(_layernorm(x, axis=-1), 0.0)
    x = x + _L1_gnn_ref(h, src, dst, L1_gnn_W1, L1_gnn_al1, L1_gnn_ar1, L1_gnn_b1, L1_gnn_W2, L1_gnn_al2, L1_gnn_ar2, L1_gnn_b2)
    return x

_drawn_inputs = setup_inputs


def setup_inputs(seed=0):
    import zlib

    import numpy as np

    out = dict(_drawn_inputs(seed))
    spreads = {'L0_gnn_gamma0': (1.0, 0.2),
     'L0_gnn_beta0': (0.0, 0.1),
     'L0_gnn_gamma1': (1.0, 0.2),
     'L1_gnn_b1': (0.0, 0.1),
     'L1_gnn_b2': (0.0, 0.1)}
    factors = {'L1_gnn_al1': 8.0, 'L1_gnn_ar1': 60.555, 'L1_gnn_al2': 64.0, 'L1_gnn_ar2': 196.394}
    for name, (base, spread) in spreads.items():
        noise = np.random.default_rng([zlib.crc32(name.encode()), seed]).standard_normal(out[name].shape)
        drawn = base * np.exp(spread * noise) if base else spread * noise
        out[name] = jnp.asarray(drawn.astype(out[name].dtype))
    for name, factor in factors.items():
        out[name] = (out[name] * factor).astype(out[name].dtype)
    return out
```

```python
from contextlib import ExitStack, contextmanager

import numpy as np
import concourse.bass as bass
from concourse import mybir

F32, I32, BF16 = mybir.dt.float32, mybir.dt.int32, mybir.dt.bfloat16
ALU, ACT = mybir.AluOpType, mybir.ActivationFunctionType
P = 128
N, E, C, H, HID, R = 12500, 200000, 64, 4, 64, 16
D = 4 * C
NT = 100
NP_ = NT * P
NB = 4
NG = NT // NB
W = NB * P
LAST = N - (NG - 1) * W
SBT = 32
SB = -(-E // (SBT * P))
T = SB * SBT
EP = T * P
TG = 14
TP = T // TG
CH = EP // P
GR = D + 2 * H
BIG = 1.0e30
SKIP = float(1 << 22)
EPS = 1e-5
assert T == TG * TP and EP == P * CH and T % 8 == 0


class Signal:

    def __init__(self, sem, per=1, inc=1, ahead=0):
        self.sem, self.per, self.inc, self.base = sem, per, inc, ahead * per * inc

    def at(self, i, k=None):
        k = self.per if k is None else k
        return i * (self.per * self.inc) + (self.base + k * self.inc)

    def wait(self, eng, i, k=None):
        eng.wait_ge(self.sem, self.at(i, k))

    def prime(self, eng):
        eng.sem_inc(self.sem, self.base)


class Turns:

    def __init__(self, sem, pool_sem):
        self.sems = (sem, pool_sem)
        self.base, self.n, self.per, self.i = [0, 0], [0, 0], [0, 0], 0
        self.last = (0,)

    def value(self, s):
        return self.i * self.per[s] + (self.base[s] + self.n[s]) if self.per[s] else self.base[s] + self.n[s]

    def wait(self, eng):
        for s in self.last:
            if self.base[s] + self.n[s] + self.per[s]:
                eng.wait_ge(self.sems[s], self.value(s))
                if self.per[s]:
                    eng.nop(nofuse=True)

    def step(self, eng, *instructions):
        self.wait(eng)
        for make in instructions:
            ins = make()
        ins.then_inc(self.sems[0], 1)
        self.n[0] += 1
        self.last = (0,)

    def dma(self, eng, *instructions, pool=False):
        self.wait(eng)
        for make in instructions:
            make().then_inc(self.sems[pool], 16)
        self.n[pool] += 16 * len(instructions)
        self.last = (int(pool),)

    @contextmanager
    def loop(self, nc, count, per, pool_per=0):
        per = [per, pool_per]
        self.base = [x + y for x, y in zip(self.base, self.n)]
        self.n, self.last = [0, 0], tuple(s for s in (0, 1) if self.base[s])
        with nc.Fori(0, count) as i:
            self.i, self.per = i, per
            yield i
            assert self.n == per, (self.n, per)
        self.base = [x + count * y for x, y in zip(self.base, per)]
        self.n, self.per, self.i, self.last = [0, 0], [0, 0], 0, (0, 1)

    def end(self, nc):
        for eng in (nc.sync, nc.scalar, nc.vector, nc.gpsimd, nc.tensor):
            for s in (0, 1):
                if self.base[s] + self.n[s]:
                    eng.wait_ge(self.sems[s], self.value(s))
        nc.all_engine_barrier()


def bc(ap, dim, shape):
    return ap.unsqueeze(dim).to_broadcast(shape)


class Shared:
    pass


def program(nc, a, out):
    q = Shared()
    q.a, q.out = a, out
    q.top = top = ExitStack()
    with top:
        seen = {}

        def unique(name):
            seen[name] = seen.get(name, 0) + 1
            return f"{name}_{seen[name]}"

        def sb(ctx, name, shape, dt=F32):
            return ctx.enter_context(nc.sbuf_tensor(unique(name), shape, dt))

        def pb(ctx, name, shape, dt=F32):
            return ctx.enter_context(nc.psum_tensor(unique(name), shape, dt))

        def sem(name):
            return top.enter_context(nc.semaphore(name))

        def dram(name, shape, dt=F32):
            return nc.dram_tensor(name, shape, dt, kind="Internal").ap()

        q.V, q.S, q.G, q.TE, q.SP = nc.vector, nc.scalar, nc.gpsimd, nc.tensor, nc.sync
        q.sb, q.pb, q.sem = sb, pb, sem

        q.table0 = dram("table0", (NP_, D))
        q.table1 = dram("table1", (NP_, D + H))
        q.hT_d = dram("hT_d", (C, 4, NP_))
        q.oT_d = dram("oT_d", (C, 4, NP_))
        q.x1_d = dram("x1_d", (NP_, D))
        q.er_d = dram("er_d", (NP_, H))
        q.sums0_x = dram("sums0", (4 * P + EP, D))
        q.sums0 = q.sums0_x[4 * P:, :]
        q.spare = 4 * P * D
        q.sums1 = dram("sums1", (EP, GR))
        q.er_start = dram("er_start", (EP, H))
        q.er_edge = dram("er_edge", (H, EP))

        q.iota_f = sb(top, "iota_f", [P, P])
        q.ident = sb(top, "ident", [P, P])
        q.upper = sb(top, "upper", [P, P])
        q.lastpos = sb(top, "lastpos", [P, T])
        q.whole = sb(top, "whole", [P, T])
        q.start_f = sb(top, "start_f", [P, SB, P], BF16)
        q.start_b = sb(top, "start_b", [P, SB, P], BF16)
        q.samep = sb(top, "samep", [P, CH])
        q.chunk_node = sb(top, "chunk_node", [P, 1], I32)
        q.head_idx = sb(top, "head_idx", [TP, TG], I32)
        q.fix_idx = sb(top, "fix_idx", [TP, TG], I32)
        q.row_idx = sb(top, "row_idx", [P, P], I32)
        q.first_idx = sb(top, "first_idx", [P, P], I32)
        q.some = sb(top, "some", [P, P])
        q.eps_c = sb(top, "eps_c", [P, 1])
        q.stat = sb(top, "stat", [C, 4])

        structure(nc, q)
        layer0_nodes(nc, q)
        layer0_edges(nc, q)
        stitch(nc, q, q.sums0, D, "s0")
        layer0_update(nc, q)
        layer0_norm_and_gat_nodes(nc, q)
        for n in (1, 2):
            spread_er(nc, q, n)
            gat_edges(nc, q, n)
            stitch(nc, q, q.sums1, GR, f"s{n}")
            gat_output(nc, q, n)


def structure(nc, q):
    V, S, G, TE, SP, a, sb, pb = q.V, q.S, q.G, q.TE, q.SP, q.a, q.sb, q.pb
    t = Turns(q.sem("t_struct"), q.sem("t_struct_pool"))
    line = a["dst_line"]
    with ExitStack() as c:
        ii = sb(c, "ii", [P, P], I32)
        t.step(G, lambda: G.iota(ii[:, :], pattern=[[1, P]], base=0, channel_multiplier=0))
        t.step(V, lambda: V.tensor_copy(q.iota_f[:, :], ii[:, :]))
        t.step(G, lambda: G.memset(q.ident[:, :], 0.0))
        t.step(G, lambda: G.affine_select(out=q.ident[:, :], in_=q.ident[:, :], compare_op=ALU.not_equal,
                                          fill=1.0, base=0, pattern=[[-1, P]], channel_multiplier=1))
        t.step(G, lambda: G.memset(q.upper[:, :], 1.0))
        t.step(G, lambda: G.affine_select(out=q.upper[:, :], in_=q.upper[:, :], compare_op=ALU.is_gt,
                                          fill=0.0, base=0, pattern=[[1, P]], channel_multiplier=-1))
        t.step(V, lambda: V.memset(q.eps_c[:, :], EPS))

    with ExitStack() as c:
        d, dp, dn = (sb(c, n, [TP, TG, P], I32) for n in ("d", "dp", "dn"))
        same, pos, lp = (sb(c, n, [TP, TG, P]) for n in ("same", "pos", "lp"))
        wh, link, fi = (sb(c, n, [TP, TG]) for n in ("wh", "link", "fi"))
        fi_i = sb(c, "fi_i", [TP, TG], I32)
        ps = pb(c, "ps_s", [P, 4, P])
        view = lambda o: line[o:o + EP].rearrange("(g p e) -> p g e", p=TP, e=P)
        t.dma(SP, lambda: SP.dma_start(dp[:, :, :], view(0)), lambda: SP.dma_start(d[:, :, :], view(1)),
              lambda: SP.dma_start(dn[:, :, :], view(2)))
        t.step(V, lambda: V.tensor_tensor(same[:, :, :], d[:, :, :], dn[:, :, :], ALU.is_equal))
        t.step(V, lambda: V.memset(same[:, :, P - 1:P], 0.0))
        t.step(V, lambda: V.tensor_scalar(pos[:, :, :], same[:, :, :], -1.0, 1.0, ALU.mult, ALU.add))
        t.step(V, lambda: V.tensor_tensor(pos[:, :, :], pos[:, :, :], bc(q.iota_f[:TP, :], 1, [TP, TG, P]), ALU.mult))
        flat = lambda x: x[:, :, :].rearrange("p g e -> p (g e)")[:, ::-1]
        t.step(V, lambda: V.tensor_tensor_scan(flat(lp), flat(same), flat(pos), 0.0, ALU.mult, ALU.add))
        t.step(V, lambda: V.tensor_tensor(wh[:, :].unsqueeze(2), dp[:, :, 0:1], d[:, :, P - 1:P], ALU.is_equal))
        t.step(V, lambda: V.tensor_tensor(link[:, :].unsqueeze(2), dp[:, :, 0:1], d[:, :, 0:1], ALU.is_equal))
        t.step(G, lambda: G.iota(fi_i[:, :], pattern=[[TP * P, TG]], base=0, channel_multiplier=P))
        t.step(V, lambda: V.tensor_copy(fi[:, :], fi_i[:, :]))
        t.step(V, lambda: V.tensor_tensor(fi[:, :].unsqueeze(2), fi[:, :].unsqueeze(2), lp[:, :, 0:1], ALU.add))
        t.step(V, lambda: V.tensor_copy(q.head_idx[:, :], fi[:, :]))
        t.step(V, lambda: V.tensor_scalar(link[:, :], link[:, :], -SKIP, SKIP, ALU.mult, ALU.add))
        t.step(V, lambda: V.tensor_tensor(fi[:, :], fi[:, :], link[:, :], ALU.add))
        t.step(V, lambda: V.tensor_copy(q.fix_idx[:, :], fi[:, :]))
        t.step(V, lambda: V.tensor_copy(same[:, :, :], bc(wh[:, :], 2, [TP, TG, P])))
        for src, dst in ((lp, q.lastpos), (same, q.whole)):
            for g0 in range(0, TG, 4):
                gs = range(g0, min(g0 + 4, TG))
                t.step(TE, *[lambda g=g, src=src: TE.transpose(ps[:, g % 4, 0:TP], src[:, g, :], q.ident[:TP, :TP])
                             for g in gs])
                t.step(V, lambda dst=dst, g0=g0, gs=gs: V.tensor_copy(
                    dst[:, g0 * TP:(g0 + len(gs)) * TP].rearrange("p (g t) -> p g t", t=TP), ps[:, 0:len(gs), 0:TP]))

    with ExitStack() as c:
        m0, m1 = (sb(c, n, [P, SB, P], I32) for n in ("m0", "m1"))
        eq = sb(c, "eq", [P, SB, P], BF16)
        view = lambda o: line[o:o + EP].rearrange("(s t e) -> t s e", t=SBT, e=P)
        load = lambda m, o: [lambda h=h: SP.dma_start(m[h * SBT:(h + 1) * SBT, :, :], view(o)) for h in range(H)]
        t.dma(SP, *load(m0, 1))
        for o, mask in ((0, q.start_f), (2, q.start_b)):
            t.dma(SP, *load(m1, o))
            t.step(V, lambda mask=mask: V.tensor_tensor(eq[:, :, :], m0[:, :, :], m1[:, :, :], ALU.is_equal))
            t.step(V, lambda mask=mask: V.tensor_scalar(mask[:, :, :], eq[:, :, ::1 - o], BIG, -BIG, ALU.mult, ALU.add))

    with ExitStack() as c:
        c0, c1 = (sb(c, n, [P, CH], I32) for n in ("c0", "c1"))
        t.dma(SP, lambda: SP.dma_start(c0[:, :], line[1:1 + EP].rearrange("(p e) -> p e", p=P)),
              lambda: SP.dma_start(c1[:, :], line[0:EP].rearrange("(p e) -> p e", p=P)))
        t.step(V, lambda: V.tensor_tensor(q.samep[:, :], c0[:, :], c1[:, :], ALU.is_equal))
        t.step(V, lambda: V.tensor_copy(q.chunk_node[:, :], c0[:, 0:1]))
        z = sb(c, "z", [P, CH * H])
        t.step(V, lambda: V.memset(z[:, :], 0.0))
        t.dma(SP, lambda: SP.dma_start(q.er_start.rearrange("(p e) h -> p (e h)", p=P), z[:, :]))

    with ExitStack() as c:
        dc = sb(c, "dc", [P, T], I32)
        hi_i, lo_i = (sb(c, n, [P, T], I32) for n in ("hi_i", "lo_i"))
        hi, lo = (sb(c, n, [P, T]) for n in ("hi", "lo"))
        oh = sb(c, "oh", [P, 2, 2, 8, P], BF16)
        zero = sb(c, "zero", [P, P], BF16)
        cnt, cum, beg, non = (sb(c, n, [P, P]) for n in ("cnt", "cum", "beg", "non"))
        hist = pb(c, "hist", [P, P])
        pre = pb(c, "pre", [P, 1])
        tr = pb(c, "tr", [P, 3, P])
        t.dma(SP, lambda: SP.dma_start(dc[:, :], a["dst_cols"]))
        t.step(V, lambda: V.tensor_scalar(hi_i[:, :], dc[:, :], 7, None, ALU.logical_shift_right),
               lambda: V.tensor_scalar(lo_i[:, :], dc[:, :], 127, None, ALU.bitwise_and))
        t.step(V, lambda: V.tensor_copy(hi[:, :], hi_i[:, :]), lambda: V.tensor_copy(lo[:, :], lo_i[:, :]),
               lambda: V.memset(zero[:, :], 0.0))
        t.step(TE, lambda: TE.matmul(hist[:, :], zero[:, :], zero[:, :], start=True, stop=False))
        t.end(nc)
        made = Signal(q.sem("hist_made"), per=2)
        used = Signal(q.sem("hist_used"), per=2, ahead=1)
        with nc.Block() as block:
            @block.vector
            def _(eng):
                with eng.Fori(0, T // 16) as i:
                    for b in range(2):
                        used.wait(eng, i - 1, b + 1)
                        for n, v in enumerate((hi, lo)):
                            ins = eng.tensor_tensor(oh[:, b, n, :, :], bc(v[:, bass.ds(i * 16 + b * 8, 8)], 2, [P, 8, P]),
                                                    bc(q.iota_f[:, :], 1, [P, 8, P]), ALU.is_equal)
                        ins.then_inc(made.sem, 1)

            @block.tensor
            def _(eng):
                used.prime(eng)
                with eng.Fori(0, T // 16) as i:
                    for b in range(2):
                        made.wait(eng, i, b + 1)
                        for k in range(8):
                            ins = eng.matmul(hist[:, :], oh[:, b, 0, k, :], oh[:, b, 1, k, :], start=False, stop=False)
                        ins.then_inc(used.sem, 1)
                eng.matmul(hist[:, :], zero[:, :], zero[:, :], start=False, stop=True).then_inc(used.sem, 1)
        V.wait_ge(used.sem, used.at(T // 16 - 1) + 1)
        t.step(V, lambda: V.tensor_copy(cnt[:, :], hist[:, :]))
        t.step(V, lambda: V.memset(beg[:, :], 0.0))
        t.step(V, lambda: V.tensor_tensor_scan(cum[:, :], cnt[:, :], beg[:, :], 0.0, ALU.add, ALU.add))
        t.step(TE, lambda: TE.matmul(pre[:, :], q.upper[:, :], cum[:, P - 1:P], start=True, stop=True))
        t.step(V, lambda: V.tensor_scalar(cum[:, :], cum[:, :], pre[:, 0:1], -1.0, ALU.add, ALU.add))
        t.step(V, lambda: V.tensor_tensor(beg[:, :], cum[:, :], cnt[:, :], ALU.subtract))
        t.step(V, lambda: V.tensor_scalar(non[:, :], cnt[:, :], 0.0, SKIP, ALU.is_equal, ALU.mult))
        t.step(V, lambda: V.scalar_tensor_tensor(beg[:, :], beg[:, :], 1.0, non[:, :], ALU.add, ALU.add))
        t.step(V, lambda: V.tensor_scalar(non[:, :], cnt[:, :], 0.0, None, ALU.is_gt))
        t.step(V, lambda: V.tensor_scalar(cum[:, :], cum[:, :], 0.0, None, ALU.max))
        t.step(TE, *[lambda k=k, m=m: TE.transpose(tr[:, k, :], m[:, :], q.ident[:, :])
                     for k, m in enumerate((cum, beg, non))])
        t.step(V, lambda: V.tensor_copy(q.row_idx[:, :], tr[:, 0, :]),
               lambda: V.tensor_copy(q.first_idx[:, :], tr[:, 1, :]),
               lambda: V.tensor_copy(q.some[:, :], tr[:, 2, :]))
        t.end(nc)


def norm_rows(t, V, S, q, x, z, st, mv, rs):
    for k in range(NB):
        t.step(V, lambda k=k: V.bn_stats(st[:, k, :], x[:, k, :]))
    t.step(V, *[lambda k=k: V.bn_aggr(mv[:, k, :], st[:, k, :]) for k in range(NB)])
    t.step(S, lambda: S.activation(rs[:, :].unsqueeze(2), mv[:, :, 1:2], ACT.Sqrt, bias=q.eps_c[:, 0:1]))
    t.step(V, lambda: V.reciprocal(rs[:, :], rs[:, :]))
    t.step(V, *[lambda k=k: V.tensor_scalar(z[:, k, :], x[:, k, :], mv[:, k, 0:1], rs[:, k:k + 1],
                                            ALU.subtract, ALU.mult) for k in range(NB)])


NORM_TURNS = NB + 4


def layer0_nodes(nc, q):
    V, S, G, TE, SP, a, sb, pb = q.V, q.S, q.G, q.TE, q.SP, q.a, q.sb, q.pb
    t = Turns(q.sem("t_nodes0"), q.sem("t_nodes0_pool"))
    with ExitStack() as c:
        x, z = (sb(c, n, [P, NB, D]) for n in ("x", "z"))
        st, mv, rs = sb(c, "st", [P, NB, 6]), sb(c, "mv", [P, NB, 2]), sb(c, "rs", [P, NB])
        wup = sb(c, "wup", [C, 2, C])
        hT = sb(c, "hT", [C, 4, W])
        up = sb(c, "up", [P, NB, D])
        pT = [pb(c, f"pT{k}", [C, 4, P]) for k in range(4)]
        pU = [pb(c, f"pU{k}", [P, 4, C]) for k in range(4)]
        t.dma(SP, lambda: SP.dma_start(wup[:, 0, :], a["L0_gnn_W_up0"]),
              lambda: SP.dma_start(wup[:, 1, :], a["L0_gnn_W_up1"]))
        xin = a["x"].rearrange("(i k p) d -> i p k d", k=NB, p=P)
        with t.loop(nc, NG, 16 + NORM_TURNS + 4 + 32) as i:
            t.dma(SP, lambda: SP.dma_start(x[:, :, :], xin[i, :, :, :]))
            norm_rows(t, V, S, q, x, z, st, mv, rs)
            t.step(TE, *[lambda k=k, pl=pl: TE.transpose(pT[k][:, pl, :], plane(z, k, pl), q.ident[:, :])
                         for k in range(NB) for pl in range(4)])
            t.step(S, *[lambda k=k: S.activation(hT[:, :, k * P:(k + 1) * P], pT[k][:, :, :], ACT.Relu)
                        for k in range(NB)])
            t.step(TE, *[lambda k=k, pl=pl: TE.matmul(pU[k][:, pl, :], hT[:, pl, k * P:(k + 1) * P],
                                                      wup[:, min(pl, 1), :], start=True, stop=True)
                         for k in range(NB) for pl in range(4)])
            t.step(V, *[lambda k=k: V.tensor_copy(up[:, k, :], pU[k][:, :, :].rearrange("p a b -> p (a b)"))
                        for k in range(NB)])
            t.dma(SP, lambda: SP.dma_start(q.table0.rearrange("(i k p) d -> i p k d", k=NB, p=P)[i, :, :, :], up[:, :, :]),
                  lambda: SP.dma_start(q.hT_d[:, :, bass.ds(i * W, W)], hT[:, :, :]))
        t.end(nc)


def plane(z, k, pl):
    return z[:, k, 0:C] if pl == 0 else z[:, k, C + pl - 1:D:3]


def layer0_edges(nc, q):
    a, sb, pb = q.a, q.sb, q.pb
    B = 4
    with ExitStack() as c:
        m1 = sb(c, "m1", [2 * R, 2 * HID])
        m23 = sb(c, "m23", [2 * HID, 2, 2 * HID])
        m4 = sb(c, "m4", [2 * HID, D])
        at = sb(c, "at", [2 * R, B, W])
        sh = sb(c, "sh", [P, B, 8, 4])
        ix = sb(c, "ix", [P, B, 8], I32)
        gb = sb(c, "gb", [P, B, 8, 4, C])
        r = sb(c, "r", [P, 2, W])
        r3 = sb(c, "r3", [P, 2, W])
        t02 = sb(c, "t02", [P, 2, 4, 2, C])
        sel = sb(c, "sel", [P, 2, 4, P])
        msg = sb(c, "msg", [P, 2, 4, 4, C])
        tmp = sb(c, "tmp", [P, 4, 3, C])
        qd = sb(c, "qd", [P, 4, C])
        p1 = sb(c, "p1", [P, 4, C])
        ost = sb(c, "ost", [P, 2, 4, D])
        pm = [pb(c, f"pm{k}", [P, W]) for k in range(2)]
        pt = [pb(c, f"pt{k}", [P, 4, D]) for k in range(2)]
        po = pb(c, "po", [P, 4, D])

        t = Turns(q.sem("t_w0"), q.sem("t_w0_pool"))
        V, SP, S = q.V, q.SP, q.S
        t.step(V, lambda: V.memset(m1[:, :], 0.0), lambda: V.memset(m23[:, :, :], 0.0))
        t.dma(SP, *[lambda g=g: SP.dma_start(m1[g * R:(g + 1) * R, g * HID:(g + 1) * HID], a["L0_gnn_M1"]) for g in range(2)],
              *[lambda g=g, n=n: SP.dma_start(m23[g * HID:(g + 1) * HID, n, g * HID:(g + 1) * HID], a[f"L0_gnn_M{n + 2}"])
                for g in range(2) for n in range(2)],
              *[lambda g=g: SP.dma_start(m4[g * HID:(g + 1) * HID, :], a["L0_gnn_M4"]) for g in range(2)])
        t.step(V, lambda: V.tensor_scalar(m4[:, 3 * C:D], m4[:, 3 * C:D], float(np.float32(1.0) / np.sqrt(np.float32(3.0))), None, ALU.mult))
        t.end(nc)


        s_at = [Signal(q.sem(f"at{g}"), inc=16) for g in range(B)]
        s_at[0].base = 16
        s_sh = [Signal(q.sem(f"sh{g}"), inc=16) for g in range(B)]
        s_ix = [Signal(q.sem(f"ix{g}"), inc=16) for g in range(B)]
        s_g = [Signal(q.sem(f"g{g}"), per=8, inc=16) for g in range(B)]
        s_mm = Signal(q.sem("mm"), per=3 * B)
        s_si = Signal(q.sem("si"), per=3 * B)
        s_mm.base = s_si.base = 3
        s_t = Signal(q.sem("t"), per=2 * B)
        s_ts = Signal(q.sem("ts"), per=2 * B)
        s_msg = Signal(q.sem("msg"), per=2 * B, ahead=1)
        s_sum = Signal(q.sem("sum"), per=2 * B, ahead=1)
        s_ev = Signal(q.sem("ev"), per=2 * B, ahead=1)
        s_st = [Signal(q.sem(f"st{k}"), per=B, inc=16, ahead=1) for k in range(2)]
        dv = Signal(q.sem("dv"), per=2 * B * 8)
        out_v = q.sums0_x.rearrange("(b j p) c -> b p j c", j=4, p=P)

        with nc.Block() as block:
            @block.sync
            def _(eng):
                for s in s_st:
                    s.prime(eng)
                eng.dma_start(at[:, 0, :], a["rbf"][0, :, :]).then_inc(s_at[0].sem, 16)
                eng.wait_ge(s_mm.sem, 1)

                def store(i, k):
                    s_ev.wait(eng, i, k)
                    eng.nop(nofuse=True)
                    eng.dma_start(out_v[i * (2 * B) + (k - 1), :, :, :], ost[:, k % 2, :, :]).then_inc(s_st[k % 2].sem, 16)

                with eng.Fori(0, SB) as i:
                    for g in range(B):
                        s_msg.wait(eng, i - 1, 2 * g + 2)
                        eng.nop(nofuse=True)
                        eng.dma_start(ix[:, g, :], a["src_cols"][i * B + g, :, :]).then_inc(s_ix[g].sem, 16)
                        eng.dma_start(sh[:, g, :, :].rearrange("p t k -> p (t k)"), a["sh"][i * B + g, :, :]).then_inc(s_sh[g].sem, 16)
                        eng.dma_start(at[:, (g + 1) % B, :], a["rbf"][i * B + (g + 1), :, :]).then_inc(s_at[(g + 1) % B].sem, 16)
                    for k in range(1, 2 * B + 1):
                        store(i, k)
                store(SB - 1, 2 * B + 1)
                s_st[0].wait(eng, SB - 1)
                s_st[1].wait(eng, SB - 1, B + 1)

            @block.gpsimd
            def _(eng):
                with eng.Fori(0, SB) as i:
                    for g in range(B):
                        s_ix[g].wait(eng, i)
                        s_msg.wait(eng, i - 1, 2 * g + 2)
                        eng.nop(nofuse=True)
                        for j in range(8):
                            eng.indirect_dma_start(out=gb[:, g, j, :, :].rearrange("p a c -> p (a c)"), out_offset=None,
                                                   in_=q.table0[:, :],
                                                   in_offset=bass.IndirectOffsetOnAxis(ap=ix[:, g, j:j + 1], axis=0)).then_inc(s_g[g].sem, 16)

            @block.tensor
            def _(eng):
                s_sum.prime(eng)

                def mlp(n, g, parity):
                    lhsT, rhs = ((m1[:, :], at[:, g, :]), (m23[:, 0, :], r[:, 0, :]), (m23[:, 1, :], r[:, 1, :]))[n]
                    eng.matmul(pm[parity][:, :], lhsT, rhs, start=True, stop=True).then_inc(s_mm.sem, 1)

                def paths(g, half):
                    for j in range(4):
                        h0 = HID * half
                        ins = eng.matmul(pt[half][:, j, :], r3[h0:h0 + HID, g % 2, j * P:(j + 1) * P],
                                         m4[h0:h0 + HID, :], start=True, stop=True)
                    ins.then_inc(s_t.sem, 1)

                def sums(i, k):
                    s_msg.wait(eng, i, k - 1)
                    s_ev.wait(eng, i, k - 1)
                    for j in range(4):
                        ins = eng.matmul(po[:, j, :], sel[:, (k - 1) % 2, j, :], msg[:, (k - 1) % 2, j, :, :].rearrange("p a c -> p (a c)"),
                                         start=True, stop=True)
                    ins.then_inc(s_sum.sem, 1)

                eng.wait_ge(s_at[0].sem, 16)
                for n in range(3):
                    if n:
                        eng.wait_ge(s_si.sem, n)
                    mlp(n, 0, n % 2 == 0)
                with eng.Fori(0, SB) as i:
                    for g in range(B):
                        x = 3 * g
                        s_at[(g + 1) % B].wait(eng, i)
                        s_si.wait(eng, i, x)
                        mlp(0, (g + 1) % B, x % 2)
                        s_msg.wait(eng, i, 2 * g - 1)
                        paths(g, 0)
                        s_si.wait(eng, i, x + 1)
                        mlp(1, (g + 1) % B, (x + 1) % 2)
                        sums(i, 2 * g + 1)
                        s_si.wait(eng, i, x + 2)
                        mlp(2, (g + 1) % B, x % 2)
                        s_msg.wait(eng, i, 2 * g)
                        paths(g, 1)
                        sums(i, 2 * g + 2)
                sums(SB - 1, 2 * B + 1)

            @block.scalar
            def _(eng):
                s_ev.prime(eng)

                def silu(n, g, parity):
                    dst = (r[:, 0, :], r[:, 1, :], r3[:, g % 2, :])[n]
                    eng.activation(dst, pm[parity][:, :], ACT.Silu).then_inc(s_si.sem, 1)

                def scaled(i, g, half):
                    k = 2 * g + 1 + half
                    s_t.wait(eng, i, k)
                    s_msg.wait(eng, i, k - 2)
                    for j in range(4):
                        ins = eng.activation(t02[:, half, j, :, :],
                                             pt[half][:, j, :].rearrange("p (a c) -> p a c", c=C)[:, 0:3:2, :],
                                             ACT.Copy, scale=sh[:, g, 4 * half + j, 0:1])
                    ins.then_inc(s_ts.sem, 1)

                def evac(i, k):
                    s_sum.wait(eng, i, k)
                    s_st[k % 2].wait(eng, i, (k + 1) // 2 - 1)
                    for j in (0, 2):
                        ins = eng.activation(ost[:, k % 2, j:j + 2, :], po[:, j:j + 2, :], ACT.Copy)
                    ins.then_inc(s_ev.sem, 1)

                for n in range(3):
                    eng.wait_ge(s_mm.sem, n + 1)
                    silu(n, 0, n % 2 == 0)
                with eng.Fori(0, SB) as i:
                    for g in range(B):
                        x = 3 * g
                        s_mm.wait(eng, i, x + 1)
                        silu(0, g + 1, x % 2)
                        s_sh[g].wait(eng, i)
                        scaled(i, g, 0)
                        s_mm.wait(eng, i, x + 2)
                        silu(1, g + 1, (x + 1) % 2)
                        evac(i, 2 * g + 1)
                        s_mm.wait(eng, i, x + 3)
                        silu(2, g + 1, x % 2)
                        scaled(i, g, 1)
                        evac(i, 2 * g + 2)
                evac(SB - 1, 2 * B + 1)

            @block.vector
            def _(eng):
                eng.memset(sel[:, 0, :, :], 0.0)
                eng.memset(msg[:, 0, :, :, :], 0.0).then_inc(s_msg.sem, s_msg.base)
                with eng.Fori(0, SB) as i:
                    n = 0

                    def own(ins):
                        nonlocal n
                        n += 1
                        ins.then_inc(dv.sem, 1)
                        return n

                    for k in range(1, 2 * B + 1):
                        g, half, b = (k - 1) // 2, (k - 1) % 2, k % 2
                        ts = slice(4 * half, 4 * half + 4)
                        x0 = gb[:, g, ts, 0, :]
                        x1 = gb[:, g, ts, 1:4, :]
                        s1 = bc(sh[:, g, ts, 1:4], 3, [P, 4, 3, C])
                        w = pt[half][:, :, :].rearrange("p t (a c) -> p t a c", c=C)
                        s_sum.wait(eng, i, k - 1)
                        eng.tensor_tensor(sel[:, b, :, :], bc(q.lastpos[:, bass.ds(i * SBT + 4 * (k - 1), 4)], 2, [P, 4, P]),
                                          bc(q.iota_f[:, :], 1, [P, 4, P]), ALU.is_equal)
                        if half == 0:
                            s_g[g].wait(eng, i)
                            s_sh[g].wait(eng, i)
                        s_msg.wait(eng, i, k - 1)
                        k1 = own(eng.tensor_tensor(tmp[:, :, :, :], x1, s1, ALU.mult))
                        dv.wait(eng, i, k1)
                        k2 = own(eng.tensor_tensor(qd[:, :, :], tmp[:, :, 0, :], tmp[:, :, 1, :], ALU.add))
                        dv.wait(eng, i, k2)
                        k3 = own(eng.tensor_tensor(qd[:, :, :], qd[:, :, :], tmp[:, :, 2, :], ALU.add))
                        s_ts.wait(eng, i, k)
                        k4 = own(eng.tensor_tensor(p1[:, :, :], x0, w[:, :, 1, :], ALU.mult))
                        dv.wait(eng, i, k3)
                        k5 = own(eng.tensor_tensor(qd[:, :, :], qd[:, :, :], w[:, :, 3, :], ALU.mult))
                        dv.wait(eng, i, k4)
                        k6 = own(eng.tensor_tensor(msg[:, b, :, 1:4, :], bc(p1[:, :, :], 2, [P, 4, 3, C]), s1, ALU.mult))
                        k7 = own(eng.tensor_tensor(tmp[:, :, :, :], x1, bc(t02[:, half, :, 1, :], 2, [P, 4, 3, C]), ALU.mult))
                        k8 = own(eng.tensor_tensor(msg[:, b, :, 0, :], x0, t02[:, half, :, 0, :], ALU.mult))
                        dv.wait(eng, i, k7)
                        eng.tensor_tensor(msg[:, b, :, 1:4, :], msg[:, b, :, 1:4, :], tmp[:, :, :, :], ALU.add)
                        dv.wait(eng, i, k8)
                        eng.tensor_tensor(msg[:, b, :, 0, :], msg[:, b, :, 0, :], qd[:, :, :], ALU.add).then_inc(s_msg.sem, 1)
                    assert n == dv.per


def stitch(nc, q, sums, cw, name):
    V, S, G, TE, SP, sb, pb = q.V, q.S, q.G, q.TE, q.SP, q.sb, q.pb
    gat = cw > D
    base, skip = (sums, 0) if gat else (q.sums0_x, q.spare)
    t = Turns(q.sem("t_" + name), q.sem("t_" + name + "_pool"))
    CK = T // 4
    with ExitStack() as c:
        tl, hd, cp = (sb(c, f"{n}_{name}", [TP, TG, cw]) for n in ("tl", "hd", "cp"))
        tT = sb(c, "tT_" + name, [P, 2, T])
        cb = sb(c, "cb_" + name, [P, 2, 1 + T])
        ps = [pb(c, f"ps{k}_{name}", [P, 4, P]) for k in range(2)]
        t.dma(SP, lambda: SP.dma_start(tl[:, :, :], sums.rearrange("(g p e) c -> p g e c", p=TP, e=P)[:, :, P - 1, :]))
        t.dma(G, pool=True, *[lambda g=g: G.indirect_dma_start(out=hd[:, g, :], out_offset=None, in_=base,
                   element_offset=skip, in_offset=bass.IndirectOffsetOnAxis(ap=q.head_idx[:, g:g + 1], axis=0)) for g in range(TG)])
        for g in range(TG):
            t.step(TE, *[lambda j=j, g=g: TE.transpose(ps[0][:, j, 0:TP], tl[:, g, j * P:(j + 1) * P], q.ident[:TP, :TP])
                         for j in range(2)])
            t.step(V, lambda g=g: V.tensor_copy(tT[:, :, g * TP:(g + 1) * TP], ps[0][:, 0:2, 0:TP]))
        t.step(V, lambda: V.memset(cb[:, :, 0:1], 0.0))
        if gat:
            dT, mT, al, gm = (sb(c, f"{n}_{name}", [H, T]) for n in ("dT", "mT", "al", "gm"))
            cd, cm = (sb(c, f"{n}_{name}", [H, 1 + T]) for n in ("cd", "cm"))
            gB = sb(c, "gB_" + name, [P, T])
            hs = sb(c, "hs_" + name, [H, D])
            for g in range(TG):
                t.step(TE, *[lambda j=j, g=g: TE.transpose(ps[1][:H, j, 0:TP], tl[:, g, D + j * H:D + (j + 1) * H], q.ident[:TP, :TP])
                             for j in range(2)])
                t.step(V, lambda g=g: V.tensor_copy(dT[:, g * TP:(g + 1) * TP], ps[1][:H, 0, 0:TP]),
                       lambda g=g: V.tensor_copy(mT[:, g * TP:(g + 1) * TP], ps[1][:H, 1, 0:TP]))
            t.step(V, lambda: V.tensor_scalar(gm[:, :], q.whole[:H, :], BIG, -BIG, ALU.mult, ALU.add),
                   lambda: V.memset(cd[:, 0:1], 0.0), lambda: V.memset(cm[:, 0:1], -BIG))
            t.step(V, lambda: V.tensor_tensor_scan(cm[:, 1:], gm[:, :], mT[:, :], -BIG, ALU.add, ALU.max))
            t.step(V, lambda: V.tensor_tensor(al[:, :], mT[:, :], cm[:, 1:], ALU.subtract),
                   lambda: V.tensor_tensor(gm[:, :], cm[:, 0:T], cm[:, 1:], ALU.subtract))
            t.step(V, lambda: V.tensor_scalar(gm[:, :], gm[:, :], 0.0, None, ALU.min))
            t.step(S, lambda: S.activation(al[:, :], al[:, :], ACT.Exp), lambda: S.activation(gm[:, :], gm[:, :], ACT.Exp))
            t.step(V, lambda: V.tensor_tensor(gm[:, :], gm[:, :], q.whole[:H, :], ALU.mult))
            t.step(V, lambda: V.tensor_tensor(dT[:, :], dT[:, :], al[:, :], ALU.mult))
            t.step(V, lambda: V.tensor_tensor_scan(cd[:, 1:], gm[:, :], dT[:, :], 0.0, ALU.mult, ALU.add))
            t.step(V, lambda: V.tensor_copy(hs[:, :].rearrange("h (k c) -> h k c", c=C), bc(q.ident[:H, :H], 2, [H, H, C])))
            pf = pb(c, "pf_" + name, [P, 2, 512])
            for j in range(2):
                for x in range(4):
                    xs = slice(x * CK, (x + 1) * CK)
                    t.step(TE, lambda j=j, xs=xs: TE.matmul(pf[:, 0, 0:CK], hs[:, j * P:(j + 1) * P], al[:, xs], start=True, stop=True),
                           lambda j=j, xs=xs: TE.matmul(pf[:, 1, 0:CK], hs[:, j * P:(j + 1) * P], gm[:, xs], start=True, stop=True))
                    t.step(V, lambda j=j, xs=xs: V.tensor_tensor(tT[:, j, xs], tT[:, j, xs], pf[:, 0, 0:CK], ALU.mult),
                           lambda xs=xs: V.tensor_copy(gB[:, xs], pf[:, 1, 0:CK]))
                t.step(V, lambda j=j: V.tensor_tensor_scan(cb[:, j, 1:], gB[:, :], tT[:, j, :], 0.0, ALU.mult, ALU.add))
        else:
            t.step(V, *[lambda j=j: V.tensor_tensor_scan(cb[:, j, 1:], q.whole[:, :], tT[:, j, :], 0.0, ALU.mult, ALU.add)
                        for j in range(2)])
        for g in range(TG):
            xs = slice(g * TP, (g + 1) * TP)
            t.step(TE, *[lambda j=j, xs=xs: TE.transpose(ps[0][:TP, j, :], cb[:, j, xs], q.ident[:, :]) for j in range(2)],
                   *([lambda j=j, m=m, xs=xs: TE.transpose(ps[1][:TP, j, 0:H], m[:, xs], q.ident[:H, :H])
                      for j, m in enumerate((cd, cm))] if gat else []))
            t.step(V, lambda g=g: V.tensor_copy(cp[:, g, 0:D].rearrange("p (j c) -> p j c", j=2), ps[0][:TP, 0:2, :]),
                   *([lambda g=g: V.tensor_copy(cp[:, g, D:GR].rearrange("p (j c) -> p j c", j=2), ps[1][:TP, 0:2, 0:H])]
                     if gat else []))
        if gat:
            mx = sb(c, "mx_" + name, [TP, TG, H])
            heads = lambda x: x[:, :, 0:D].rearrange("p g (h c) -> p g h c", c=C)
            t.step(V, lambda: V.tensor_tensor(mx[:, :, :], hd[:, :, D + H:GR], cp[:, :, D + H:GR], ALU.max))
            for x in (hd, cp):
                t.step(V, lambda x=x: V.tensor_tensor(x[:, :, D + H:GR], x[:, :, D + H:GR], mx[:, :, :], ALU.subtract))
                t.step(S, lambda x=x: S.activation(x[:, :, D + H:GR], x[:, :, D + H:GR], ACT.Exp))
                for g in range(TG):
                    t.step(V, lambda x=x, g=g: V.tensor_tensor(heads(x)[:, g, :, :], heads(x)[:, g, :, :],
                                                             bc(x[:, g, D + H:GR], 2, [TP, H, C]), ALU.mult))
                t.step(V, lambda x=x: V.tensor_tensor(x[:, :, D:D + H], x[:, :, D:D + H], x[:, :, D + H:GR], ALU.mult))
        t.step(V, lambda: V.tensor_tensor(hd[:, :, :], hd[:, :, :], cp[:, :, :], ALU.add))
        t.dma(G, pool=True, *[lambda g=g: G.indirect_dma_start(out=base, element_offset=skip, out_offset=bass.IndirectOffsetOnAxis(ap=q.fix_idx[:, g:g + 1], axis=0),
                                                    in_=hd[:, g, :], in_offset=None, bounds_check=EP - 1, oob_is_err=False)
                   for g in range(TG)])
        t.end(nc)


def node_rows(t, q, base, skip, i, ixn, rows):
    V, G = q.V, q.G
    t.step(V, lambda: V.tensor_copy(ixn[:, :], q.row_idx[:, bass.ds(i * NB, NB)]))
    t.dma(G, pool=True, *[lambda k=k: G.indirect_dma_start(out=rows[:, k, :], out_offset=None, in_=base, element_offset=skip,
               in_offset=bass.IndirectOffsetOnAxis(ap=ixn[:, k:k + 1], axis=0)) for k in range(NB)])


def layer0_update(nc, q):
    V, S, G, TE, SP, a, sb, pb = q.V, q.S, q.G, q.TE, q.SP, q.a, q.sb, q.pb
    t = Turns(q.sem("t_upd"), q.sem("t_upd_pool"))
    with ExitStack() as c:
        wl = sb(c, "wl", [P, 2, C])
        wb, wsc = sb(c, "wb", [C, 2, C]), sb(c, "wsc", [C, 2, C])
        wc = sb(c, "wc", [C, 9])
        gmm = sb(c, "gmm", [C, 3])
        ixn = sb(c, "ixn_u", [P, NB], I32)
        rows = sb(c, "rows_u", [P, NB, D])
        hT = sb(c, "hT_u", [C, 4, W])
        gT = sb(c, "gT_u", [P, 2, W])
        sq = sb(c, "sq_u", [C, 3, W])
        a0, a0s, pp, rr, vv = (sb(c, n + "_u", [C, W]) for n in ("a0", "a0s", "pp", "rr", "vv"))
        bb = sb(c, "bb_u", [C, 4, W])
        oT = sb(c, "oT_u", [C, 4, W])
        bst = sb(c, "bst", [C, NG, 6])
        ss = sb(c, "ss", [C, 3, NG])
        mv = sb(c, "mv_u", [C, 2])
        pG = [pb(c, f"pG{j}", [P, W]) for j in range(2)]
        pA = [pb(c, f"pA{j}", [C, W]) for j in range(4)]
        pO = [pb(c, f"pO{j}", [C, W]) for j in range(2)] + [pG[0][:C, :], pG[1][:C, :]]
        pO = [x[:, :] for x in pO]
        t.dma(SP, *[lambda h=h, n=n: SP.dma_start(wl[h * C:(h + 1) * C, n, :], a[f"L0_gnn_W_lin{n}"]) for h in range(2) for n in range(2)],
              *[lambda n=n: SP.dma_start(wb[:, n, :], a[f"L0_gnn_WB{n}"]) for n in range(2)],
              *[lambda n=n: SP.dma_start(wsc[:, n, :], a[f"L0_gnn_Wsc{n}"]) for n in range(2)],
              lambda: SP.dma_start(wc[:, 0:5], a["L0_gnn_Wc0"]), lambda: SP.dma_start(wc[:, 5:9], a["L0_gnn_Wc1"]),
              *[lambda k=k, n=n: SP.dma_start(gmm[:, k:k + 1], a["L0_gnn_" + n].unsqueeze(1)) for k, n in enumerate(("gamma0", "beta0", "gamma1"))])

        def body(i, width):
            node_rows(t, q, q.sums0_x, q.spare, i, ixn, rows)
            t.dma(SP, lambda: SP.dma_start(hT[:, :, :], q.hT_d[:, :, bass.ds(i * W, W)]))
            t.step(V, lambda: V.tensor_tensor(rows[:, :, :], rows[:, :, :], bc(q.some[:, bass.ds(i * NB, NB)], 2, [P, NB, D]), ALU.mult))
            t.step(TE, *[lambda j=j, k=k: TE.transpose(pG[j][:, k * P:(k + 1) * P], rows[:, k, j * P:(j + 1) * P], q.ident[:, :])
                         for j in range(2) for k in range(NB)])
            t.step(V, lambda: V.tensor_copy(gT[:, 0, :], pG[0][:, :]))
            t.step(S, lambda: S.activation(gT[:, 1, :], pG[1][:, :], ACT.Copy))
            t.step(TE, *[lambda pl=pl: TE.matmul(pA[pl][:, :], wl[C * (pl % 2):C * (pl % 2) + C, min(pl, 1), :],
                                                 gT[C * (pl % 2):C * (pl % 2) + C, pl // 2, :], start=True, stop=True) for pl in range(4)])
            t.step(S, lambda: S.activation(a0[:, :], pA[0][:, :], ACT.Copy),
                   lambda: S.activation(a0s[:, :], pA[0][:, :], ACT.Square),
                   *[lambda x=x: S.activation(sq[:, x, :], pA[1 + x][:, :], ACT.Square) for x in range(3)])
            tt = lambda o, x, y, op: t.step(V, lambda: V.tensor_tensor(o, x, y, op))
            stt = lambda o, x, w, y: t.step(V, lambda: V.scalar_tensor_tensor(o, x, wc[:, w:w + 1], y, ALU.mult, ALU.add))
            tt(vv[:, :], sq[:, 0, :], sq[:, 1, :], ALU.add)
            tt(vv[:, :], vv[:, :], sq[:, 2, :], ALU.add)
            t.step(V, lambda: V.tensor_scalar(pp[:, :], a0s[:, :], wc[:, 3:4], wc[:, 0:1], ALU.mult, ALU.add),
                   lambda: V.tensor_scalar(rr[:, :], a0s[:, :], wc[:, 7:8], wc[:, 5:6], ALU.mult, ALU.add))
            stt(pp[:, :], a0[:, :], 1, pp[:, :])
            stt(pp[:, :], vv[:, :], 4, pp[:, :])
            tt(pp[:, :], pp[:, :], a0[:, :], ALU.mult)
            stt(bb[:, 0, :], vv[:, :], 2, pp[:, :])
            stt(rr[:, :], a0[:, :], 6, rr[:, :])
            stt(rr[:, :], vv[:, :], 8, rr[:, :])
            t.step(V, *[lambda x=x: V.tensor_tensor(bb[:, 1 + x, :], rr[:, :], pA[1 + x][:, :], ALU.mult) for x in range(3)])
            t.step(TE, *[f for pl in range(4) for f in (
                lambda pl=pl: TE.matmul(pO[pl], wb[:, min(pl, 1), :], bb[:, pl, :], start=True, stop=False),
                lambda pl=pl: TE.matmul(pO[pl], wsc[:, min(pl, 1), :], hT[:, pl, :], start=False, stop=True))])
            t.step(V, lambda: V.bn_stats(bst[:, bass.ds(i, 1), :].rearrange("p a b -> p (a b)"), pO[0][:, 0:width]))
            t.step(S, *[lambda x=x: S.activation(sq[:, x, 0:width], pO[1 + x][:, 0:width], ACT.Square,
                                                 accum_out=ss[:, x, bass.ds(i, 1)]) for x in range(3)])
            t.step(V, *[lambda pl=pl: V.tensor_copy(oT[:, pl, :], pO[pl]) for pl in range(4)])
            t.dma(SP, lambda: SP.dma_start(q.oT_d[:, :, bass.ds(i * W, W)], oT[:, :, :]))

        with t.loop(nc, NG - 1, BODY_TURNS, 16 * NB) as i:
            body(i, W)
        body(NG - 1, LAST)
        t.step(V, lambda: V.bn_aggr(mv[:, :], bst[:, :, :].rearrange("p a b -> p (a b)")))
        t.step(V, lambda: V.tensor_reduce(q.stat[:, 3:4], ss[:, :, :].rearrange("p a b -> p (a b)"), mybir.AxisListType.X, ALU.add))
        t.step(S, lambda: S.activation(q.stat[:, 0:1], mv[:, 1:2], ACT.Sqrt, bias=q.eps_c[:C, 0:1]),
               lambda: S.activation(q.stat[:, 2:3], q.stat[:, 3:4], ACT.Sqrt, scale=1.0 / (3.0 * N), bias=q.eps_c[:C, 0:1]))
        t.step(V, lambda: V.reciprocal(q.stat[:, 0:1], q.stat[:, 0:1]), lambda: V.reciprocal(q.stat[:, 2:3], q.stat[:, 2:3]))
        t.step(V, lambda: V.tensor_tensor(q.stat[:, 0:3:2], q.stat[:, 0:3:2], gmm[:, 0:3:2], ALU.mult))
        t.step(V, lambda: V.tensor_tensor(q.stat[:, 1:2], mv[:, 0:1], q.stat[:, 0:1], ALU.mult))
        t.step(V, lambda: V.tensor_tensor(q.stat[:, 1:2], gmm[:, 1:2], q.stat[:, 1:2], ALU.subtract))
        t.end(nc)


BODY_TURNS = 1 + 16 + 1 + 1 + 2 + 1 + 1 + 2 + 1 + 6 + 1 + 1 + 1 + 1 + 1 + 16


class Project:

    TURNS = 3 + 32

    def __init__(self, t, q, c, n):
        self.t, self.q = t, q
        V, SP, a = q.V, q.SP, q.a
        self.w = q.sb(c, "we", [P, 2, D + 2 * H])
        alr = q.sb(c, "alr", [P, 2, D])
        wt = q.sb(c, "wt", [P, 2, D])
        self.hT = q.sb(c, "hT_p", [P, 2, W])
        self.f = q.sb(c, "f_p", [P, NB, D + H])
        self.er = q.sb(c, "er_p", [P, NB, H])
        self.pZ = [q.pb(c, f"pZ{j}", [P, W]) for j in range(2)]
        self.pF = [q.pb(c, f"pF{k}", [P, D + 2 * H]) for k in range(NB)]
        w, w_in = self.w, a[f"L1_gnn_W{n}"].rearrange("(j p) c -> p j c", p=P)
        t.dma(SP, lambda: SP.dma_start(w[:, :, 0:D], w_in),
              *[lambda k=k, v=v: SP.dma_start(alr[:, k, :], a[f"L1_gnn_{v}{n}"].rearrange("h c -> (h c)").partition_broadcast(P))
                for k, v in enumerate(("al", "ar"))])
        for k in range(2):
            t.step(V, lambda k=k: V.tensor_tensor(wt[:, :, :], w[:, :, 0:D], bc(alr[:, k, :], 1, [P, 2, D]), ALU.mult))
            t.step(V, lambda k=k: V.tensor_reduce(w[:, :, D + k * H:D + (k + 1) * H],
                                                  wt[:, :, :].rearrange("p j (h c) -> p j h c", c=C), mybir.AxisListType.X, ALU.add))

    def emit(self, i, z, func):
        t, q = self.t, self.q
        V, S, TE, SP = q.V, q.S, q.TE, q.SP
        t.step(TE, *[lambda j=j, k=k: TE.transpose(self.pZ[j][:, k * P:(k + 1) * P], z[:, k, j * P:(j + 1) * P], q.ident[:, :])
                     for j in range(2) for k in range(NB)])
        t.step(S, *[lambda j=j: S.activation(self.hT[:, j, :], self.pZ[j][:, :], func) for j in range(2)])
        t.step(TE, *[lambda j=j, k=k: TE.matmul(self.pF[k][:, :], self.hT[:, j, k * P:(k + 1) * P], self.w[:, j, :],
                                                start=j == 0, stop=j == 1) for k in range(NB) for j in range(2)])
        t.step(V, *[lambda k=k: V.tensor_copy(self.f[:, k, :], self.pF[k][:, 0:D + H]) for k in range(NB)],
               *[lambda k=k: V.tensor_copy(self.er[:, k, :], self.pF[k][:, D + H:]) for k in range(NB)])
        rows = lambda x: x.rearrange("(i k p) d -> i p k d", k=NB, p=P)[i, :, :, :]
        t.dma(SP, lambda: SP.dma_start(rows(q.table1), self.f[:, :, :]), lambda: SP.dma_start(rows(q.er_d), self.er[:, :, :]))


def layer0_norm_and_gat_nodes(nc, q):
    V, S, G, TE, SP, a, sb, pb = q.V, q.S, q.G, q.TE, q.SP, q.a, q.sb, q.pb
    t = Turns(q.sem("t_n1"), q.sem("t_n1_pool"))
    with ExitStack() as c:
        oT = sb(c, "oT_n", [C, 4, W])
        x, z = sb(c, "x_n", [P, NB, D]), sb(c, "z_n", [P, NB, D])
        st, mv, rs = sb(c, "st_n", [P, NB, 6]), sb(c, "mv_n", [P, NB, 2]), sb(c, "rs_n", [P, NB])
        pN = [pb(c, f"pN{k}", [P, 2, 4, C]) for k in range(2)]
        pr = Project(t, q, c, 1)
        rows = lambda y, i: y.rearrange("(i k p) d -> i p k d", k=NB, p=P)[i, :, :, :]
        with t.loop(nc, NG, 32 + 1 + 1 + 1 + 16 + NORM_TURNS + 4 + 32) as i:
            t.dma(SP, lambda: SP.dma_start(oT[:, :, :], q.oT_d[:, :, bass.ds(i * W, W)]),
                  lambda: SP.dma_start(x[:, :, :], rows(a["x"], i)))
            t.step(V, lambda: V.tensor_scalar(oT[:, 0, :], oT[:, 0, :], q.stat[:, 0:1], q.stat[:, 1:2], ALU.mult, ALU.add),
                   lambda: V.tensor_scalar(oT[:, 1:4, :], oT[:, 1:4, :], q.stat[:, 2:3], None, ALU.mult))
            t.step(TE, *[lambda k=k, pl=pl: TE.transpose(pN[k // 2][:, k % 2, pl, :], oT[:, pl, k * P:(k + 1) * P], q.ident[:C, :C])
                         for k in range(NB) for pl in range(4)])
            t.step(V, *[lambda k=k: V.tensor_tensor(x[:, k, 0:C], x[:, k, 0:C], pN[k // 2][:, k % 2, 0, :], ALU.add) for k in range(NB)],
                   *[lambda k=k: V.tensor_tensor(x[:, k, C:D].rearrange("p (c x) -> p x c", x=3),
                                                 x[:, k, C:D].rearrange("p (c x) -> p x c", x=3),
                                                 pN[k // 2][:, k % 2, 1:4, :], ALU.add) for k in range(NB)])
            t.dma(SP, lambda: SP.dma_start(rows(q.x1_d, i), x[:, :, :]))
            norm_rows(t, V, S, q, x, z, st, mv, rs)
            pr.emit(i, z, ACT.Relu)
        t.end(nc)


def spread_er(nc, q, n):
    V, S, G, TE, SP, a, sb, pb = q.V, q.S, q.G, q.TE, q.SP, q.a, q.sb, q.pb
    t = Turns(q.sem(f"t_er{n}"), q.sem(f"t_er{n}_pool"))
    KB = 10
    with ExitStack() as c:
        er = sb(c, "er_s", [P, NT, H])
        er_k, ix_k = sb(c, "er_k", [P, KB, H]), sb(c, "ix_k", [P, KB], I32)
        ch, held = sb(c, "ch", [P, CH, H]), sb(c, "held", [P, H, CH])
        ini = sb(c, "ini", [P, H])
        t.dma(SP, lambda: SP.dma_start(er[:, :, :], q.er_d.rearrange("(t p) h -> p t h", p=P)))
        t.dma(G, pool=True, *[lambda: G.indirect_dma_start(out=ini[:, :], out_offset=None, in_=q.er_d,
                                              in_offset=bass.IndirectOffsetOnAxis(ap=q.chunk_node[:, 0:1], axis=0))])
        with t.loop(nc, NT // KB, 1, 16 * KB) as i:
            t.step(V, lambda: V.tensor_copy(er_k[:, :, :], er[:, bass.ds(i * KB, KB), :]),
                   lambda: V.tensor_copy(ix_k[:, :], q.first_idx[:, bass.ds(i * KB, KB)]))
            t.dma(G, pool=True, *[lambda k=k: G.indirect_dma_start(
                out=q.er_start, out_offset=bass.IndirectOffsetOnAxis(ap=ix_k[:, k:k + 1], axis=0),
                in_=er_k[:, k, :], in_offset=None, bounds_check=EP - 1, oob_is_err=False) for k in range(KB)])
        t.dma(SP, lambda: SP.dma_start(ch[:, :, :].rearrange("p e h -> p (e h)"), q.er_start.rearrange("(p e) h -> p (e h)", p=P)))
        t.step(V, *[lambda h=h: V.tensor_tensor_scan(held[:, h, :], q.samep[:, :], ch[:, :, h], ini[:, h:h + 1], ALU.mult, ALU.add)
                    for h in range(H)])
        t.dma(SP, lambda: SP.dma_start(q.er_edge.rearrange("h (p e) -> p h e", p=P), held[:, :, :]))
        t.end(nc)


def gat_edges(nc, q, n):
    a, sb, pb = q.a, q.sb, q.pb
    FR = D + H
    NQ = SBT // 4
    with ExitStack() as c:
        er = sb(c, f"er_g{n}", [P, SB, P])
        ix = sb(c, f"ix_g{n}", [P, 2, SBT], I32)
        gb = sb(c, f"gb_g{n}", [P, 2, SBT, FR])
        elc = sb(c, f"elc{n}", [P, H, SBT])
        fs, mm_, ee, ww = (sb(c, f"{x}{n}", [P, P]) for x in ("fs", "mm_", "ee", "ww"))
        mT = sb(c, f"mT_g{n}", [P, SBT, H])
        sel = sb(c, f"sel_g{n}", [P, 2, 4, P])
        ost = sb(c, f"ost_g{n}", [P, 2, 4, GR])
        pE = pb(c, f"pE{n}", [P, P])
        pW = pb(c, f"pW{n}", [P, 2, P])
        po = [pb(c, f"po{k}_{n}", [P, 2, 512]) for k in range(2)]

        nm = lambda x: f"{x}_g{n}"
        s_er = q.sem(nm("er"))
        s_ix = [Signal(q.sem(nm(f"ix{p}")), inc=16) for p in range(2)]
        s_g = [Signal(q.sem(nm(f"g{p}")), per=SBT, inc=16) for p in range(2)]
        s_elc = Signal(q.sem(nm("elc")))
        s_elT = Signal(q.sem(nm("elT")))
        s_d = Signal(q.sem(nm("d")))
        s_w = Signal(q.sem(nm("w")))
        s_wT = Signal(q.sem(nm("wT")))
        s_we = Signal(q.sem(nm("we")))
        s_msg = Signal(q.sem(nm("msg")), per=NQ)
        s_sum = Signal(q.sem(nm("sum")), per=2 * NQ, ahead=2)
        s_ev = Signal(q.sem(nm("ev")), per=2 * NQ, ahead=1)
        s_st = [Signal(q.sem(nm(f"st{p}")), per=NQ // 2, inc=16, ahead=1) for p in range(2)]
        dv = Signal(q.sem(nm("dv")), per=6)
        out_v = q.sums1.rearrange("(b j p) c -> b p j c", j=4, p=P)

        def over(eng, body):
            with eng.Fori(0, SB // 2) as i:
                for p in range(2):
                    body(i * 2 + p, i, p)
            for s in range(SB // 2 * 2, SB):
                body(s, s // 2, s % 2)

        with nc.Block() as block:
            @block.sync
            def _(eng):
                for s in s_st:
                    s.prime(eng)
                view = q.er_edge.rearrange("h (s t e) -> h t s e", t=SBT, e=P)
                for h in range(H):
                    eng.dma_start(er[h * SBT:(h + 1) * SBT, :, :], view[h, :, :, :]).then_inc(s_er, 16)

                def body(s, i, p):
                    s_sum.wait(eng, s - 2)
                    eng.nop(nofuse=True)
                    eng.dma_start(ix[:, p, :].rearrange("p (g j) -> p g j", j=8),
                                  a["src_cols"].rearrange("(s g) p j -> s p g j", g=4)[s, :, :, :]).then_inc(s_ix[p].sem, 16)

                def stores(s, i, p):
                    for k in range(1, NQ + 1):
                        s_ev.wait(eng, s, 2 * k)
                        eng.nop(nofuse=True)
                        eng.dma_start(out_v[s * NQ + (k - 1), :, :, :], ost[:, k % 2, :, :]).then_inc(s_st[k % 2].sem, 16)

                body(0, 0, 0)
                with eng.Fori(0, SB // 2) as i:
                    for p in range(2):
                        body(i * 2 + (p + 1), i, 1 - p)
                        stores(i * 2 + p, i, p)
                stores(SB - 1, SB // 2, 0)
                for s in s_st:
                    s.wait(eng, SB - 1)

            @block.gpsimd
            def _(eng):
                def body(s, i, p):
                    s_ix[p].wait(eng, i)
                    s_sum.wait(eng, s - 2)
                    eng.nop(nofuse=True)
                    for j in range(SBT):
                        eng.indirect_dma_start(out=gb[:, p, j, :], out_offset=None, in_=q.table1[:, :],
                                               in_offset=bass.IndirectOffsetOnAxis(ap=ix[:, p, j:j + 1], axis=0)).then_inc(s_g[p].sem, 16)
                over(eng, body)

            @block.tensor
            def _(eng):
                s_sum.prime(eng)

                def body(s, i, p):
                    s_elc.wait(eng, s)
                    eng.transpose(pE[:, :], elc[:, :, :].rearrange("p h t -> p (h t)"), q.ident[:, :]).then_inc(s_elT.sem, 1)
                    s_w.wait(eng, s)
                    eng.transpose(pW[:, 0, :], ww[:, :], q.ident[:, :])
                    eng.transpose(pW[:, 1, :], mm_[:, :], q.ident[:, :]).then_inc(s_wT.sem, 1)
                    for k in range(1, NQ + 1):
                        s_msg.wait(eng, s, k)
                        for x in range(2):
                            s_ev.wait(eng, s, 2 * k + x - 2)
                            for j in range(2):
                                tl = 4 * (k - 1) + 2 * x + j
                                ins = eng.matmul(po[x][:, j, 0:FR], sel[:, k % 2, 2 * x + j, :], gb[:, p, tl, :], start=True, stop=True)
                            ins.then_inc(s_sum.sem, 1)
                over(eng, body)

            @block.scalar
            def _(eng):
                s_ev.prime(eng)

                def body(s, i, p):
                    s_g[p].wait(eng, i)
                    eng.activation(elc[:, :, :], gb[:, p, :, D:FR].rearrange("p t h -> p h t"), ACT.Copy).then_inc(s_elc.sem, 1)
                    s_d.wait(eng, s)
                    eng.activation(ww[:, :], ee[:, :], ACT.Exp).then_inc(s_w.sem, 1)
                    s_wT.wait(eng, s)
                    view = lambda k: pW[:, k, :].rearrange("p (h t) -> p t h", t=SBT)
                    eng.activation(gb[:, p, :, D:FR], view(0), ACT.Copy)
                    eng.activation(mT[:, :, :], view(1), ACT.Copy).then_inc(s_we.sem, 1)
                    s_we.wait(eng, s)
                    for k in range(1, NQ + 1):
                        s_st[k % 2].wait(eng, s, (k + 1) // 2 - 1)
                        for x in range(2):
                            tl = 4 * (k - 1) + 2 * x
                            eng.activation(ost[:, k % 2, 2 * x:2 * x + 2, FR:GR], mT[:, tl:tl + 2, :], ACT.Copy)
                            s_sum.wait(eng, s, 2 * k + x - 1)
                            eng.activation(ost[:, k % 2, 2 * x:2 * x + 2, 0:FR], po[x][:, :, 0:FR], ACT.Copy).then_inc(s_ev.sem, 1)
                over(eng, body)

            @block.vector
            def _(eng):
                eng.wait_ge(s_er, 16 * H)

                def body(s, i, p):
                    er_s = er[:, bass.ds(s, 1), :].rearrange("p a e -> p (a e)")
                    f_m, b_m = (m[:, bass.ds(s, 1), :].rearrange("p a e -> p (a e)") for m in (q.start_f, q.start_b))
                    s_elT.wait(eng, s)
                    eng.tensor_tensor_scan(fs[:, :], f_m, pE[:, :], -BIG, ALU.add, ALU.max).then_inc(dv.sem, 1)
                    dv.wait(eng, s, 1)
                    eng.tensor_tensor_scan(mm_[:, ::-1], b_m, fs[:, ::-1], -BIG, ALU.add, ALU.max).then_inc(dv.sem, 1)
                    eng.tensor_tensor(ee[:, :], pE[:, :], er_s, ALU.add).then_inc(dv.sem, 1)
                    dv.wait(eng, s, 2)
                    eng.tensor_tensor(mm_[:, :], mm_[:, :], er_s, ALU.add).then_inc(dv.sem, 1)
                    dv.wait(eng, s, 3)
                    eng.scalar_tensor_tensor(ee[:, :], ee[:, :], 0.2, ee[:, :], ALU.mult, ALU.max).then_inc(dv.sem, 1)
                    dv.wait(eng, s, 4)
                    eng.scalar_tensor_tensor(mm_[:, :], mm_[:, :], 0.2, mm_[:, :], ALU.mult, ALU.max).then_inc(dv.sem, 1)
                    dv.wait(eng, s, 6)
                    eng.tensor_tensor(ee[:, :], ee[:, :], mm_[:, :], ALU.subtract).then_inc(s_d.sem, 1)
                    s_we.wait(eng, s)
                    for k in range(1, NQ + 1):
                        tl = slice(4 * (k - 1), 4 * k)
                        s_sum.wait(eng, s, 2 * k - 4)
                        eng.tensor_tensor(sel[:, k % 2, :, :], bc(q.lastpos[:, bass.ds(s * SBT + 4 * (k - 1), 4)], 2, [P, 4, P]),
                                          bc(q.iota_f[:, :], 1, [P, 4, P]), ALU.is_equal)
                        f = gb[:, p, tl, 0:D].rearrange("p t (h c) -> p t h c", c=C)
                        eng.tensor_tensor(f, f, bc(gb[:, p, tl, D:FR], 3, [P, 4, H, C]), ALU.mult).then_inc(s_msg.sem, 1)
                over(eng, body)


def gat_output(nc, q, n):
    V, S, G, TE, SP, a, sb, pb = q.V, q.S, q.G, q.TE, q.SP, q.a, q.sb, q.pb
    t = Turns(q.sem(f"t_o{n}"), q.sem(f"t_o{n}_pool"))
    with ExitStack() as c:
        ixn = sb(c, "ixn", [P, NB], I32)
        rows = sb(c, "rows", [P, NB, GR])
        bias = sb(c, "bias", [P, D])
        v, ex = sb(c, "v", [P, NB, D]), sb(c, "ex", [P, NB, D])
        ns, rd = sb(c, "ns", [P, NB]), sb(c, "rd", [P, NB, H])
        x1 = sb(c, "x1", [P, NB, D])
        t.dma(SP, lambda: SP.dma_start(bias[:, :], a[f"L1_gnn_b{n}"].partition_broadcast(P)))
        pr = Project(t, q, c, 2) if n == 1 else None
        view = lambda y, i: y.rearrange("(i k p) d -> i p k d", k=NB, p=P)[i, :, :, :]
        with t.loop(nc, NG, 10 + (37 if n == 1 else 34), 16 * NB) as i:
            node_rows(t, q, q.sums1, 0, i, ixn, rows)
            some = q.some[:, bass.ds(i * NB, NB)]
            t.step(V, lambda: V.tensor_scalar(ns[:, :], some, -1.0, 1.0, ALU.mult, ALU.add))
            t.step(V, lambda: V.tensor_tensor(rd[:, :, :], rows[:, :, D:D + H], bc(ns[:, :], 2, [P, NB, H]), ALU.add))
            t.step(V, lambda: V.reciprocal(rd[:, :, :], rd[:, :, :]))
            t.step(V, lambda: V.tensor_tensor(rd[:, :, :], rd[:, :, :], bc(some, 2, [P, NB, H]), ALU.mult))
            heads = lambda y: y[:, :, 0:D].rearrange("p k (h c) -> p (k h) c", c=C)
            t.step(V, *[lambda k=k: V.tensor_tensor(v[:, k, :].rearrange("p (h c) -> p h c", c=C),
                                                  rows[:, k, 0:D].rearrange("p (h c) -> p h c", c=C),
                                                  bc(rd[:, k, :], 2, [P, H, C]), ALU.mult) for k in range(NB)])
            t.step(V, lambda: V.tensor_tensor(v[:, :, :], v[:, :, :], bc(bias[:, :], 1, [P, NB, D]), ALU.add))
            t.step(V, lambda: V.tensor_scalar(ex[:, :, :], v[:, :, :], 0.0, None, ALU.min))
            t.step(S, lambda: S.activation(ex[:, :, :], ex[:, :, :], ACT.Exp))
            t.step(V, lambda: V.tensor_scalar(v[:, :, :], v[:, :, :], 0.0, -1.0, ALU.max, ALU.add))
            if n == 1:
                t.step(V, lambda: V.tensor_tensor(v[:, :, :], v[:, :, :], ex[:, :, :], ALU.add))
                pr.emit(i, v, ACT.Copy)
            else:
                t.step(V, lambda: V.tensor_tensor(v[:, :, :], v[:, :, :], ex[:, :, :], ALU.add))
                t.dma(SP, lambda: SP.dma_start(x1[:, :, :], view(q.x1_d, i)))
                t.step(V, lambda: V.tensor_tensor(v[:, :, :], v[:, :, :], x1[:, :, :], ALU.add))
                t.dma(SP, lambda: SP.dma_start(view(q.out, i), v[:, :, :]))
        t.end(nc)


def kernel(**inputs):
    import numpy as _np
    import concourse.bacc as _bacc
    from concourse import mybir as _mybir
    from concourse.bass_utils import run_bass_kernel_spmd as _run

    x = _np.asarray(inputs["x"])
    src, dst = _np.asarray(inputs["src"]), _np.asarray(inputs["dst"])
    pad = EP - E
    srcp = _np.concatenate([src, _np.zeros(pad, src.dtype)])
    dstp = _np.concatenate([dst, _np.full(pad, N, dst.dtype)])
    rbf = _np.concatenate([_np.asarray(inputs["edge_attr_16"]), _np.zeros((pad + 2 * W, R), _np.float32)])
    sh = _np.concatenate([_np.asarray(inputs["edge_attr_4"]), _np.zeros((pad, 4), _np.float32)])
    arrays = {
        "x": _np.concatenate([x, _np.zeros((NP_ - N, D), x.dtype)]),
        "src_cols": srcp.reshape(EP // 1024, 8, P).transpose(0, 2, 1),
        "dst_cols": dstp.reshape(T, P).T,
        "dst_line": _np.concatenate([_np.full(1, -1, dst.dtype), dstp, _np.full(1, -2, dst.dtype)]),
        "rbf": rbf.reshape(EP // 1024 + 1, 2, W, R).transpose(0, 1, 3, 2).reshape(-1, 2 * R, W),
        "sh": sh.reshape(EP // 1024, 8, P, 4).transpose(0, 2, 1, 3).reshape(-1, P, 32),
    }
    for k, v in inputs.items():
        if k[:2] in ("L0", "L1"):
            arrays[k] = _np.asarray(v)
    arrays = {k: _np.ascontiguousarray(v) for k, v in arrays.items()}
    nc = _bacc.Bacc("TRN2", target_bir_lowering=False, num_devices=1)
    a = {k: nc.dram_tensor("in_" + k, v.shape, _mybir.dt.from_np(v.dtype), kind="ExternalInput").ap() for k, v in arrays.items()}
    out = nc.dram_tensor("out", (NP_, D), F32, kind="ExternalOutput").ap()
    program(nc, a, out)
    r = _run(nc, [{"in_" + k: v for k, v in arrays.items()}], core_ids=[0])
    return r.results[0]["out"][:N]
```

```python
from contextlib import ExitStack, contextmanager

import numpy as np
import concourse.bass as bass
from concourse import mybir

F32, I32, BF16 = mybir.dt.float32, mybir.dt.int32, mybir.dt.bfloat16
ALU, ACT = mybir.AluOpType, mybir.ActivationFunctionType
P = 128
N, E, C, H, HID, R = 12500, 200000, 64, 4, 64, 16
D = 4 * C
NT = 104
NP_ = NT * P
NB = 2
NG = NT // NB
K = 4
W = NB * P
HALF = 4 * P
FULL = N // W
LAST = N - FULL * W
SBT = 32
SB = -(-E // (SBT * P))
T = SB * SBT
EP = T * P
TG = 14
TP = T // TG
CH = EP // P
GR = D + 2 * H
SPARE = 4
BIG = 1.0e30
SKIP = float(1 << 22)
EPS = 1e-5
assert NG % K == 0 and FULL % K == 0 and K * NB == 8 and T == TG * TP and EP == P * CH and T % 8 == 0


class Signal:

    def __init__(self, sem, per=1, inc=1, ahead=0):
        self.sem, self.per, self.inc, self.base = sem, per, inc, ahead * per * inc

    def at(self, i, k=None, back=0):
        k = (self.per if k is None else k) - back * self.per
        return i * (self.per * self.inc) + (self.base + k * self.inc)

    def wait(self, eng, i, k=None, back=0):
        eng.wait_ge(self.sem, self.at(i, k, back))

    def prime(self, eng):
        eng.sem_inc(self.sem, self.base)


class Turns:

    def __init__(self, sem, pool_sem):
        self.sems = (sem, pool_sem)
        self.base, self.n, self.per, self.i = [0, 0], [0, 0], [0, 0], 0
        self.last = (0,)
        self.queue = None

    def value(self, s):
        return self.i * self.per[s] + (self.base[s] + self.n[s]) if self.per[s] else self.base[s] + self.n[s]

    def wait(self, eng):
        for s in self.last:
            if self.base[s] + self.n[s] + self.per[s]:
                eng.wait_ge(self.sems[s], self.value(s))
                if self.per[s]:
                    eng.nop(nofuse=True)

    def step(self, eng, *instructions):
        if self.queue is not None:
            self.queue.append((self._step, eng, instructions, 0))
        else:
            self._step(eng, instructions, 0)

    def dma(self, eng, *instructions, pool=False):
        if self.queue is not None:
            self.queue.append((self._dma, eng, instructions, int(pool)))
        else:
            self._dma(eng, instructions, int(pool))

    def _step(self, eng, instructions, _):
        self.wait(eng)
        for make in instructions:
            ins = make()
        ins.then_inc(self.sems[0], 1)
        self.n[0] += 1
        self.last = (0,)

    def _dma(self, eng, instructions, pool):
        self.wait(eng)
        for make in instructions:
            make().then_inc(self.sems[pool], 16)
        self.n[pool] += 16 * len(instructions)
        self.last = (pool,)

    def begin(self, per, i):
        self.base = [x + y for x, y in zip(self.base, self.n)]
        self.n, self.last = [0, 0], tuple(s for s in (0, 1) if self.base[s])
        self.i, self.per = i, per

    def close(self, count):
        assert self.n == self.per, (self.n, self.per)
        self.base = [x + count * y for x, y in zip(self.base, self.per)]
        self.n, self.per, self.i, self.last = [0, 0], [0, 0], 0, (0, 1)

    def end(self, nc):
        for eng in (nc.sync, nc.scalar, nc.vector, nc.gpsimd, nc.tensor):
            for s in (0, 1):
                if self.base[s] + self.n[s]:
                    eng.wait_ge(self.sems[s], self.value(s))
        nc.all_engine_barrier()


def queued(t, body, i):
    t.queue = []
    body(i)
    steps, t.queue = t.queue, None
    return steps


def side_by_side(queues):
    for n in range(max(map(len, queues))):
        for queue in queues:
            if n < len(queue):
                emit, eng, instructions, pool = queue[n]
                emit(eng, instructions, pool)


def chains_loop(nc, chains, count, bodies):
    K = len(chains)

    def parts(k, i):
        steps = queued(chains[k], bodies[k], i * K + k)
        cut = len(steps) * k // K
        return steps[:cut], steps[cut:]

    for t in chains:
        if not t.base[0] + t.n[0]:
            nc.sync.sem_inc(t.sems[0], 1)
            t.n[0] += 1
    side_by_side([parts(k, 0)[0] for k in range(K)])
    with nc.Fori(0, count - 1) as i:
        turn = [parts(k, i)[1] + parts(k, i + 1)[0] for k in range(K)]
        for t, steps in zip(chains, turn):
            t.begin([sum(16 * len(ins) if emit == t._dma else 1 for emit, _, ins, pool in steps if pool == s)
                     for s in (0, 1)], i)
        side_by_side(turn)
        for t in chains:
            t.close(count - 1)
    side_by_side([parts(k, count - 1)[1] for k in range(K)])


def bc(ap, dim, shape):
    return ap.unsqueeze(dim).to_broadcast(shape)


class Shared:
    pass


def program(nc, a, out):
    q = Shared()
    q.a, q.out = a, out
    q.top = top = ExitStack()
    with top:
        seen = {}

        def unique(name):
            seen[name] = seen.get(name, 0) + 1
            return f"{name}_{seen[name]}"

        def sb(ctx, name, shape, dt=F32):
            return ctx.enter_context(nc.sbuf_tensor(unique(name), shape, dt))

        def pb(ctx, name, shape, dt=F32):
            return ctx.enter_context(nc.psum_tensor(unique(name), shape, dt))

        def sem(name):
            return top.enter_context(nc.semaphore(name))

        def dram(name, shape, dt=F32):
            return nc.dram_tensor(name, shape, dt, kind="Internal").ap()

        q.V, q.S, q.G, q.TE, q.SP = nc.vector, nc.scalar, nc.gpsimd, nc.tensor, nc.sync
        q.sb, q.pb, q.sem = sb, pb, sem

        q.table0 = dram("table0", (NP_, D))
        q.table1 = dram("table1", (NP_, D + H))
        q.hT_d = dram("hT_d", (C, 4, NP_))
        q.oT_d = dram("oT_d", (C, 4, NP_))
        q.x1_d = dram("x1_d", (NP_, D))
        q.er_d = dram("er_d", (NP_, H))
        q.sums0_x = dram("sums0", (8 * P + EP, D))
        q.sums0 = q.sums0_x[8 * P:, :]
        q.spare = 8 * P * D
        q.sums1 = dram("sums1", (EP, GR))
        q.er_start = dram("er_start", (EP, H))
        q.er_edge = dram("er_edge", (H, EP))

        q.iota_f = sb(top, "iota_f", [P, P])
        q.ident = sb(top, "ident", [P, P])
        q.upper = sb(top, "upper", [P, P])
        q.lastpos = sb(top, "lastpos", [P, T])
        q.whole = sb(top, "whole", [P, T])
        q.start_f = sb(top, "start_f", [P, SB, P], BF16)
        q.start_b = sb(top, "start_b", [P, SB, P], BF16)
        q.samep = sb(top, "samep", [P, CH])
        q.chunk_node = sb(top, "chunk_node", [P, 1], I32)
        q.head_idx = sb(top, "head_idx", [TP, TG], I32)
        q.fix_idx = sb(top, "fix_idx", [TP, TG], I32)
        q.row_idx = sb(top, "row_idx", [P, P], I32)
        q.first_idx = sb(top, "first_idx", [P, P], I32)
        q.some = sb(top, "some", [P, P])
        q.eps_c = sb(top, "eps_c", [P, 1])
        q.stat = sb(top, "stat", [C, 4])

        structure(nc, q)
        layer0_nodes(nc, q)
        layer0_edges(nc, q)
        stitch(nc, q, q.sums0, D, "s0")
        layer0_update(nc, q)
        layer0_norm_and_gat_nodes(nc, q)
        for n in (1, 2):
            spread_er(nc, q, n)
            gat_edges(nc, q, n)
            stitch(nc, q, q.sums1, GR, f"s{n}")
            gat_output(nc, q, n)


def structure(nc, q):
    V, S, G, TE, SP, a, sb, pb = q.V, q.S, q.G, q.TE, q.SP, q.a, q.sb, q.pb
    t = Turns(q.sem("t_struct"), q.sem("t_struct_pool"))
    line = a["dst_line"]
    with ExitStack() as c:
        ii = sb(c, "ii", [P, P], I32)
        t.step(G, lambda: G.iota(ii[:, :], pattern=[[1, P]], base=0, channel_multiplier=0))
        t.step(V, lambda: V.tensor_copy(q.iota_f[:, :], ii[:, :]))
        t.step(G, lambda: G.memset(q.ident[:, :], 0.0))
        t.step(G, lambda: G.affine_select(out=q.ident[:, :], in_=q.ident[:, :], compare_op=ALU.not_equal,
                                          fill=1.0, base=0, pattern=[[-1, P]], channel_multiplier=1))
        t.step(G, lambda: G.memset(q.upper[:, :], 1.0))
        t.step(G, lambda: G.affine_select(out=q.upper[:, :], in_=q.upper[:, :], compare_op=ALU.is_gt,
                                          fill=0.0, base=0, pattern=[[1, P]], channel_multiplier=-1))
        t.step(V, lambda: V.memset(q.eps_c[:, :], EPS))

    with ExitStack() as c:
        d, dp, dn = (sb(c, n, [TP, TG, P], I32) for n in ("d", "dp", "dn"))
        same, pos, lp = (sb(c, n, [TP, TG, P]) for n in ("same", "pos", "lp"))
        wh, link, fi = (sb(c, n, [TP, TG]) for n in ("wh", "link", "fi"))
        fi_i = sb(c, "fi_i", [TP, TG], I32)
        ps = pb(c, "ps_s", [P, 4, P])
        view = lambda o: line[o:o + EP].rearrange("(g p e) -> p g e", p=TP, e=P)
        t.dma(SP, lambda: SP.dma_start(dp[:, :, :], view(0)), lambda: SP.dma_start(d[:, :, :], view(1)),
              lambda: SP.dma_start(dn[:, :, :], view(2)))
        t.step(V, lambda: V.tensor_tensor(same[:, :, :], d[:, :, :], dn[:, :, :], ALU.is_equal))
        t.step(V, lambda: V.memset(same[:, :, P - 1:P], 0.0))
        t.step(V, lambda: V.tensor_scalar(pos[:, :, :], same[:, :, :], -1.0, 1.0, ALU.mult, ALU.add))
        t.step(V, lambda: V.tensor_tensor(pos[:, :, :], pos[:, :, :], bc(q.iota_f[:TP, :], 1, [TP, TG, P]), ALU.mult))
        flat = lambda x: x[:, :, :].rearrange("p g e -> p (g e)")[:, ::-1]
        t.step(V, lambda: V.tensor_tensor_scan(flat(lp), flat(same), flat(pos), 0.0, ALU.mult, ALU.add))
        t.step(V, lambda: V.tensor_tensor(wh[:, :].unsqueeze(2), dp[:, :, 0:1], d[:, :, P - 1:P], ALU.is_equal))
        t.step(V, lambda: V.tensor_tensor(link[:, :].unsqueeze(2), dp[:, :, 0:1], d[:, :, 0:1], ALU.is_equal))
        t.step(G, lambda: G.iota(fi_i[:, :], pattern=[[TP * P, TG]], base=0, channel_multiplier=P))
        t.step(V, lambda: V.tensor_copy(fi[:, :], fi_i[:, :]))
        t.step(V, lambda: V.tensor_tensor(fi[:, :].unsqueeze(2), fi[:, :].unsqueeze(2), lp[:, :, 0:1], ALU.add))
        t.step(V, lambda: V.tensor_copy(q.head_idx[:, :], fi[:, :]))
        t.step(V, lambda: V.tensor_scalar(link[:, :], link[:, :], -SKIP, SKIP, ALU.mult, ALU.add))
        t.step(V, lambda: V.tensor_tensor(fi[:, :], fi[:, :], link[:, :], ALU.add))
        t.step(V, lambda: V.tensor_copy(q.fix_idx[:, :], fi[:, :]))
        t.step(V, lambda: V.tensor_copy(same[:, :, :], bc(wh[:, :], 2, [TP, TG, P])))
        for src, dst in ((lp, q.lastpos), (same, q.whole)):
            for g0 in range(0, TG, 4):
                gs = range(g0, min(g0 + 4, TG))
                t.step(TE, *[lambda g=g, src=src: TE.transpose(ps[:, g % 4, 0:TP], src[:, g, :], q.ident[:TP, :TP])
                             for g in gs])
                t.step(V, lambda dst=dst, g0=g0, gs=gs: V.tensor_copy(
                    dst[:, g0 * TP:(g0 + len(gs)) * TP].rearrange("p (g t) -> p g t", t=TP), ps[:, 0:len(gs), 0:TP]))

    with ExitStack() as c:
        m0, m1 = (sb(c, n, [P, SB, P], I32) for n in ("m0", "m1"))
        eq = sb(c, "eq", [P, SB, P], BF16)
        view = lambda o: line[o:o + EP].rearrange("(s t e) -> t s e", t=SBT, e=P)
        load = lambda m, o: [lambda h=h: SP.dma_start(m[h * SBT:(h + 1) * SBT, :, :], view(o)) for h in range(H)]
        t.dma(SP, *load(m0, 1))
        for o, mask in ((0, q.start_f), (2, q.start_b)):
            t.dma(SP, *load(m1, o))
            t.step(V, lambda mask=mask: V.tensor_tensor(eq[:, :, :], m0[:, :, :], m1[:, :, :], ALU.is_equal))
            t.step(V, lambda mask=mask: V.tensor_scalar(mask[:, :, :], eq[:, :, ::1 - o], BIG, -BIG, ALU.mult, ALU.add))

    with ExitStack() as c:
        c0, c1 = (sb(c, n, [P, CH], I32) for n in ("c0", "c1"))
        t.dma(SP, lambda: SP.dma_start(c0[:, :], line[1:1 + EP].rearrange("(p e) -> p e", p=P)),
              lambda: SP.dma_start(c1[:, :], line[0:EP].rearrange("(p e) -> p e", p=P)))
        t.step(V, lambda: V.tensor_tensor(q.samep[:, :], c0[:, :], c1[:, :], ALU.is_equal))
        t.step(V, lambda: V.tensor_copy(q.chunk_node[:, :], c0[:, 0:1]))
        z = sb(c, "z", [P, CH * H])
        t.step(V, lambda: V.memset(z[:, :], 0.0))
        t.dma(SP, lambda: SP.dma_start(q.er_start.rearrange("(p e) h -> p (e h)", p=P), z[:, :]))

    with ExitStack() as c:
        dc = sb(c, "dc", [P, T], I32)
        hi_i, lo_i = (sb(c, n, [P, T], I32) for n in ("hi_i", "lo_i"))
        hi, lo = (sb(c, n, [P, T]) for n in ("hi", "lo"))
        oh = sb(c, "oh", [P, 2, 2, 8, P], BF16)
        zero = sb(c, "zero", [P, P], BF16)
        cnt, cum, beg, non = (sb(c, n, [P, P]) for n in ("cnt", "cum", "beg", "non"))
        hist = pb(c, "hist", [P, P])
        pre = pb(c, "pre", [P, 1])
        tr = pb(c, "tr", [P, 3, P])
        t.dma(SP, lambda: SP.dma_start(dc[:, :], a["dst_cols"]))
        t.step(V, lambda: V.tensor_scalar(hi_i[:, :], dc[:, :], 7, None, ALU.logical_shift_right),
               lambda: V.tensor_scalar(lo_i[:, :], dc[:, :], 127, None, ALU.bitwise_and))
        t.step(V, lambda: V.tensor_copy(hi[:, :], hi_i[:, :]), lambda: V.tensor_copy(lo[:, :], lo_i[:, :]),
               lambda: V.memset(zero[:, :], 0.0))
        t.step(TE, lambda: TE.matmul(hist[:, :], zero[:, :], zero[:, :], start=True, stop=False))
        t.end(nc)
        made = Signal(q.sem("hist_made"), per=2)
        used = Signal(q.sem("hist_used"), per=2, ahead=1)
        with nc.Block() as block:
            @block.vector
            def _(eng):
                with eng.Fori(0, T // 16) as i:
                    for b in range(2):
                        used.wait(eng, i, b + 1, back=1)
                        for n, v in enumerate((hi, lo)):
                            ins = eng.tensor_tensor(oh[:, b, n, :, :], bc(v[:, bass.ds(i * 16 + b * 8, 8)], 2, [P, 8, P]),
                                                    bc(q.iota_f[:, :], 1, [P, 8, P]), ALU.is_equal)
                        ins.then_inc(made.sem, 1)

            @block.tensor
            def _(eng):
                used.prime(eng)
                with eng.Fori(0, T // 16) as i:
                    for b in range(2):
                        made.wait(eng, i, b + 1)
                        for k in range(8):
                            ins = eng.matmul(hist[:, :], oh[:, b, 0, k, :], oh[:, b, 1, k, :], start=False, stop=False)
                        ins.then_inc(used.sem, 1)
                eng.matmul(hist[:, :], zero[:, :], zero[:, :], start=False, stop=True).then_inc(used.sem, 1)
        V.wait_ge(used.sem, used.at(T // 16 - 1) + 1)
        t.step(V, lambda: V.tensor_copy(cnt[:, :], hist[:, :]))
        t.step(V, lambda: V.memset(beg[:, :], 0.0))
        t.step(V, lambda: V.tensor_tensor_scan(cum[:, :], cnt[:, :], beg[:, :], 0.0, ALU.add, ALU.add))
        t.step(TE, lambda: TE.matmul(pre[:, :], q.upper[:, :], cum[:, P - 1:P], start=True, stop=True))
        t.step(V, lambda: V.tensor_scalar(cum[:, :], cum[:, :], pre[:, 0:1], -1.0, ALU.add, ALU.add))
        t.step(V, lambda: V.tensor_tensor(beg[:, :], cum[:, :], cnt[:, :], ALU.subtract))
        t.step(V, lambda: V.tensor_scalar(non[:, :], cnt[:, :], 0.0, SKIP, ALU.is_equal, ALU.mult))
        t.step(V, lambda: V.scalar_tensor_tensor(beg[:, :], beg[:, :], 1.0, non[:, :], ALU.add, ALU.add))
        t.step(V, lambda: V.tensor_scalar(non[:, :], cnt[:, :], 0.0, None, ALU.is_gt))
        t.step(V, lambda: V.tensor_scalar(cum[:, :], cum[:, :], 0.0, None, ALU.max))
        t.step(TE, *[lambda k=k, m=m: TE.transpose(tr[:, k, :], m[:, :], q.ident[:, :])
                     for k, m in enumerate((cum, beg, non))])
        t.step(V, lambda: V.tensor_copy(q.row_idx[:, :], tr[:, 0, :]),
               lambda: V.tensor_copy(q.first_idx[:, :], tr[:, 1, :]),
               lambda: V.tensor_copy(q.some[:, :], tr[:, 2, :]))
        t.end(nc)


def norm_rows(t, V, S, q, x, z, st, mv, rs):
    for k in range(NB):
        t.step(V, lambda k=k: V.bn_stats(st[:, k, :], x[:, k, :]))
    t.step(V, *[lambda k=k: V.bn_aggr(mv[:, k, :], st[:, k, :]) for k in range(NB)])
    t.step(S, lambda: S.activation(rs[:, :].unsqueeze(2), mv[:, :, 1:2], ACT.Sqrt, bias=q.eps_c[:, 0:1]))
    t.step(V, lambda: V.reciprocal(rs[:, :], rs[:, :]))
    t.step(V, *[lambda k=k: V.tensor_scalar(z[:, k, :], x[:, k, :], mv[:, k, 0:1], rs[:, k:k + 1],
                                            ALU.subtract, ALU.mult) for k in range(NB)])


def layer0_nodes(nc, q):
    V, S, G, TE, SP, a, sb, pb = q.V, q.S, q.G, q.TE, q.SP, q.a, q.sb, q.pb
    chains = [Turns(q.sem(f"t_nodes{k}"), q.sem(f"t_nodes{k}_pool")) for k in range(K)]
    with ExitStack() as c:
        wup = sb(c, "wup", [C, 2, C])
        xin = a["x"].rearrange("(i k p) d -> i p k d", k=NB, p=P)
        table = q.table0.rearrange("(i k p) d -> i p k d", k=NB, p=P)

        def chain(t):
            x, z = (sb(c, n, [P, NB, D]) for n in ("x", "z"))
            st, mv, rs = sb(c, "st", [P, NB, 6]), sb(c, "mv", [P, NB, 2]), sb(c, "rs", [P, NB])
            hT = sb(c, "hT", [C, 4, W])
            up = sb(c, "up", [P, NB, D])
            banks = [pb(c, "bank", [P, 4 * P]) for _ in range(NB)]
            pT = [b[:C, :].rearrange("c (a n) -> c a n", a=4) for b in banks]
            pU = [b[:, 0:D] for b in banks]

            def body(i):
                t.dma(SP, lambda: SP.dma_start(x[:, :, :], xin[i, :, :, :]))
                norm_rows(t, V, S, q, x, z, st, mv, rs)
                t.step(TE, *[lambda k=k, pl=pl: TE.transpose(pT[k][:, pl, :], plane(z, k, pl), q.ident[:, :])
                             for k in range(NB) for pl in range(4)])
                t.step(S, *[lambda k=k: S.activation(hT[:, :, k * P:(k + 1) * P], pT[k], ACT.Relu)
                            for k in range(NB)])
                t.step(TE, *[lambda k=k, pl=pl: TE.matmul(pU[k][:, pl * C:(pl + 1) * C], hT[:, pl, k * P:(k + 1) * P],
                                                          wup[:, min(pl, 1), :], start=True, stop=True)
                             for k in range(NB) for pl in range(4)])
                t.step(S, *[lambda k=k: S.activation(up[:, k, :], pU[k], ACT.Copy) for k in range(NB)])
                t.dma(SP, lambda: SP.dma_start(table[i, :, :, :], up[:, :, :]),
                      lambda: SP.dma_start(q.hT_d[:, :, bass.ds(i * W, W)], hT[:, :, :]))
            return body

        bodies = [chain(t) for t in chains]
        chains[0].dma(SP, lambda: SP.dma_start(wup[:, 0, :], a["L0_gnn_W_up0"]),
                      lambda: SP.dma_start(wup[:, 1, :], a["L0_gnn_W_up1"]))
        chains[0].end(nc)
        chains_loop(nc, chains, NG // K, bodies)
        for t in chains:
            t.end(nc)


def plane(z, k, pl):
    return z[:, k, 0:C] if pl == 0 else z[:, k, C + pl - 1:D:3]


def layer0_edges(nc, q):
    a, sb, pb = q.a, q.sb, q.pb
    B = 4
    with ExitStack() as c:
        m1 = sb(c, "m1", [2 * R, 2 * HID])
        m23 = sb(c, "m23", [2 * HID, 2, 2 * HID])
        m4 = sb(c, "m4", [2 * HID, D])
        at = sb(c, "at", [2 * R, B, HALF])
        sh = sb(c, "sh", [P, B, 8, 4])
        ix = sb(c, "ix", [P, B, 8], I32)
        gb = sb(c, "gb", [P, B, 8, 4, C])
        r = sb(c, "r", [P, 2, HALF])
        r3 = sb(c, "r3", [P, 2, HALF])
        t02 = sb(c, "t02", [P, 2, 4, 2, C])
        sel = sb(c, "sel", [P, 2, 4, P])
        msg = sb(c, "msg", [P, 2, 4, 4, C])
        tmp = sb(c, "tmp", [P, 4, 3, C])
        qd = sb(c, "qd", [P, 4, C])
        p1 = sb(c, "p1", [P, 4, C])
        ost = sb(c, "ost", [P, 2, 4, D])
        pm = [pb(c, f"pm{k}", [P, HALF]) for k in range(2)]
        pt = [pb(c, f"pt{k}", [P, 4, D]) for k in range(2)]
        po = pb(c, "po", [P, 4, D])

        t = Turns(q.sem("t_w0"), q.sem("t_w0_pool"))
        V, SP, S = q.V, q.SP, q.S
        t.step(V, lambda: V.memset(m1[:, :], 0.0), lambda: V.memset(m23[:, :, :], 0.0))
        t.dma(SP, *[lambda g=g: SP.dma_start(m1[g * R:(g + 1) * R, g * HID:(g + 1) * HID], a["L0_gnn_M1"]) for g in range(2)],
              *[lambda g=g, n=n: SP.dma_start(m23[g * HID:(g + 1) * HID, n, g * HID:(g + 1) * HID], a[f"L0_gnn_M{n + 2}"])
                for g in range(2) for n in range(2)],
              *[lambda g=g: SP.dma_start(m4[g * HID:(g + 1) * HID, :], a["L0_gnn_M4"]) for g in range(2)])
        t.step(V, lambda: V.tensor_scalar(m4[:, 3 * C:D], m4[:, 3 * C:D], float(np.float32(1.0) / np.sqrt(np.float32(3.0))), None, ALU.mult))
        t.end(nc)


        s_at = [Signal(q.sem(f"at{g}"), inc=16) for g in range(B)]
        s_at[0].base = 16
        s_sh = [Signal(q.sem(f"sh{g}"), inc=16) for g in range(B)]
        s_ix = [Signal(q.sem(f"ix{g}"), inc=16) for g in range(B)]
        s_g = [Signal(q.sem(f"g{g}"), per=8, inc=16) for g in range(B)]
        s_mm = Signal(q.sem("mm"), per=3 * B)
        s_si = Signal(q.sem("si"), per=3 * B)
        s_mm.base = s_si.base = 3
        s_t = Signal(q.sem("t"), per=2 * B)
        s_ts = Signal(q.sem("ts"), per=2 * B)
        s_msg = Signal(q.sem("msg"), per=2 * B, ahead=1)
        s_sum = Signal(q.sem("sum"), per=2 * B, ahead=1)
        s_ev = Signal(q.sem("ev"), per=2 * B, ahead=1)
        s_st = [Signal(q.sem(f"st{k}"), per=B, inc=16, ahead=1) for k in range(2)]
        dv = Signal(q.sem("dv"), per=2 * B * 8)
        out_v = q.sums0_x.rearrange("(b j p) c -> b p j c", j=4, p=P)

        with nc.Block() as block:
            @block.sync
            def _(eng):
                for s in s_st:
                    s.prime(eng)

                def load(i, g):
                    eng.dma_start(ix[:, g, :], a["src_cols"][i * B + g, :, :]).then_inc(s_ix[g].sem, 16)
                    eng.dma_start(at[:, g, :], a["rbf"][i * B + g, :, :]).then_inc(s_at[g].sem, 16)
                    eng.dma_start(sh[:, g, :, :].rearrange("p t k -> p (t k)"), a["sh"][i * B + g, :, :]).then_inc(s_sh[g].sem, 16)

                def store(i, k):
                    s_ev.wait(eng, i, k)
                    eng.nop(nofuse=True)
                    eng.dma_start(out_v[i * (2 * B) + (k - 1), :, :, :], ost[:, k % 2, :, :]).then_inc(s_st[k % 2].sem, 16)

                for g in range(B):
                    load(0, g)
                with eng.Fori(0, SB) as i:
                    for g in range(B):
                        store(i, 2 * g + 1)
                        store(i, 2 * g + 2)
                        s_msg.wait(eng, i, 2 * g + 2)
                        eng.nop(nofuse=True)
                        load(i + 1, g)
                for k in (1, 2):
                    store(SB - 1, 2 * B + k)
                    s_st[k % 2].wait(eng, SB - 1, B + 1)
                for g in range(B):
                    for s in (s_ix[g], s_sh[g]):
                        s.wait(eng, SB)
                    eng.wait_ge(s_at[g].sem, 16 * (SB + 1))

            @block.gpsimd
            def _(eng):
                with eng.Fori(0, SB) as i:
                    for g in range(B):
                        s_ix[g].wait(eng, i)
                        s_msg.wait(eng, i, 2 * g + 2, back=1)
                        eng.nop(nofuse=True)
                        for j in range(8):
                            eng.indirect_dma_start(out=gb[:, g, j, :, :].rearrange("p a c -> p (a c)"), out_offset=None,
                                                   in_=q.table0[:, :],
                                                   in_offset=bass.IndirectOffsetOnAxis(ap=ix[:, g, j:j + 1], axis=0)).then_inc(s_g[g].sem, 16)

            @block.tensor
            def _(eng):
                s_sum.prime(eng)

                def mlp(n, g, parity):
                    lhsT, rhs = ((m1[:, :], at[:, g, :]), (m23[:, 0, :], r[:, 0, :]), (m23[:, 1, :], r[:, 1, :]))[n]
                    eng.matmul(pm[parity][:, :], lhsT, rhs, start=True, stop=True).then_inc(s_mm.sem, 1)

                def paths(g, half):
                    for j in range(4):
                        h0 = HID * half
                        ins = eng.matmul(pt[half][:, j, :], r3[h0:h0 + HID, g % 2, j * P:(j + 1) * P],
                                         m4[h0:h0 + HID, :], start=True, stop=True)
                    ins.then_inc(s_t.sem, 1)

                def sums(i, k):
                    s_msg.wait(eng, i, k - 2)
                    s_ev.wait(eng, i, k - 1)
                    for j in range(4):
                        ins = eng.matmul(po[:, j, :], sel[:, k % 2, j, :], msg[:, k % 2, j, :, :].rearrange("p a c -> p (a c)"),
                                         start=True, stop=True)
                    ins.then_inc(s_sum.sem, 1)

                eng.wait_ge(s_at[0].sem, 16)
                for n in range(3):
                    if n:
                        eng.wait_ge(s_si.sem, n)
                    mlp(n, 0, n % 2 == 0)
                with eng.Fori(0, SB) as i:
                    for g in range(B):
                        x = 3 * g
                        s_at[(g + 1) % B].wait(eng, i)
                        s_si.wait(eng, i, x)
                        mlp(0, (g + 1) % B, x % 2)
                        s_msg.wait(eng, i, 2 * g - 1)
                        paths(g, 0)
                        s_si.wait(eng, i, x + 1)
                        mlp(1, (g + 1) % B, (x + 1) % 2)
                        sums(i, 2 * g + 1)
                        s_msg.wait(eng, i, 2 * g)
                        paths(g, 1)
                        s_si.wait(eng, i, x + 2)
                        mlp(2, (g + 1) % B, x % 2)
                        sums(i, 2 * g + 2)
                for k in (1, 2):
                    sums(SB - 1, 2 * B + k)

            @block.scalar
            def _(eng):
                s_ev.prime(eng)

                def silu(n, g, parity):
                    dst = (r[:, 0, :], r[:, 1, :], r3[:, g % 2, :])[n]
                    eng.activation(dst, pm[parity][:, :], ACT.Silu).then_inc(s_si.sem, 1)

                def scaled(i, g, half):
                    k = 2 * g + 1 + half
                    s_t.wait(eng, i, k)
                    s_msg.wait(eng, i, k - 2)
                    for j in range(4):
                        ins = eng.activation(t02[:, half, j, :, :],
                                             pt[half][:, j, :].rearrange("p (a c) -> p a c", c=C)[:, 0:3:2, :],
                                             ACT.Copy, scale=sh[:, g, 4 * half + j, 0:1])
                    ins.then_inc(s_ts.sem, 1)

                def evac(i, k):
                    s_sum.wait(eng, i, k)
                    s_st[k % 2].wait(eng, i, (k + 1) // 2 - 1)
                    for j in (0, 2):
                        ins = eng.activation(ost[:, k % 2, j:j + 2, :], po[:, j:j + 2, :], ACT.Copy)
                    ins.then_inc(s_ev.sem, 1)

                for n in range(3):
                    eng.wait_ge(s_mm.sem, n + 1)
                    silu(n, 0, n % 2 == 0)
                with eng.Fori(0, SB) as i:
                    for g in range(B):
                        x = 3 * g
                        s_mm.wait(eng, i, x + 1)
                        silu(0, g + 1, x % 2)
                        s_sh[g].wait(eng, i)
                        scaled(i, g, 0)
                        s_mm.wait(eng, i, x + 2)
                        silu(1, g + 1, (x + 1) % 2)
                        evac(i, 2 * g + 1)
                        scaled(i, g, 1)
                        s_mm.wait(eng, i, x + 3)
                        silu(2, g + 1, x % 2)
                        evac(i, 2 * g + 2)
                for k in (1, 2):
                    evac(SB - 1, 2 * B + k)

            @block.vector
            def _(eng):
                eng.memset(sel[:, :, :, :], 0.0)
                eng.memset(msg[:, :, :, :, :], 0.0).then_inc(s_msg.sem, s_msg.base)
                with eng.Fori(0, SB) as i:
                    n = 0

                    def own(ins):
                        nonlocal n
                        n += 1
                        ins.then_inc(dv.sem, 1)
                        return n

                    for k in range(1, 2 * B + 1):
                        g, half, b = (k - 1) // 2, (k - 1) % 2, k % 2
                        ts = slice(4 * half, 4 * half + 4)
                        x0 = gb[:, g, ts, 0, :]
                        x1 = gb[:, g, ts, 1:4, :]
                        s1 = bc(sh[:, g, ts, 1:4], 3, [P, 4, 3, C])
                        w = pt[half][:, :, :].rearrange("p t (a c) -> p t a c", c=C)
                        s_sum.wait(eng, i, k)
                        eng.tensor_tensor(sel[:, b, :, :], bc(q.lastpos[:, bass.ds(i * SBT + 4 * (k - 1), 4)], 2, [P, 4, P]),
                                          bc(q.iota_f[:, :], 1, [P, 4, P]), ALU.is_equal)
                        if half == 0:
                            s_g[g].wait(eng, i)
                            s_sh[g].wait(eng, i)
                        s_msg.wait(eng, i, k - 1)
                        k1 = own(eng.tensor_tensor(tmp[:, :, :, :], x1, s1, ALU.mult))
                        dv.wait(eng, i, k1)
                        k2 = own(eng.tensor_tensor(qd[:, :, :], tmp[:, :, 0, :], tmp[:, :, 1, :], ALU.add))
                        dv.wait(eng, i, k2)
                        k3 = own(eng.tensor_tensor(qd[:, :, :], qd[:, :, :], tmp[:, :, 2, :], ALU.add))
                        s_ts.wait(eng, i, k)
                        k4 = own(eng.tensor_tensor(p1[:, :, :], x0, w[:, :, 1, :], ALU.mult))
                        dv.wait(eng, i, k3)
                        k5 = own(eng.tensor_tensor(qd[:, :, :], qd[:, :, :], w[:, :, 3, :], ALU.mult))
                        dv.wait(eng, i, k4)
                        k6 = own(eng.tensor_tensor(msg[:, b, :, 1:4, :], bc(p1[:, :, :], 2, [P, 4, 3, C]), s1, ALU.mult))
                        k7 = own(eng.tensor_tensor(tmp[:, :, :, :], x1, bc(t02[:, half, :, 1, :], 2, [P, 4, 3, C]), ALU.mult))
                        k8 = own(eng.tensor_tensor(msg[:, b, :, 0, :], x0, t02[:, half, :, 0, :], ALU.mult))
                        dv.wait(eng, i, k7)
                        eng.tensor_tensor(msg[:, b, :, 1:4, :], msg[:, b, :, 1:4, :], tmp[:, :, :, :], ALU.add)
                        dv.wait(eng, i, k8)
                        eng.tensor_tensor(msg[:, b, :, 0, :], msg[:, b, :, 0, :], qd[:, :, :], ALU.add).then_inc(s_msg.sem, 1)
                    assert n == dv.per


def stitch(nc, q, sums, cw, name):
    V, S, G, TE, SP, sb, pb = q.V, q.S, q.G, q.TE, q.SP, q.sb, q.pb
    gat = cw > D
    base, skip = (sums, 0) if gat else (q.sums0_x, q.spare)
    t = Turns(q.sem("t_" + name), q.sem("t_" + name + "_pool"))
    CK = T // 4
    with ExitStack() as c:
        tl, hd, cp = (sb(c, f"{n}_{name}", [TP, TG, cw]) for n in ("tl", "hd", "cp"))
        tT = sb(c, "tT_" + name, [P, 2, T])
        cb = sb(c, "cb_" + name, [P, 2, 1 + T])
        ps = [pb(c, f"ps{k}_{name}", [P, 4, P]) for k in range(2)]
        t.dma(SP, lambda: SP.dma_start(tl[:, :, :], sums.rearrange("(g p e) c -> p g e c", p=TP, e=P)[:, :, P - 1, :]))
        t.dma(G, pool=True, *[lambda g=g: G.indirect_dma_start(out=hd[:, g, :], out_offset=None, in_=base,
                   element_offset=skip, in_offset=bass.IndirectOffsetOnAxis(ap=q.head_idx[:, g:g + 1], axis=0)) for g in range(TG)])
        for g in range(TG):
            t.step(TE, *[lambda j=j, g=g: TE.transpose(ps[0][:, j, 0:TP], tl[:, g, j * P:(j + 1) * P], q.ident[:TP, :TP])
                         for j in range(2)])
            t.step(V, lambda g=g: V.tensor_copy(tT[:, :, g * TP:(g + 1) * TP], ps[0][:, 0:2, 0:TP]))
        t.step(V, lambda: V.memset(cb[:, :, 0:1], 0.0))
        if gat:
            dT, mT, al, gm = (sb(c, f"{n}_{name}", [H, T]) for n in ("dT", "mT", "al", "gm"))
            cd, cm = (sb(c, f"{n}_{name}", [H, 1 + T]) for n in ("cd", "cm"))
            gB = sb(c, "gB_" + name, [P, T])
            hs = sb(c, "hs_" + name, [H, D])
            for g in range(TG):
                t.step(TE, *[lambda j=j, g=g: TE.transpose(ps[1][:H, j, 0:TP], tl[:, g, D + j * H:D + (j + 1) * H], q.ident[:TP, :TP])
                             for j in range(2)])
                t.step(V, lambda g=g: V.tensor_copy(dT[:, g * TP:(g + 1) * TP], ps[1][:H, 0, 0:TP]),
                       lambda g=g: V.tensor_copy(mT[:, g * TP:(g + 1) * TP], ps[1][:H, 1, 0:TP]))
            t.step(V, lambda: V.tensor_scalar(gm[:, :], q.whole[:H, :], BIG, -BIG, ALU.mult, ALU.add),
                   lambda: V.memset(cd[:, 0:1], 0.0), lambda: V.memset(cm[:, 0:1], -BIG))
            t.step(V, lambda: V.tensor_tensor_scan(cm[:, 1:], gm[:, :], mT[:, :], -BIG, ALU.add, ALU.max))
            t.step(V, lambda: V.tensor_tensor(al[:, :], mT[:, :], cm[:, 1:], ALU.subtract),
                   lambda: V.tensor_tensor(gm[:, :], cm[:, 0:T], cm[:, 1:], ALU.subtract))
            t.step(V, lambda: V.tensor_scalar(gm[:, :], gm[:, :], 0.0, None, ALU.min))
            t.step(S, lambda: S.activation(al[:, :], al[:, :], ACT.Exp), lambda: S.activation(gm[:, :], gm[:, :], ACT.Exp))
            t.step(V, lambda: V.tensor_tensor(gm[:, :], gm[:, :], q.whole[:H, :], ALU.mult))
            t.step(V, lambda: V.tensor_tensor(dT[:, :], dT[:, :], al[:, :], ALU.mult))
            t.step(V, lambda: V.tensor_tensor_scan(cd[:, 1:], gm[:, :], dT[:, :], 0.0, ALU.mult, ALU.add))
            t.step(V, lambda: V.tensor_copy(hs[:, :].rearrange("h (k c) -> h k c", c=C), bc(q.ident[:H, :H], 2, [H, H, C])))
            pf = pb(c, "pf_" + name, [P, 2, 512])
            for j in range(2):
                for x in range(4):
                    xs = slice(x * CK, (x + 1) * CK)
                    t.step(TE, lambda j=j, xs=xs: TE.matmul(pf[:, 0, 0:CK], hs[:, j * P:(j + 1) * P], al[:, xs], start=True, stop=True),
                           lambda j=j, xs=xs: TE.matmul(pf[:, 1, 0:CK], hs[:, j * P:(j + 1) * P], gm[:, xs], start=True, stop=True))
                    t.step(V, lambda j=j, xs=xs: V.tensor_tensor(tT[:, j, xs], tT[:, j, xs], pf[:, 0, 0:CK], ALU.mult),
                           lambda xs=xs: V.tensor_copy(gB[:, xs], pf[:, 1, 0:CK]))
                t.step(V, lambda j=j: V.tensor_tensor_scan(cb[:, j, 1:], gB[:, :], tT[:, j, :], 0.0, ALU.mult, ALU.add))
        else:
            t.step(V, *[lambda j=j: V.tensor_tensor_scan(cb[:, j, 1:], q.whole[:, :], tT[:, j, :], 0.0, ALU.mult, ALU.add)
                        for j in range(2)])
        for g in range(TG):
            xs = slice(g * TP, (g + 1) * TP)
            t.step(TE, *[lambda j=j, xs=xs: TE.transpose(ps[0][:TP, j, :], cb[:, j, xs], q.ident[:, :]) for j in range(2)],
                   *([lambda j=j, m=m, xs=xs: TE.transpose(ps[1][:TP, j, 0:H], m[:, xs], q.ident[:H, :H])
                      for j, m in enumerate((cd, cm))] if gat else []))
            t.step(V, lambda g=g: V.tensor_copy(cp[:, g, 0:D].rearrange("p (j c) -> p j c", j=2), ps[0][:TP, 0:2, :]),
                   *([lambda g=g: V.tensor_copy(cp[:, g, D:GR].rearrange("p (j c) -> p j c", j=2), ps[1][:TP, 0:2, 0:H])]
                     if gat else []))
        if gat:
            mx = sb(c, "mx_" + name, [TP, TG, H])
            heads = lambda x: x[:, :, 0:D].rearrange("p g (h c) -> p g h c", c=C)
            t.step(V, lambda: V.tensor_tensor(mx[:, :, :], hd[:, :, D + H:GR], cp[:, :, D + H:GR], ALU.max))
            for x in (hd, cp):
                t.step(V, lambda x=x: V.tensor_tensor(x[:, :, D + H:GR], x[:, :, D + H:GR], mx[:, :, :], ALU.subtract))
                t.step(S, lambda x=x: S.activation(x[:, :, D + H:GR], x[:, :, D + H:GR], ACT.Exp))
                for g in range(TG):
                    t.step(V, lambda x=x, g=g: V.tensor_tensor(heads(x)[:, g, :, :], heads(x)[:, g, :, :],
                                                             bc(x[:, g, D + H:GR], 2, [TP, H, C]), ALU.mult))
                t.step(V, lambda x=x: V.tensor_tensor(x[:, :, D:D + H], x[:, :, D:D + H], x[:, :, D + H:GR], ALU.mult))
        t.step(V, lambda: V.tensor_tensor(hd[:, :, :], hd[:, :, :], cp[:, :, :], ALU.add))
        t.dma(G, pool=True, *[lambda g=g: G.indirect_dma_start(out=base, element_offset=skip, out_offset=bass.IndirectOffsetOnAxis(ap=q.fix_idx[:, g:g + 1], axis=0),
                                                    in_=hd[:, g, :], in_offset=None, bounds_check=EP - 1, oob_is_err=False)
                   for g in range(TG)])
        t.end(nc)


def node_rows(t, q, base, skip, i, ixn, rows):
    V, G = q.V, q.G
    t.step(V, lambda: V.tensor_copy(ixn[:, :], q.row_idx[:, bass.ds(i * NB, NB)]))
    t.dma(G, pool=True, *[lambda k=k: G.indirect_dma_start(out=rows[:, k, :], out_offset=None, in_=base, element_offset=skip,
               in_offset=bass.IndirectOffsetOnAxis(ap=ixn[:, k:k + 1], axis=0)) for k in range(NB)])


def layer0_update(nc, q):
    V, S, G, TE, SP, a, sb, pb = q.V, q.S, q.G, q.TE, q.SP, q.a, q.sb, q.pb
    chains = [Turns(q.sem(f"t_upd{k}"), q.sem(f"t_upd{k}_pool")) for k in range(K)]
    t0 = chains[0]
    with ExitStack() as c:
        wl = sb(c, "wl", [P, 2, C])
        ws = sb(c, "ws", [P, 2, C])
        wc = sb(c, "wc", [C, 9])
        gmm = sb(c, "gmm", [C, 3])
        bst = sb(c, "bst", [C, FULL + 1, 6])
        ss = sb(c, "ss", [C, 3, FULL + 1])
        mv = sb(c, "mv_u", [C, 2])

        def chain(t):
            ixn = sb(c, "ixn", [P, NB], I32)
            rows = sb(c, "rows", [P, NB, D])
            gT = sb(c, "gT", [P, 2, W])
            sq = sb(c, "sq", [C, 3, W])
            a0, a0s, pp, rr, vv = (sb(c, n, [C, W]) for n in ("a0", "a0s", "pp", "rr", "vv"))
            bh = sb(c, "bh", [P, 4, W])
            oT = sb(c, "oT", [C, 4, W])
            banks = [pb(c, "bank", [P, 2, W]) for _ in range(2)]
            pG = [b[:, 0, :] for b in banks]
            pA = pO = [banks[pl % 2][:C, pl // 2, :] for pl in range(4)]

            def body(i, width=W):
                node_rows(t, q, q.sums0_x, q.spare, i, ixn, rows)
                t.dma(SP, lambda: SP.dma_start(bh[C:P, :, :], q.hT_d[:, :, bass.ds(i * W, W)]))
                t.step(V, lambda: V.tensor_tensor(rows[:, :, :], rows[:, :, :], bc(q.some[:, bass.ds(i * NB, NB)], 2, [P, NB, D]), ALU.mult))
                t.step(TE, *[lambda j=j, k=k: TE.transpose(pG[j][:, k * P:(k + 1) * P], rows[:, k, j * P:(j + 1) * P], q.ident[:, :])
                             for j in range(2) for k in range(NB)])
                t.step(S, *[lambda j=j: S.activation(gT[:, j, :], pG[j], ACT.Copy) for j in range(2)])
                t.step(TE, *[lambda pl=pl: TE.matmul(pA[pl], wl[C * (pl % 2):C * (pl % 2) + C, min(pl, 1), :],
                                                     gT[C * (pl % 2):C * (pl % 2) + C, pl // 2, :], start=True, stop=True) for pl in range(4)])
                t.step(S, lambda: S.activation(a0[:, :], pA[0], ACT.Copy),
                       lambda: S.activation(a0s[:, :], pA[0], ACT.Square),
                       *[lambda x=x: S.activation(sq[:, x, :], pA[1 + x], ACT.Square) for x in range(3)])
                tt = lambda o, x, y, op: t.step(V, lambda: V.tensor_tensor(o, x, y, op))
                stt = lambda o, x, w, y: lambda: V.scalar_tensor_tensor(o, x, wc[:, w:w + 1], y, ALU.mult, ALU.add)
                t.step(V, lambda: V.tensor_scalar(pp[:, :], a0s[:, :], wc[:, 3:4], wc[:, 0:1], ALU.mult, ALU.add),
                       lambda: V.tensor_scalar(rr[:, :], a0s[:, :], wc[:, 7:8], wc[:, 5:6], ALU.mult, ALU.add),
                       lambda: V.tensor_tensor(vv[:, :], sq[:, 0, :], sq[:, 1, :], ALU.add))
                t.step(V, stt(pp[:, :], a0[:, :], 1, pp[:, :]), stt(rr[:, :], a0[:, :], 6, rr[:, :]),
                       lambda: V.tensor_tensor(vv[:, :], vv[:, :], sq[:, 2, :], ALU.add))
                t.step(V, stt(pp[:, :], vv[:, :], 4, pp[:, :]), stt(rr[:, :], vv[:, :], 8, rr[:, :]))
                tt(pp[:, :], pp[:, :], a0[:, :], ALU.mult)
                t.step(V, stt(bh[0:C, 0, :], vv[:, :], 2, pp[:, :]),
                       *[lambda x=x: V.tensor_tensor(bh[0:C, 1 + x, :], rr[:, :], pA[1 + x], ALU.mult) for x in range(3)])
                t.step(TE, *[lambda pl=pl: TE.matmul(pO[pl], ws[:, min(pl, 1), :], bh[:, pl, :], start=True, stop=True) for pl in range(4)])
                if width:
                    t.step(V, lambda: V.bn_stats(bst[:, bass.ds(i, 1), :].rearrange("p a b -> p (a b)"), pO[0][:, 0:width]))
                    t.step(S, *[lambda x=x: S.activation(sq[:, x, 0:width], pO[1 + x][:, 0:width], ACT.Square,
                                                         accum_out=ss[:, x, bass.ds(i, 1)]) for x in range(3)])
                t.step(S, *[lambda pl=pl: S.activation(oT[:, pl, :], pO[pl], ACT.Copy) for pl in range(4)])
                t.dma(SP, lambda: SP.dma_start(q.oT_d[:, :, bass.ds(i * W, W)], oT[:, :, :]))
            return body

        bodies = [chain(t) for t in chains]
        t0.dma(SP, *[lambda h=h, n=n: SP.dma_start(wl[h * C:(h + 1) * C, n, :], a[f"L0_gnn_W_lin{n}"]) for h in range(2) for n in range(2)],
               *[lambda h=h, n=n, v=v: SP.dma_start(ws[h * C:(h + 1) * C, n, :], a[f"L0_gnn_{v}{n}"]) for h, v in enumerate(("WB", "Wsc")) for n in range(2)],
               lambda: SP.dma_start(wc[:, 0:5], a["L0_gnn_Wc0"]), lambda: SP.dma_start(wc[:, 5:9], a["L0_gnn_Wc1"]),
               *[lambda k=k, n=n: SP.dma_start(gmm[:, k:k + 1], a["L0_gnn_" + n].unsqueeze(1)) for k, n in enumerate(("gamma0", "beta0", "gamma1"))])
        t0.end(nc)
        chains_loop(nc, chains, FULL // K, bodies)
        for g0 in range(FULL, NG, K):
            side_by_side([queued(t, lambda g: bodies[g - g0](g, LAST if g == FULL else 0), g0 + k) for k, t in enumerate(chains)])
        for t in chains:
            t.end(nc)
        t = t0
        t.step(V, lambda: V.bn_aggr(mv[:, :], bst[:, :, :].rearrange("p a b -> p (a b)")))
        t.step(V, lambda: V.tensor_reduce(q.stat[:, 3:4], ss[:, :, :].rearrange("p a b -> p (a b)"), mybir.AxisListType.X, ALU.add))
        t.step(S, lambda: S.activation(q.stat[:, 0:1], mv[:, 1:2], ACT.Sqrt, bias=q.eps_c[:C, 0:1]),
               lambda: S.activation(q.stat[:, 2:3], q.stat[:, 3:4], ACT.Sqrt, scale=1.0 / (3.0 * N), bias=q.eps_c[:C, 0:1]))
        t.step(V, lambda: V.reciprocal(q.stat[:, 0:1], q.stat[:, 0:1]), lambda: V.reciprocal(q.stat[:, 2:3], q.stat[:, 2:3]))
        t.step(V, lambda: V.tensor_tensor(q.stat[:, 0:3:2], q.stat[:, 0:3:2], gmm[:, 0:3:2], ALU.mult))
        t.step(V, lambda: V.tensor_tensor(q.stat[:, 1:2], mv[:, 0:1], q.stat[:, 0:1], ALU.mult))
        t.step(V, lambda: V.tensor_tensor(q.stat[:, 1:2], gmm[:, 1:2], q.stat[:, 1:2], ALU.subtract))
        t.end(nc)


class Features:

    @staticmethod
    def weights(t, q, c, n):
        V, SP, a = q.V, q.SP, q.a
        w = q.sb(c, "we", [P, 2, D + 2 * H])
        alr = q.sb(c, "alr", [P, 2, D])
        wt = q.sb(c, "wt", [P, 2, D])
        t.dma(SP, lambda: SP.dma_start(w[:, :, 0:D], a[f"L1_gnn_W{n}"].rearrange("(j p) c -> p j c", p=P)),
              *[lambda k=k, v=v: SP.dma_start(alr[:, k, :], a[f"L1_gnn_{v}{n}"].rearrange("h c -> (h c)").partition_broadcast(P))
                for k, v in enumerate(("al", "ar"))])
        for k in range(2):
            t.step(V, lambda k=k: V.tensor_tensor(wt[:, :, :], w[:, :, 0:D], bc(alr[:, k, :], 1, [P, 2, D]), ALU.mult))
            t.step(V, lambda k=k: V.tensor_reduce(w[:, :, D + k * H:D + (k + 1) * H],
                                                  wt[:, :, :].rearrange("p j (h c) -> p j h c", c=C), mybir.AxisListType.X, ALU.add))
        return w

    def __init__(self, t, q, c, w, banks):
        self.t, self.q, self.w = t, q, w
        self.hT = q.sb(c, "hT_p", [P, 2, W])
        self.f = q.sb(c, "f_p", [P, NB, D + H])
        self.er = q.sb(c, "er_p", [P, NB, H])
        self.ix = q.sb(c, "ix_p", [P, NB], I32)
        self.pZ = [b[:, 0:W] for b in banks]
        self.pF = [b[:, 0:D + 2 * H] for b in banks]

    def emit(self, i, z, func):
        t, q = self.t, self.q
        V, S, TE, SP = q.V, q.S, q.TE, q.SP
        t.step(TE, *[lambda j=j, k=k: TE.transpose(self.pZ[j][:, k * P:(k + 1) * P], z[:, k, j * P:(j + 1) * P], q.ident[:, :])
                     for j in range(2) for k in range(NB)])
        t.step(S, *[lambda j=j: S.activation(self.hT[:, j, :], self.pZ[j], func) for j in range(2)])
        t.step(TE, *[lambda j=j, k=k: TE.matmul(self.pF[k], self.hT[:, j, k * P:(k + 1) * P], self.w[:, j, :],
                                                start=j == 0, stop=j == 1) for k in range(NB) for j in range(2)])
        t.step(S, *[lambda k=k: S.activation(self.f[:, k, :], self.pF[k][:, 0:D + H], ACT.Copy) for k in range(NB)],
               *[lambda k=k: S.activation(self.er[:, k, :], self.pF[k][:, D + H:], ACT.Copy) for k in range(NB)])
        rows = lambda x: x.rearrange("(i k p) d -> i p k d", k=NB, p=P)[i, :, :, :]
        t.step(V, lambda: V.tensor_copy(self.ix[:, :], q.first_idx[:, bass.ds(i * NB, NB)]))
        t.dma(q.G, pool=True, *[lambda k=k: q.G.indirect_dma_start(
            out=q.er_start, out_offset=bass.IndirectOffsetOnAxis(ap=self.ix[:, k:k + 1], axis=0),
            in_=self.er[:, k, :], in_offset=None, bounds_check=EP - 1, oob_is_err=False) for k in range(NB)])
        t.dma(SP, lambda: SP.dma_start(rows(q.table1), self.f[:, :, :]), lambda: SP.dma_start(rows(q.er_d), self.er[:, :, :]))


def layer0_norm_and_gat_nodes(nc, q):
    V, S, G, TE, SP, a, sb, pb = q.V, q.S, q.G, q.TE, q.SP, q.a, q.sb, q.pb
    chains = [Turns(q.sem(f"t_n1_{k}"), q.sem(f"t_n1_{k}_pool")) for k in range(K)]
    rows = lambda y, i: y.rearrange("(i k p) d -> i p k d", k=NB, p=P)[i, :, :, :]
    with ExitStack() as c:
        w = Features.weights(chains[0], q, c, 1)
        chains[0].end(nc)

        def chain(t):
            oT = sb(c, "oT_n", [C, 4, W])
            x, z = sb(c, "x_n", [P, NB, D]), sb(c, "z_n", [P, NB, D])
            st, mv, rs = sb(c, "st_n", [P, NB, 6]), sb(c, "mv_n", [P, NB, 2]), sb(c, "rs_n", [P, NB])
            banks = [pb(c, "bank", [P, 4 * P]) for _ in range(NB)]
            pN = banks[0][:, :].rearrange("p (k a c) -> p k a c", k=NB, c=C)
            ft = Features(t, q, c, w, banks)

            def body(i):
                t.dma(SP, lambda: SP.dma_start(oT[:, :, :], q.oT_d[:, :, bass.ds(i * W, W)]),
                      lambda: SP.dma_start(x[:, :, :], rows(a["x"], i)))
                t.step(S, lambda: S.activation(oT[:, 0, :], oT[:, 0, :], ACT.Identity, scale=q.stat[:, 0:1], bias=q.stat[:, 1:2]),
                       lambda: S.activation(oT[:, 1:4, :], oT[:, 1:4, :], ACT.Copy, scale=q.stat[:, 2:3]))
                t.step(TE, *[lambda k=k, pl=pl: TE.transpose(pN[:, k, pl, :], oT[:, pl, k * P:(k + 1) * P], q.ident[:C, :C])
                             for k in range(NB) for pl in range(4)])
                t.step(V, *[lambda k=k: V.tensor_tensor(x[:, k, 0:C], x[:, k, 0:C], pN[:, k, 0, :], ALU.add) for k in range(NB)],
                       *[lambda k=k: V.tensor_tensor(x[:, k, C:D].rearrange("p (c x) -> p x c", x=3),
                                                     x[:, k, C:D].rearrange("p (c x) -> p x c", x=3),
                                                     pN[:, k, 1:4, :], ALU.add) for k in range(NB)])
                t.dma(SP, lambda: SP.dma_start(rows(q.x1_d, i), x[:, :, :]))
                norm_rows(t, V, S, q, x, z, st, mv, rs)
                ft.emit(i, z, ACT.Relu)
            return body

        chains_loop(nc, chains, NG // K, [chain(t) for t in chains])
        for t in chains:
            t.end(nc)


def spread_er(nc, q, n):
    V, S, G, TE, SP, a, sb, pb = q.V, q.S, q.G, q.TE, q.SP, q.a, q.sb, q.pb
    t = Turns(q.sem(f"t_er{n}"), q.sem(f"t_er{n}_pool"))
    with ExitStack() as c:
        ch, held = sb(c, "ch", [P, CH, H]), sb(c, "held", [P, H, CH])
        ini = sb(c, "ini", [P, H])
        t.dma(G, pool=True, *[lambda: G.indirect_dma_start(out=ini[:, :], out_offset=None, in_=q.er_d,
                                              in_offset=bass.IndirectOffsetOnAxis(ap=q.chunk_node[:, 0:1], axis=0))])
        t.dma(SP, lambda: SP.dma_start(ch[:, :, :].rearrange("p e h -> p (e h)"), q.er_start.rearrange("(p e) h -> p (e h)", p=P)))
        t.step(V, *[lambda h=h: V.tensor_tensor_scan(held[:, h, :], q.samep[:, :], ch[:, :, h], ini[:, h:h + 1], ALU.mult, ALU.add)
                    for h in range(H)])
        t.dma(SP, lambda: SP.dma_start(q.er_edge.rearrange("h (p e) -> p h e", p=P), held[:, :, :]))
        t.end(nc)


def gat_edges(nc, q, n):
    a, sb, pb = q.a, q.sb, q.pb
    FR = D + H
    NQ = SBT // 4
    with ExitStack() as c:
        er = sb(c, f"er_g{n}", [P, SB, P])
        ix = sb(c, f"ix_g{n}", [P, 2, SBT], I32)
        gb = sb(c, f"gb_g{n}", [P, 2, SBT, FR])
        elc = sb(c, f"elc{n}", [P, H, SBT])
        fs, mm_, ee, ww = (sb(c, f"{x}{n}", [P, P]) for x in ("fs", "mm_", "ee", "ww"))
        mT = sb(c, f"mT_g{n}", [P, 2, SBT, H])
        sel = sb(c, f"sel_g{n}", [P, 2, 4, P])
        ost = sb(c, f"ost_g{n}", [P, 2, 4, GR])
        pE = pb(c, f"pE{n}", [P, P])
        pW = pb(c, f"pW{n}", [P, 2, P])
        po = [pb(c, f"po{k}_{n}", [P, 2, 512]) for k in range(2)]

        nm = lambda x: f"{x}_g{n}"
        s_er = q.sem(nm("er"))
        s_ix = [Signal(q.sem(nm(f"ix{p}")), inc=16) for p in range(2)]
        s_g = [Signal(q.sem(nm(f"g{p}")), per=SBT, inc=16) for p in range(2)]
        s_elc = Signal(q.sem(nm("elc")))
        s_elT = Signal(q.sem(nm("elT")))
        s_d = Signal(q.sem(nm("d")))
        s_w = Signal(q.sem(nm("w")))
        s_wT = Signal(q.sem(nm("wT")))
        s_we = Signal(q.sem(nm("we")))
        s_msg = Signal(q.sem(nm("msg")), per=NQ)
        s_sum = Signal(q.sem(nm("sum")), per=2 * NQ, ahead=2)
        s_ev = Signal(q.sem(nm("ev")), per=2 * NQ, ahead=1)
        s_st = [Signal(q.sem(nm(f"st{p}")), per=NQ // 2, inc=16, ahead=1) for p in range(2)]
        dv = Signal(q.sem(nm("dv")), per=6)
        out_v = q.sums1.rearrange("(b j p) c -> b p j c", j=4, p=P)

        def over(eng, body, first=None):
            if first:
                first()
            with eng.Fori(0, SB // 2) as i:
                for p in range(2):
                    body(i * 2 + p, i, p, False)
            body(SB - 1, SB // 2, 0, True)

        assert SB % 2 == 1
        PREP = (NQ - 2, NQ - 1)

        with nc.Block() as block:
            @block.sync
            def _(eng):
                for s in s_st:
                    s.prime(eng)
                view = q.er_edge.rearrange("h (s t e) -> h t s e", t=SBT, e=P)
                for h in range(H):
                    eng.dma_start(er[h * SBT:(h + 1) * SBT, :, :], view[h, :, :, :]).then_inc(s_er, 16)

                def indices(s, p):
                    eng.dma_start(ix[:, p, :].rearrange("p (g j) -> p g j", j=8),
                                  a["src_cols"].rearrange("(s g) p j -> s p g j", g=4)[s, :, :, :]).then_inc(s_ix[p].sem, 16)

                def body(s, i, p, last):
                    if not last:
                        s_sum.wait(eng, s, 1)
                        eng.nop(nofuse=True)
                        indices(i * 2 + (p + 2), p)
                    for k in range(1, NQ + 1):
                        s_ev.wait(eng, s, 2 * k)
                        eng.nop(nofuse=True)
                        eng.dma_start(out_v[s * NQ + (k - 1), :, :, :], ost[:, k % 2, :, :]).then_inc(s_st[k % 2].sem, 16)

                def first():
                    indices(0, 0)
                    indices(1, 1)

                over(eng, body, first)
                s_ix[1].wait(eng, SB // 2)
                for s in s_st:
                    s.wait(eng, SB - 1)

            @block.gpsimd
            def _(eng):
                def body(s, i, p, last):
                    s_ix[p].wait(eng, i)
                    for k in range(1, NQ + 1):
                        s_sum.wait(eng, s, 2 * k, back=2)
                        eng.nop(nofuse=True)
                        for j in range(4 * k - 4, 4 * k):
                            eng.indirect_dma_start(out=gb[:, p, j, :], out_offset=None, in_=q.table1[:, :],
                                                   in_offset=bass.IndirectOffsetOnAxis(ap=ix[:, p, j:j + 1], axis=0)).then_inc(s_g[p].sem, 16)
                over(eng, body)

            @block.tensor
            def _(eng):
                s_sum.prime(eng)

                def el_rows(s):
                    s_elc.wait(eng, s)
                    eng.transpose(pE[:, :], elc[:, :, :].rearrange("p h t -> p (h t)"), q.ident[:, :]).then_inc(s_elT.sem, 1)

                def weights_back(s):
                    s_w.wait(eng, s)
                    eng.transpose(pW[:, 0, :], ww[:, :], q.ident[:, :])
                    eng.transpose(pW[:, 1, :], mm_[:, :], q.ident[:, :]).then_inc(s_wT.sem, 1)

                def first():
                    el_rows(0)
                    weights_back(0)

                def body(s, i, p, last):
                    for k in range(1, NQ + 1):
                        s_msg.wait(eng, s, k)
                        for x in range(2):
                            s_ev.wait(eng, s, 2 * k + x - 3)
                            for j in range(2):
                                tl = 4 * (k - 1) + 2 * x + j
                                ins = eng.matmul(po[x][:, j, 0:FR], sel[:, k % 2, 2 * x + j, :], gb[:, p, tl, :], start=True, stop=True)
                            ins.then_inc(s_sum.sem, 1)
                        if k in PREP and not last:
                            (el_rows, weights_back)[PREP.index(k)](s + 1)
                over(eng, body, first)

            @block.scalar
            def _(eng):
                s_ev.prime(eng)

                def el_side_by_side(s, i, p):
                    s_g[p].wait(eng, i)
                    eng.activation(elc[:, :, :], gb[:, p, :, D:FR].rearrange("p t h -> p h t"), ACT.Copy).then_inc(s_elc.sem, 1)
                    s_d.wait(eng, s)
                    eng.activation(ww[:, :], ee[:, :], ACT.Exp).then_inc(s_w.sem, 1)

                def weights_in_place(s, i, p):
                    s_wT.wait(eng, s)
                    view = lambda k: pW[:, k, :].rearrange("p (h t) -> p t h", t=SBT)
                    eng.activation(gb[:, p, :, D:FR], view(0), ACT.Copy)
                    eng.activation(mT[:, p, :, :], view(1), ACT.Copy).then_inc(s_we.sem, 1)

                def first():
                    el_side_by_side(0, 0, 0)
                    weights_in_place(0, 0, 0)

                def body(s, i, p, last):
                    s_we.wait(eng, s)
                    for k in range(1, NQ + 1):
                        s_st[k % 2].wait(eng, s, (k + 1) // 2 - 1)
                        for x in range(2):
                            tl = 4 * (k - 1) + 2 * x
                            eng.activation(ost[:, k % 2, 2 * x:2 * x + 2, FR:GR], mT[:, p, tl:tl + 2, :], ACT.Copy)
                            s_sum.wait(eng, s, 2 * k + x - 1)
                            eng.activation(ost[:, k % 2, 2 * x:2 * x + 2, 0:FR], po[x][:, :, 0:FR], ACT.Copy).then_inc(s_ev.sem, 1)
                        if k in PREP and not last:
                            (el_side_by_side, weights_in_place)[PREP.index(k)](s + 1, i + p, 1 - p)
                over(eng, body, first)

            @block.vector
            def _(eng):
                eng.wait_ge(s_er, 16 * H)

                def weights(s):
                    er_s = er[:, bass.ds(s, 1), :].rearrange("p a e -> p (a e)")
                    f_m, b_m = (m[:, bass.ds(s, 1), :].rearrange("p a e -> p (a e)") for m in (q.start_f, q.start_b))
                    s_elT.wait(eng, s)
                    eng.tensor_tensor_scan(fs[:, :], f_m, pE[:, :], -BIG, ALU.add, ALU.max).then_inc(dv.sem, 1)
                    eng.tensor_tensor(ee[:, :], pE[:, :], er_s, ALU.add).then_inc(dv.sem, 1)
                    dv.wait(eng, s, 1)
                    eng.tensor_tensor_scan(mm_[:, ::-1], b_m, fs[:, ::-1], -BIG, ALU.add, ALU.max).then_inc(dv.sem, 1)
                    dv.wait(eng, s, 2)
                    eng.scalar_tensor_tensor(ee[:, :], ee[:, :], 0.2, ee[:, :], ALU.mult, ALU.max).then_inc(dv.sem, 1)
                    dv.wait(eng, s, 3)
                    eng.tensor_tensor(mm_[:, :], mm_[:, :], er_s, ALU.add).then_inc(dv.sem, 1)
                    dv.wait(eng, s, 5)
                    eng.scalar_tensor_tensor(mm_[:, :], mm_[:, :], 0.2, mm_[:, :], ALU.mult, ALU.max).then_inc(dv.sem, 1)
                    dv.wait(eng, s, 6)
                    eng.tensor_tensor(ee[:, :], ee[:, :], mm_[:, :], ALU.subtract).then_inc(s_d.sem, 1)

                def body(s, i, p, last):
                    s_we.wait(eng, s)
                    for k in range(1, NQ + 1):
                        tl = slice(4 * (k - 1), 4 * k)
                        s_sum.wait(eng, s, 2 * k - 4)
                        eng.tensor_tensor(sel[:, k % 2, :, :], bc(q.lastpos[:, bass.ds(s * SBT + 4 * (k - 1), 4)], 2, [P, 4, P]),
                                          bc(q.iota_f[:, :], 1, [P, 4, P]), ALU.is_equal)
                        f = gb[:, p, tl, 0:D].rearrange("p t (h c) -> p t h c", c=C)
                        eng.tensor_tensor(f, f, bc(gb[:, p, tl, D:FR], 3, [P, 4, H, C]), ALU.mult).then_inc(s_msg.sem, 1)
                        if k == PREP[0] and not last:
                            weights(s + 1)
                over(eng, body, lambda: weights(0))


def gat_output(nc, q, n):
    V, S, G, TE, SP, a, sb, pb = q.V, q.S, q.G, q.TE, q.SP, q.a, q.sb, q.pb
    chains = [Turns(q.sem(f"t_o{n}_{k}"), q.sem(f"t_o{n}_{k}_pool")) for k in range(K)]
    view = lambda y, i: y.rearrange("(i k p) d -> i p k d", k=NB, p=P)[i, :, :, :]
    with ExitStack() as c:
        bias = sb(c, "bias", [P, D])
        chains[0].dma(SP, lambda: SP.dma_start(bias[:, :], a[f"L1_gnn_b{n}"].partition_broadcast(P)))
        w = Features.weights(chains[0], q, c, 2) if n == 1 else None
        chains[0].end(nc)

        def chain(t):
            ixn = sb(c, "ixn", [P, NB], I32)
            rows = sb(c, "rows", [P, NB, GR])
            v, ex = sb(c, "v", [P, NB, D]), sb(c, "ex", [P, NB, D])
            ns, rd = sb(c, "ns", [P, NB]), sb(c, "rd", [P, NB, H])
            x1 = sb(c, "x1", [P, NB, D])
            if n == 1:
                ft = Features(t, q, c, w, [pb(c, "bank", [P, 4 * P]) for _ in range(NB)])

            def body(i):
                node_rows(t, q, q.sums1, 0, i, ixn, rows)
                some = q.some[:, bass.ds(i * NB, NB)]
                t.step(V, lambda: V.tensor_scalar(ns[:, :], some, -1.0, 1.0, ALU.mult, ALU.add))
                t.step(V, lambda: V.tensor_tensor(rd[:, :, :], rows[:, :, D:D + H], bc(ns[:, :], 2, [P, NB, H]), ALU.add))
                t.step(V, lambda: V.reciprocal(rd[:, :, :], rd[:, :, :]))
                t.step(V, lambda: V.tensor_tensor(rd[:, :, :], rd[:, :, :], bc(some, 2, [P, NB, H]), ALU.mult))
                t.step(V, *[lambda k=k: V.tensor_tensor(v[:, k, :].rearrange("p (h c) -> p h c", c=C),
                                                      rows[:, k, 0:D].rearrange("p (h c) -> p h c", c=C),
                                                      bc(rd[:, k, :], 2, [P, H, C]), ALU.mult) for k in range(NB)])
                t.step(V, lambda: V.tensor_tensor(v[:, :, :], v[:, :, :], bc(bias[:, :], 1, [P, NB, D]), ALU.add))
                t.step(V, lambda: V.tensor_scalar(ex[:, :, :], v[:, :, :], 0.0, None, ALU.min))
                t.step(S, lambda: S.activation(ex[:, :, :], ex[:, :, :], ACT.Exp))
                t.step(V, lambda: V.tensor_scalar(v[:, :, :], v[:, :, :], 0.0, -1.0, ALU.max, ALU.add))
                t.step(V, lambda: V.tensor_tensor(v[:, :, :], v[:, :, :], ex[:, :, :], ALU.add))
                if n == 1:
                    ft.emit(i, v, ACT.Copy)
                else:
                    t.dma(SP, lambda: SP.dma_start(x1[:, :, :], view(q.x1_d, i)))
                    t.step(V, lambda: V.tensor_tensor(v[:, :, :], v[:, :, :], x1[:, :, :], ALU.add))
                    t.dma(SP, lambda: SP.dma_start(view(q.out, i), v[:, :, :]))
            return body

        chains_loop(nc, chains, NG // K, [chain(t) for t in chains])
        for t in chains:
            t.end(nc)


def kernel(**inputs):
    import numpy as _np
    import concourse.bacc as _bacc
    from concourse import mybir as _mybir
    from concourse.bass_utils import run_bass_kernel_spmd as _run

    x = _np.asarray(inputs["x"])
    src, dst = _np.asarray(inputs["src"]), _np.asarray(inputs["dst"])
    pad = EP - E
    srcp = _np.concatenate([src, _np.zeros(pad + SPARE * 1024, src.dtype)])
    dstp = _np.concatenate([dst, _np.full(pad, N, dst.dtype)])
    rbf = _np.concatenate([_np.asarray(inputs["edge_attr_16"]), _np.zeros((pad + SPARE * 1024, R), _np.float32)])
    sh = _np.concatenate([_np.asarray(inputs["edge_attr_4"]), _np.zeros((pad + SPARE * 1024, 4), _np.float32)])
    arrays = {
        "x": _np.concatenate([x, _np.zeros((NP_ - N, D), x.dtype)]),
        "src_cols": srcp.reshape(EP // 1024 + SPARE, 8, P).transpose(0, 2, 1),
        "dst_cols": dstp.reshape(T, P).T,
        "dst_line": _np.concatenate([_np.full(1, -1, dst.dtype), dstp, _np.full(1, -2, dst.dtype)]),
        "rbf": rbf.reshape(EP // 1024 + SPARE, 2, HALF, R).transpose(0, 1, 3, 2).reshape(-1, 2 * R, HALF),
        "sh": sh.reshape(EP // 1024 + SPARE, 8, P, 4).transpose(0, 2, 1, 3).reshape(-1, P, 32),
    }
    for k, v in inputs.items():
        if k[:2] in ("L0", "L1"):
            arrays[k] = _np.asarray(v)
    arrays = {k: _np.ascontiguousarray(v) for k, v in arrays.items()}
    nc = _bacc.Bacc("TRN2", target_bir_lowering=False, num_devices=1)
    a = {k: nc.dram_tensor("in_" + k, v.shape, _mybir.dt.from_np(v.dtype), kind="ExternalInput").ap() for k, v in arrays.items()}
    out = nc.dram_tensor("out", (NP_, D), F32, kind="ExternalOutput").ap()
    program(nc, a, out)
    r = _run(nc, [{"in_" + k: v for k, v in arrays.items()}], core_ids=[0])
    return r.results[0]["out"][:N]
```

```python
from contextlib import ExitStack, contextmanager

import numpy as np
import concourse.bass as bass
from concourse import mybir

F32, I32, BF16 = mybir.dt.float32, mybir.dt.int32, mybir.dt.bfloat16
ALU, ACT = mybir.AluOpType, mybir.ActivationFunctionType
P = 128
N, E, C, H, HID, R = 12500, 200000, 64, 4, 64, 16
D = 4 * C
NT = 104
NP_ = NT * P
NB = 2
NG = NT // NB
K = 4
W = NB * P
HALF = 4 * P
FULL = N // W
LAST = N - FULL * W
SBT = 32
SB = -(-E // (SBT * P))
T = SB * SBT
EP = T * P
TG = 14
TP = T // TG
CH = EP // P
GR = D + 2 * H
SPARE = 4
BIG = 1.0e30
SKIP = float(1 << 22)
EPS = 1e-5
assert NG % K == 0 and FULL % K == 0 and K * NB == 8 and T == TG * TP and EP == P * CH and T % 8 == 0


class Signal:

    def __init__(self, sem, per=1, inc=1, ahead=0):
        self.sem, self.per, self.inc, self.base = sem, per, inc, ahead * per * inc

    def at(self, i, k=None, back=0):
        k = (self.per if k is None else k) - back * self.per
        return i * (self.per * self.inc) + (self.base + k * self.inc)

    def wait(self, eng, i, k=None, back=0):
        eng.wait_ge(self.sem, self.at(i, k, back))

    def prime(self, eng):
        eng.sem_inc(self.sem, self.base)


class Step:

    def __init__(self, lay, args, adds, length):
        self.lay, self.args, self.adds, self.length = lay, args, adds, length


class Turns:

    def __init__(self, sem, pool_sem):
        self.sems = (sem, pool_sem)
        self.base, self.n, self.per, self.i = [0, 0], [0, 0], [0, 0], 0
        self.last = (0,)
        self.queue = None

    def value(self, s):
        return self.i * self.per[s] + (self.base[s] + self.n[s]) if self.per[s] else self.base[s] + self.n[s]

    def wait(self, eng):
        for s in self.last:
            if self.base[s] + self.n[s] + self.per[s]:
                eng.wait_ge(self.sems[s], self.value(s))
                if self.per[s]:
                    eng.nop(nofuse=True)

    def step(self, eng, *instructions):
        if self.queue is not None:
            self.queue.append(Step(self._step, (eng, instructions), (1, 0), 0.2 + 0.4 * len(instructions)))
        else:
            self._step(eng, instructions)

    def dma(self, eng, *instructions):
        if self.queue is not None:
            self.queue.append(Step(self._dma, (eng, instructions), (16 * len(instructions), 0), 2.3))
        else:
            self._dma(eng, instructions)

    def pool_dma(self, pool, instructions, eng=None, beside=()):
        if self.queue is not None:
            self.queue.append(Step(self._pool_dma, (pool, instructions, eng, beside),
                                   (16 * len(beside), 16 * len(instructions)), 2.0 + len(instructions)))
        else:
            self._pool_dma(pool, instructions, eng, beside)

    def _step(self, eng, instructions):
        self.wait(eng)
        for make in instructions:
            ins = make()
        ins.then_inc(self.sems[0], 1)
        self.n[0] += 1
        self.last = (0,)

    def _dma(self, eng, instructions):
        self.wait(eng)
        for make in instructions:
            make().then_inc(self.sems[0], 16)
        self.n[0] += 16 * len(instructions)
        self.last = (0,)

    def _pool_dma(self, pool, instructions, eng, beside):
        self.wait(pool)
        if beside:
            self.wait(eng)
        for make in instructions:
            make().then_inc(self.sems[1], 16)
        for make in beside:
            make().then_inc(self.sems[0], 16)
        self.n[1] += 16 * len(instructions)
        self.n[0] += 16 * len(beside)
        self.last = (0, 1) if beside else (1,)

    def begin(self, per, i):
        self.base = [x + y for x, y in zip(self.base, self.n)]
        self.n, self.last = [0, 0], tuple(s for s in (0, 1) if self.base[s])
        self.i, self.per = i, per

    def close(self, count):
        assert self.n == self.per, (self.n, self.per)
        self.base = [x + count * y for x, y in zip(self.base, self.per)]
        self.n, self.per, self.i, self.last = [0, 0], [0, 0], 0, (0, 1)

    def end(self, nc):
        for eng in (nc.sync, nc.scalar, nc.vector, nc.gpsimd, nc.tensor):
            for s in (0, 1):
                if self.base[s] + self.n[s]:
                    eng.wait_ge(self.sems[s], self.value(s))
        nc.all_engine_barrier()


def queued(t, body, i):
    t.queue = []
    body(i)
    steps, t.queue = t.queue, None
    return steps


def side_by_side(queues):
    order = []
    for k, queue in enumerate(queues):
        at = 0.0
        for n, step in enumerate(queue):
            order.append((at, k, n))
            at += step.length
    for _, k, n in sorted(order):
        queues[k][n].lay(*queues[k][n].args)


def chains_loop(nc, chains, count, bodies):
    K = len(chains)

    def parts(k, i):
        steps = queued(chains[k], bodies[k], i * K + k)
        ahead, cut = 0.0, 0
        while ahead < sum(x.length for x in steps) * k / K:
            ahead, cut = ahead + steps[cut].length, cut + 1
        return steps[:cut], steps[cut:]

    for t in chains:
        if not t.base[0] + t.n[0]:
            nc.sync.sem_inc(t.sems[0], 1)
            t.n[0] += 1
    side_by_side([parts(k, 0)[0] for k in range(K)])
    with nc.Fori(0, count - 1) as i:
        turn = [parts(k, i)[1] + parts(k, i + 1)[0] for k in range(K)]
        for t, steps in zip(chains, turn):
            t.begin([sum(step.adds[s] for step in steps) for s in (0, 1)], i)
        side_by_side(turn)
        for t in chains:
            t.close(count - 1)
    side_by_side([parts(k, count - 1)[1] for k in range(K)])


def bc(ap, dim, shape):
    return ap.unsqueeze(dim).to_broadcast(shape)


class Shared:
    pass


def program(nc, a, out):
    q = Shared()
    q.a, q.out = a, out
    q.top = top = ExitStack()
    with top:
        seen = {}

        def unique(name):
            seen[name] = seen.get(name, 0) + 1
            return f"{name}_{seen[name]}"

        def sb(ctx, name, shape, dt=F32):
            return ctx.enter_context(nc.sbuf_tensor(unique(name), shape, dt))

        def pb(ctx, name, shape, dt=F32):
            return ctx.enter_context(nc.psum_tensor(unique(name), shape, dt))

        def sem(name):
            return top.enter_context(nc.semaphore(name))

        def dram(name, shape, dt=F32):
            return nc.dram_tensor(name, shape, dt, kind="Internal").ap()

        q.V, q.S, q.G, q.TE, q.SP = nc.vector, nc.scalar, nc.gpsimd, nc.tensor, nc.sync
        q.sb, q.pb, q.sem = sb, pb, sem

        q.table0 = dram("table0", (NP_, D))
        q.table1 = dram("table1", (NP_, D + H))
        q.hT_d = dram("hT_d", (C, 4, NP_))
        q.oT_d = dram("oT_d", (C, 4, NP_))
        q.x1_d = dram("x1_d", (NP_, D))
        q.er_d = dram("er_d", (NP_, H))
        q.sums0_x = dram("sums0", (8 * P + EP, D))
        q.sums0 = q.sums0_x[8 * P:, :]
        q.spare = 8 * P * D
        q.sums1 = dram("sums1", (EP, GR))
        q.er_start = dram("er_start", (EP, H))
        q.behind_d = dram("behind", (1 + P * P,))
        q.er_edge = dram("er_edge", (H, EP))

        q.iota_f = sb(top, "iota_f", [P, P])
        q.ident = sb(top, "ident", [P, P])
        q.upper = sb(top, "upper", [P, P])
        q.lastpos = sb(top, "lastpos", [P, T])
        q.whole = sb(top, "whole", [P, T])
        q.start_f = sb(top, "start_f", [P, SB, P], BF16)
        q.start_b = sb(top, "start_b", [P, SB, P], BF16)
        q.samep = sb(top, "samep", [P, CH])
        q.chunk_node = sb(top, "chunk_node", [P, 1], I32)
        q.head_idx = sb(top, "head_idx", [TP, TG], I32)
        q.fix_idx = sb(top, "fix_idx", [TP, TG], I32)
        q.node_id = sb(top, "node_id", [P, P], I32)
        q.cut_idx = sb(top, "cut_idx", [P, P], I32)
        q.cut_f = sb(top, "cut_f", [P, P])
        q.upto = sb(top, "upto", [P, P])
        q.row_idx = sb(top, "row_idx", [P, P], I32)
        q.first_idx = sb(top, "first_idx", [P, P], I32)
        q.some = sb(top, "some", [P, P])
        q.eps_c = sb(top, "eps_c", [P, 1])
        q.stat = sb(top, "stat", [C, 4])

        structure(nc, q)
        layer0_nodes(nc, q)
        node_edges(nc, q)
        layer0_edges(nc, q)
        stitch(nc, q, q.sums0, D, "s0")
        layer0_update(nc, q)
        layer0_norm_and_gat_nodes(nc, q)
        for n in (1, 2):
            spread_er(nc, q, n)
            gat_edges(nc, q, n)
            stitch(nc, q, q.sums1, GR, f"s{n}")
            gat_output(nc, q, n)


def structure(nc, q):
    V, S, G, TE, SP, a, sb, pb = q.V, q.S, q.G, q.TE, q.SP, q.a, q.sb, q.pb
    t = Turns(q.sem("t_struct"), q.sem("t_struct_pool"))
    line = a["dst_line"]
    with ExitStack() as c:
        ii = sb(c, "ii", [P, P], I32)
        t.step(G, lambda: G.iota(ii[:, :], pattern=[[1, P]], base=0, channel_multiplier=0))
        t.step(V, lambda: V.tensor_copy(q.iota_f[:, :], ii[:, :]))
        t.step(G, lambda: G.memset(q.ident[:, :], 0.0))
        t.step(G, lambda: G.affine_select(out=q.ident[:, :], in_=q.ident[:, :], compare_op=ALU.not_equal,
                                          fill=1.0, base=0, pattern=[[-1, P]], channel_multiplier=1))
        t.step(G, lambda: G.memset(q.upper[:, :], 1.0))
        t.step(G, lambda: G.affine_select(out=q.upper[:, :], in_=q.upper[:, :], compare_op=ALU.is_gt,
                                          fill=0.0, base=0, pattern=[[1, P]], channel_multiplier=-1))
        t.step(V, lambda: V.memset(q.eps_c[:, :], EPS))

    with ExitStack() as c:
        d, dp, dn = (sb(c, n, [TP, TG, P], I32) for n in ("d", "dp", "dn"))
        same, pos, lp = (sb(c, n, [TP, TG, P]) for n in ("same", "pos", "lp"))
        wh, link, fi = (sb(c, n, [TP, TG]) for n in ("wh", "link", "fi"))
        fi_i = sb(c, "fi_i", [TP, TG], I32)
        ps = pb(c, "ps_s", [P, 4, P])
        view = lambda o: line[o:o + EP].rearrange("(g p e) -> p g e", p=TP, e=P)
        t.dma(SP, lambda: SP.dma_start(dp[:, :, :], view(0)), lambda: SP.dma_start(d[:, :, :], view(1)),
              lambda: SP.dma_start(dn[:, :, :], view(2)))
        t.step(V, lambda: V.tensor_tensor(same[:, :, :], d[:, :, :], dn[:, :, :], ALU.is_equal))
        t.step(V, lambda: V.memset(same[:, :, P - 1:P], 0.0))
        t.step(V, lambda: V.tensor_scalar(pos[:, :, :], same[:, :, :], -1.0, 1.0, ALU.mult, ALU.add))
        t.step(V, lambda: V.tensor_tensor(pos[:, :, :], pos[:, :, :], bc(q.iota_f[:TP, :], 1, [TP, TG, P]), ALU.mult))
        flat = lambda x: x[:, :, :].rearrange("p g e -> p (g e)")[:, ::-1]
        t.step(V, lambda: V.tensor_tensor_scan(flat(lp), flat(same), flat(pos), 0.0, ALU.mult, ALU.add))
        t.step(V, lambda: V.tensor_tensor(wh[:, :].unsqueeze(2), dp[:, :, 0:1], d[:, :, P - 1:P], ALU.is_equal))
        t.step(V, lambda: V.tensor_tensor(link[:, :].unsqueeze(2), dp[:, :, 0:1], d[:, :, 0:1], ALU.is_equal))
        t.step(G, lambda: G.iota(fi_i[:, :], pattern=[[TP * P, TG]], base=0, channel_multiplier=P))
        t.step(V, lambda: V.tensor_copy(fi[:, :], fi_i[:, :]))
        t.step(V, lambda: V.tensor_tensor(fi[:, :].unsqueeze(2), fi[:, :].unsqueeze(2), lp[:, :, 0:1], ALU.add))
        t.step(V, lambda: V.tensor_copy(q.head_idx[:, :], fi[:, :]))
        t.step(V, lambda: V.tensor_scalar(link[:, :], link[:, :], -SKIP, SKIP, ALU.mult, ALU.add))
        t.step(V, lambda: V.tensor_tensor(fi[:, :], fi[:, :], link[:, :], ALU.add))
        t.step(V, lambda: V.tensor_copy(q.fix_idx[:, :], fi[:, :]))
        t.step(V, lambda: V.tensor_copy(same[:, :, :], bc(wh[:, :], 2, [TP, TG, P])))
        hi_i, lo_i = (sb(c, n, [TP, TG], I32) for n in ("hi_i", "lo_i"))
        hi, lo = (sb(c, n, [TP, TG]) for n in ("hi", "lo"))
        oh = sb(c, "oh", [TP, 2, TG, P], BF16)
        cnt, cum, zero = (sb(c, n, [P, P]) for n in ("cnt", "cum", "zero"))
        hist, pre = pb(c, "hist", [P, P]), pb(c, "pre", [P, 1])
        ends = d[:, :, P - 1:P]
        t.step(V, lambda: V.tensor_scalar(hi_i[:, :].unsqueeze(2), ends, 7, None, ALU.logical_shift_right),
               lambda: V.tensor_scalar(lo_i[:, :].unsqueeze(2), ends, 127, None, ALU.bitwise_and))
        t.step(V, lambda: V.tensor_copy(hi[:, :], hi_i[:, :]), lambda: V.tensor_copy(lo[:, :], lo_i[:, :]),
               lambda: V.memset(zero[:, :], 0.0))
        t.step(V, *[lambda n=n, v=v: V.tensor_tensor(oh[:, n, :, :], bc(v[:, :], 2, [TP, TG, P]),
                                                     bc(q.iota_f[:TP, :], 1, [TP, TG, P]), ALU.is_equal)
                    for n, v in enumerate((hi, lo))])
        t.step(TE, *[lambda g=g: TE.matmul(hist[:, :], oh[:, 0, g, :], oh[:, 1, g, :], start=g == 0, stop=g == TG - 1)
                     for g in range(TG)])
        t.step(V, lambda: V.tensor_copy(cnt[:, :], hist[:, :]))
        t.step(V, lambda: V.tensor_tensor_scan(cum[:, :], cnt[:, :], zero[:, :], 0.0, ALU.add, ALU.add))
        t.step(TE, lambda: TE.matmul(pre[:, :], q.upper[:, :], cum[:, P - 1:P], start=True, stop=True))
        t.step(V, lambda: V.tensor_scalar(cum[:, :], cum[:, :], pre[:, 0:1], None, ALU.add))
        t.step(V, lambda: V.tensor_scalar(cum[:, :], cum[:, :], float(T - 1), None, ALU.min))
        t.step(TE, lambda: TE.transpose(hist[:, :], cum[:, :], q.ident[:, :]))
        t.step(V, lambda: V.tensor_copy(q.cut_f[:, :], hist[:, :]), lambda: V.tensor_copy(q.cut_idx[:, :], hist[:, :]))
        t.step(G, lambda: G.iota(q.node_id[:, :], pattern=[[P, P]], base=0, channel_multiplier=1))
        t.step(V, lambda: V.memset(q.upto[:, :], 0.0))
        for src, dst in ((lp, q.lastpos), (same, q.whole)):
            for g0 in range(0, TG, 4):
                gs = range(g0, min(g0 + 4, TG))
                t.step(TE, *[lambda g=g, src=src: TE.transpose(ps[:, g % 4, 0:TP], src[:, g, :], q.ident[:TP, :TP])
                             for g in gs])
                t.step(V, lambda dst=dst, g0=g0, gs=gs: V.tensor_copy(
                    dst[:, g0 * TP:(g0 + len(gs)) * TP].rearrange("p (g t) -> p g t", t=TP), ps[:, 0:len(gs), 0:TP]))

    with ExitStack() as c:
        m0, m1 = (sb(c, n, [P, SB, P], I32) for n in ("m0", "m1"))
        eq = sb(c, "eq", [P, SB, P], BF16)
        view = lambda o: line[o:o + EP].rearrange("(s t e) -> t s e", t=SBT, e=P)
        load = lambda m, o: [lambda h=h: SP.dma_start(m[h * SBT:(h + 1) * SBT, :, :], view(o)) for h in range(H)]
        t.dma(SP, *load(m0, 1))
        for o, mask in ((0, q.start_f), (2, q.start_b)):
            t.dma(SP, *load(m1, o))
            t.step(V, lambda mask=mask: V.tensor_tensor(eq[:, :, :], m0[:, :, :], m1[:, :, :], ALU.is_equal))
            t.step(V, lambda mask=mask: V.tensor_scalar(mask[:, :, :], eq[:, :, ::1 - o], BIG, -BIG, ALU.mult, ALU.add))

    with ExitStack() as c:
        c0, c1 = (sb(c, n, [P, CH], I32) for n in ("c0", "c1"))
        t.dma(SP, lambda: SP.dma_start(c0[:, :], line[1:1 + EP].rearrange("(p e) -> p e", p=P)),
              lambda: SP.dma_start(c1[:, :], line[0:EP].rearrange("(p e) -> p e", p=P)))
        t.step(V, lambda: V.tensor_tensor(q.samep[:, :], c0[:, :], c1[:, :], ALU.is_equal))
        t.step(V, lambda: V.tensor_copy(q.chunk_node[:, :], c0[:, 0:1]))
        z = sb(c, "z", [P, CH * H])
        t.step(V, lambda: V.memset(z[:, :], 0.0))
        t.dma(SP, lambda: SP.dma_start(q.er_start.rearrange("(p e) h -> p (e h)", p=P), z[:, :]))
    t.end(nc)


def norm_rows(t, V, S, q, x, z, st, mv, rs):
    t.step(V, *[lambda k=k: V.bn_stats(st[:, k, :], x[:, k, :]) for k in range(NB)])
    t.step(V, *[lambda k=k: V.bn_aggr(mv[:, k, :], st[:, k, :]) for k in range(NB)])
    t.step(S, lambda: S.activation(rs[:, :].unsqueeze(2), mv[:, :, 1:2], ACT.Sqrt, bias=q.eps_c[:, 0:1]))
    t.step(V, lambda: V.reciprocal(rs[:, :], rs[:, :]))
    t.step(V, *[lambda k=k: V.tensor_scalar(z[:, k, :], x[:, k, :], mv[:, k, 0:1], rs[:, k:k + 1],
                                            ALU.subtract, ALU.mult) for k in range(NB)])


def layer0_nodes(nc, q):
    V, S, G, TE, SP, a, sb, pb = q.V, q.S, q.G, q.TE, q.SP, q.a, q.sb, q.pb
    chains = [Turns(q.sem(f"t_nodes{k}"), q.sem(f"t_nodes{k}_pool")) for k in range(K)]
    with ExitStack() as c:
        wup = sb(c, "wup", [C, 2, C])
        xin = a["x"].rearrange("(i k p) d -> i p k d", k=NB, p=P)
        table = q.table0.rearrange("(i k p) d -> i p k d", k=NB, p=P)

        def chain(t):
            x, z = (sb(c, n, [P, NB, D]) for n in ("x", "z"))
            st, mv, rs = sb(c, "st", [P, NB, 6]), sb(c, "mv", [P, NB, 2]), sb(c, "rs", [P, NB])
            ixc, ends = sb(c, "ixc", [P, NB], I32), sb(c, "ends", [P, NB, P], I32)
            le = sb(c, "le", [P, NB, P])
            hT = sb(c, "hT", [C, 4, W])
            up = sb(c, "up", [P, NB, D])
            banks = [pb(c, "bank", [P, 4 * P]) for _ in range(NB)]
            pT = [b[:C, :].rearrange("c (a n) -> c a n", a=4) for b in banks]
            pU = [b[:, 0:D] for b in banks]

            def body(i):
                here = bass.ds(i * NB, NB)
                t.step(V, lambda: V.tensor_copy(ixc[:, :], q.cut_idx[:, here]))
                t.pool_dma(G, [lambda k=k: G.indirect_dma_start(out=ends[:, k, :], out_offset=None, in_=a["dst_rows"],
                               in_offset=bass.IndirectOffsetOnAxis(ap=ixc[:, k:k + 1], axis=0)) for k in range(NB)],
                           SP, [lambda: SP.dma_start(x[:, :, :], xin[i, :, :, :])])
                t.step(V, lambda: V.tensor_tensor(le[:, :, :], ends[:, :, :], bc(q.node_id[:, here], 2, [P, NB, P]), ALU.is_le))
                t.step(V, lambda: V.tensor_reduce(q.upto[:, here], le[:, :, :], mybir.AxisListType.X, ALU.add))
                norm_rows(t, V, S, q, x, z, st, mv, rs)
                t.step(TE, *[lambda k=k, pl=pl: TE.transpose(pT[k][:, pl, :], plane(z, k, pl), q.ident[:, :])
                             for k in range(NB) for pl in range(4)])
                t.step(S, *[lambda k=k: S.activation(hT[:, :, k * P:(k + 1) * P], pT[k], ACT.Relu)
                            for k in range(NB)])
                t.step(TE, *[lambda k=k, pl=pl: TE.matmul(pU[k][:, pl * C:(pl + 1) * C], hT[:, pl, k * P:(k + 1) * P],
                                                          wup[:, min(pl, 1), :], start=True, stop=True)
                             for k in range(NB) for pl in range(4)])
                t.step(S, *[lambda k=k: S.activation(up[:, k, :], pU[k], ACT.Copy) for k in range(NB)])
                t.dma(SP, lambda: SP.dma_start(table[i, :, :, :], up[:, :, :]),
                      lambda: SP.dma_start(q.hT_d[:, :, bass.ds(i * W, W)], hT[:, :, :]))
            return body

        bodies = [chain(t) for t in chains]
        chains[0].dma(SP, lambda: SP.dma_start(wup[:, 0, :], a["L0_gnn_W_up0"]),
                      lambda: SP.dma_start(wup[:, 1, :], a["L0_gnn_W_up1"]))
        chains[0].end(nc)
        chains_loop(nc, chains, NG // K, bodies)
        for t in chains:
            t.end(nc)


def node_edges(nc, q):
    V, TE, SP, sb, pb = q.V, q.TE, q.SP, q.sb, q.pb
    t = Turns(q.sem("t_ends"), q.sem("t_ends_pool"))
    with ExitStack() as c:
        cum, cut, cnt, beg, non = (sb(c, n, [P, P]) for n in ("cum_e", "cut_e", "cnt_e", "beg_e", "non_e"))
        tr = pb(c, "tr", [P, 3, P])
        line = lambda o: q.behind_d[o:o + P * P].rearrange("(t e) -> t e", e=P)
        t.step(V, lambda: V.scalar_tensor_tensor(cut[:, :], q.cut_f[:, :], float(P), q.upto[:, :], ALU.mult, ALU.add))
        t.step(TE, lambda: TE.transpose(tr[:, 0, :], cut[:, :], q.ident[:, :]))
        t.step(V, lambda: V.tensor_copy(cum[:, :], tr[:, 0, :]), lambda: V.memset(non[:, :], 0.0))
        t.dma(SP, lambda: SP.dma_start(line(1), cum[:, :]), lambda: SP.dma_start(q.behind_d[0:1], non[0, 0:1]))
        t.dma(SP, lambda: SP.dma_start(beg[:, :], line(0)))
        t.step(V, lambda: V.tensor_tensor(cnt[:, :], cum[:, :], beg[:, :], ALU.subtract))
        t.step(V, lambda: V.tensor_scalar(cum[:, :], cum[:, :], -1.0, 0.0, ALU.add, ALU.max),
               lambda: V.tensor_scalar(non[:, :], cnt[:, :], 0.0, SKIP, ALU.is_equal, ALU.mult))
        t.step(V, lambda: V.tensor_tensor(beg[:, :], beg[:, :], non[:, :], ALU.add))
        t.step(V, lambda: V.tensor_scalar(non[:, :], cnt[:, :], 0.0, None, ALU.is_gt))
        t.step(TE, *[lambda k=k, m=m: TE.transpose(tr[:, k, :], m[:, :], q.ident[:, :])
                     for k, m in enumerate((cum, beg, non))])
        t.step(V, lambda: V.tensor_copy(q.row_idx[:, :], tr[:, 0, :]),
               lambda: V.tensor_copy(q.first_idx[:, :], tr[:, 1, :]),
               lambda: V.tensor_copy(q.some[:, :], tr[:, 2, :]))
        t.end(nc)


def plane(z, k, pl):
    return z[:, k, 0:C] if pl == 0 else z[:, k, C + pl - 1:D:3]


def layer0_edges(nc, q):
    a, sb, pb = q.a, q.sb, q.pb
    B = 4
    with ExitStack() as c:
        m1 = sb(c, "m1", [2 * R, 2 * HID])
        m23 = sb(c, "m23", [2 * HID, 2, 2 * HID])
        m4 = sb(c, "m4", [2 * HID, D])
        at = sb(c, "at", [2 * R, B, HALF])
        sh = sb(c, "sh", [P, B, 8, 4])
        ix = sb(c, "ix", [P, B, 8], I32)
        gb = sb(c, "gb", [P, B, 8, 4, C])
        r = sb(c, "r", [P, 2, HALF])
        r3 = sb(c, "r3", [P, 2, HALF])
        t02 = sb(c, "t02", [P, 2, 4, 2, C])
        sel = sb(c, "sel", [P, 2, 4, P])
        msg = sb(c, "msg", [P, 2, 4, 4, C])
        dots = sb(c, "dots", [P, 4, 4, 3, C])
        tmp = sb(c, "tmp", [P, 4, 3, C])
        qd = sb(c, "qd", [P, 4, C])
        p1 = sb(c, "p1", [P, 4, C])
        ost = sb(c, "ost", [P, 2, 4, D])
        pm = [pb(c, f"pm{k}", [P, HALF]) for k in range(2)]
        pt = [pb(c, f"pt{k}", [P, 4, D]) for k in range(2)]
        po = pb(c, "po", [P, 4, D])

        t = Turns(q.sem("t_w0"), q.sem("t_w0_pool"))
        V, SP, S = q.V, q.SP, q.S
        t.step(V, lambda: V.memset(m1[:, :], 0.0), lambda: V.memset(m23[:, :, :], 0.0))
        t.dma(SP, *[lambda g=g: SP.dma_start(m1[g * R:(g + 1) * R, g * HID:(g + 1) * HID], a["L0_gnn_M1"]) for g in range(2)],
              *[lambda g=g, n=n: SP.dma_start(m23[g * HID:(g + 1) * HID, n, g * HID:(g + 1) * HID], a[f"L0_gnn_M{n + 2}"])
                for g in range(2) for n in range(2)],
              *[lambda g=g: SP.dma_start(m4[g * HID:(g + 1) * HID, :], a["L0_gnn_M4"]) for g in range(2)])
        t.step(V, lambda: V.tensor_scalar(m4[:, 3 * C:D], m4[:, 3 * C:D], float(np.float32(1.0) / np.sqrt(np.float32(3.0))), None, ALU.mult))
        t.end(nc)

        s_at = [Signal(q.sem(f"at{g}"), inc=16) for g in range(B)]
        s_at[0].base = 16
        s_sh = [Signal(q.sem(f"sh{g}"), inc=16) for g in range(B)]
        s_ix = [Signal(q.sem(f"ix{g}"), inc=16) for g in range(B)]
        s_g = [Signal(q.sem(f"g{g}"), per=8, inc=16) for g in range(B)]
        s_dot = Signal(q.sem("dot"), per=2 * B)
        s_mm = Signal(q.sem("mm"), per=3 * B)
        s_si = Signal(q.sem("si"), per=3 * B)
        s_mm.base = s_si.base = 3
        s_t = Signal(q.sem("t"), per=2 * B)
        s_ts = Signal(q.sem("ts"), per=2 * B)
        s_msg = Signal(q.sem("msg"), per=2 * B, ahead=1)
        s_sum = Signal(q.sem("sum"), per=2 * B, ahead=1)
        s_ev = Signal(q.sem("ev"), per=2 * B, ahead=1)
        s_st = [Signal(q.sem(f"st{k}"), per=B, inc=16, ahead=1) for k in range(2)]
        dv = Signal(q.sem("dv"), per=2 * B * 7)
        s1_of = lambda g, ts: bc(sh[:, g, ts, 1:4], 3, [P, 4, 3, C])
        out_v = q.sums0_x.rearrange("(b j p) c -> b p j c", j=4, p=P)

        with nc.Block() as block:
            @block.sync
            def _(eng):
                for s in s_st:
                    s.prime(eng)

                def load(i, g):
                    eng.dma_start(ix[:, g, :], a["src_cols"][i * B + g, :, :]).then_inc(s_ix[g].sem, 16)
                    eng.dma_start(at[:, g, :], a["rbf"][i * B + g, :, :]).then_inc(s_at[g].sem, 16)
                    eng.dma_start(sh[:, g, :, :].rearrange("p t k -> p (t k)"), a["sh"][i * B + g, :, :]).then_inc(s_sh[g].sem, 16)

                def store(i, k):
                    s_ev.wait(eng, i, k)
                    eng.nop(nofuse=True)
                    eng.dma_start(out_v[i * (2 * B) + (k - 1), :, :, :], ost[:, k % 2, :, :]).then_inc(s_st[k % 2].sem, 16)

                for g in range(B):
                    load(0, g)
                with eng.Fori(0, SB) as i:
                    for g in range(B):
                        store(i, 2 * g + 1)
                        store(i, 2 * g + 2)
                        s_msg.wait(eng, i, 2 * g + 2)
                        eng.nop(nofuse=True)
                        load(i + 1, g)
                for k in (1, 2):
                    store(SB - 1, 2 * B + k)
                    s_st[k % 2].wait(eng, SB - 1, B + 1)
                for g in range(B):
                    for s in (s_ix[g], s_sh[g]):
                        s.wait(eng, SB)
                    eng.wait_ge(s_at[g].sem, 16 * (SB + 1))

            @block.gpsimd
            def _(eng):
                def gathers(i, g):
                    s_ix[g].wait(eng, i)
                    s_msg.wait(eng, i, 2 * g + 2, back=1)
                    eng.nop(nofuse=True)
                    for j in range(8):
                        eng.indirect_dma_start(out=gb[:, g, j, :, :].rearrange("p a c -> p (a c)"), out_offset=None,
                                               in_=q.table0[:, :],
                                               in_offset=bass.IndirectOffsetOnAxis(ap=ix[:, g, j:j + 1], axis=0)).then_inc(s_g[g].sem, 16)

                def products(i, g):
                    s_g[g].wait(eng, i)
                    s_sh[g].wait(eng, i)
                    for k in (2 * g + 1, 2 * g + 2):
                        ts = slice(4 * ((k - 1) % 2), 4 * ((k - 1) % 2) + 4)
                        s_msg.wait(eng, i, k - 4)
                        eng.nop(nofuse=True)
                        eng.tensor_tensor(dots[:, k % 4, :, :, :], gb[:, g, ts, 1:4, :], s1_of(g, ts), ALU.mult).then_inc(s_dot.sem, 1)

                with eng.Fori(0, SB) as i:
                    gathers(i, 0)
                    for g in range(1, B):
                        gathers(i, g)
                        products(i, g - 1)
                    products(i, B - 1)

            @block.tensor
            def _(eng):
                s_sum.prime(eng)

                def mlp(n, g, parity):
                    lhsT, rhs = ((m1[:, :], at[:, g, :]), (m23[:, 0, :], r[:, 0, :]), (m23[:, 1, :], r[:, 1, :]))[n]
                    eng.matmul(pm[parity][:, :], lhsT, rhs, start=True, stop=True).then_inc(s_mm.sem, 1)

                def paths(g, half):
                    for j in range(4):
                        h0 = HID * half
                        ins = eng.matmul(pt[half][:, j, :], r3[h0:h0 + HID, g % 2, j * P:(j + 1) * P],
                                         m4[h0:h0 + HID, :], start=True, stop=True)
                    ins.then_inc(s_t.sem, 1)

                def sums(i, k):
                    s_msg.wait(eng, i, k - 2)
                    s_ev.wait(eng, i, k - 1)
                    for j in range(4):
                        ins = eng.matmul(po[:, j, :], sel[:, k % 2, j, :], msg[:, k % 2, j, :, :].rearrange("p a c -> p (a c)"),
                                         start=True, stop=True)
                    ins.then_inc(s_sum.sem, 1)

                eng.wait_ge(s_at[0].sem, 16)
                for n in range(3):
                    if n:
                        eng.wait_ge(s_si.sem, n)
                    mlp(n, 0, n % 2 == 0)
                with eng.Fori(0, SB) as i:
                    for g in range(B):
                        x = 3 * g
                        s_at[(g + 1) % B].wait(eng, i)
                        s_si.wait(eng, i, x)
                        mlp(0, (g + 1) % B, x % 2)
                        s_msg.wait(eng, i, 2 * g - 1)
                        paths(g, 0)
                        s_si.wait(eng, i, x + 1)
                        mlp(1, (g + 1) % B, (x + 1) % 2)
                        sums(i, 2 * g + 1)
                        s_msg.wait(eng, i, 2 * g)
                        paths(g, 1)
                        s_si.wait(eng, i, x + 2)
                        mlp(2, (g + 1) % B, x % 2)
                        sums(i, 2 * g + 2)
                for k in (1, 2):
                    sums(SB - 1, 2 * B + k)

            @block.scalar
            def _(eng):
                s_ev.prime(eng)

                def silu(n, g, parity):
                    dst = (r[:, 0, :], r[:, 1, :], r3[:, g % 2, :])[n]
                    eng.activation(dst, pm[parity][:, :], ACT.Silu).then_inc(s_si.sem, 1)

                def scaled(i, g, half):
                    k = 2 * g + 1 + half
                    s_t.wait(eng, i, k)
                    s_msg.wait(eng, i, k - 2)
                    for j in range(4):
                        ins = eng.activation(t02[:, half, j, :, :],
                                             pt[half][:, j, :].rearrange("p (a c) -> p a c", c=C)[:, 0:3:2, :],
                                             ACT.Copy, scale=sh[:, g, 4 * half + j, 0:1])
                    ins.then_inc(s_ts.sem, 1)

                def evac(i, k):
                    s_sum.wait(eng, i, k)
                    s_st[k % 2].wait(eng, i, (k + 1) // 2 - 1)
                    for j in (0, 2):
                        ins = eng.activation(ost[:, k % 2, j:j + 2, :], po[:, j:j + 2, :], ACT.Copy)
                    ins.then_inc(s_ev.sem, 1)

                for n in range(3):
                    eng.wait_ge(s_mm.sem, n + 1)
                    silu(n, 0, n % 2 == 0)
                with eng.Fori(0, SB) as i:
                    for g in range(B):
                        x = 3 * g
                        s_mm.wait(eng, i, x + 1)
                        silu(0, g + 1, x % 2)
                        s_sh[g].wait(eng, i)
                        scaled(i, g, 0)
                        s_mm.wait(eng, i, x + 2)
                        silu(1, g + 1, (x + 1) % 2)
                        evac(i, 2 * g + 1)
                        scaled(i, g, 1)
                        s_mm.wait(eng, i, x + 3)
                        silu(2, g + 1, x % 2)
                        evac(i, 2 * g + 2)
                for k in (1, 2):
                    evac(SB - 1, 2 * B + k)

            @block.vector
            def _(eng):
                eng.memset(sel[:, :, :, :], 0.0)
                eng.memset(msg[:, :, :, :, :], 0.0).then_inc(s_msg.sem, s_msg.base)
                with eng.Fori(0, SB) as i:
                    n = 0

                    def own(ins):
                        nonlocal n
                        n += 1
                        ins.then_inc(dv.sem, 1)
                        return n

                    for k in range(1, 2 * B + 1):
                        g, half, b = (k - 1) // 2, (k - 1) % 2, k % 2
                        ts = slice(4 * half, 4 * half + 4)
                        x0 = gb[:, g, ts, 0, :]
                        x1 = gb[:, g, ts, 1:4, :]
                        s1 = s1_of(g, ts)
                        w = pt[half][:, :, :].rearrange("p t (a c) -> p t a c", c=C)
                        s_sum.wait(eng, i, k)
                        eng.tensor_tensor(sel[:, b, :, :], bc(q.lastpos[:, bass.ds(i * SBT + 4 * (k - 1), 4)], 2, [P, 4, P]),
                                          bc(q.iota_f[:, :], 1, [P, 4, P]), ALU.is_equal)
                        if half == 0:
                            s_g[g].wait(eng, i)
                            s_sh[g].wait(eng, i)
                        s_msg.wait(eng, i, k - 1)
                        s_dot.wait(eng, i, k)
                        k2 = own(eng.tensor_tensor(qd[:, :, :], dots[:, k % 4, :, 0, :], dots[:, k % 4, :, 1, :], ALU.add))
                        dv.wait(eng, i, k2)
                        k3 = own(eng.tensor_tensor(qd[:, :, :], qd[:, :, :], dots[:, k % 4, :, 2, :], ALU.add))
                        s_ts.wait(eng, i, k)
                        k4 = own(eng.tensor_tensor(p1[:, :, :], x0, w[:, :, 1, :], ALU.mult))
                        dv.wait(eng, i, k3)
                        k5 = own(eng.tensor_tensor(qd[:, :, :], qd[:, :, :], w[:, :, 3, :], ALU.mult))
                        dv.wait(eng, i, k4)
                        k6 = own(eng.tensor_tensor(msg[:, b, :, 1:4, :], bc(p1[:, :, :], 2, [P, 4, 3, C]), s1, ALU.mult))
                        k7 = own(eng.tensor_tensor(tmp[:, :, :, :], x1, bc(t02[:, half, :, 1, :], 2, [P, 4, 3, C]), ALU.mult))
                        k8 = own(eng.tensor_tensor(msg[:, b, :, 0, :], x0, t02[:, half, :, 0, :], ALU.mult))
                        dv.wait(eng, i, k7)
                        eng.tensor_tensor(msg[:, b, :, 1:4, :], msg[:, b, :, 1:4, :], tmp[:, :, :, :], ALU.add)
                        dv.wait(eng, i, k8)
                        eng.tensor_tensor(msg[:, b, :, 0, :], msg[:, b, :, 0, :], qd[:, :, :], ALU.add).then_inc(s_msg.sem, 1)
                    assert n == dv.per


def stitch(nc, q, sums, cw, name):
    V, S, G, TE, SP, sb, pb = q.V, q.S, q.G, q.TE, q.SP, q.sb, q.pb
    gat = cw > D
    base, skip = (sums, 0) if gat else (q.sums0_x, q.spare)
    t = Turns(q.sem("t_" + name), q.sem("t_" + name + "_pool"))
    heads_in = Turns(q.sem("t_hd_" + name), q.sem("t_hd_" + name + "_pool"))
    CK = T // 4
    with ExitStack() as c:
        tl, hd, cp = (sb(c, f"{n}_{name}", [TP, TG, cw]) for n in ("tl", "hd", "cp"))
        tT = sb(c, "tT_" + name, [P, 2, T])
        cb = sb(c, "cb_" + name, [P, 2, 1 + T])
        ps = [pb(c, f"ps{k}_{name}", [P, 4, P]) for k in range(2)]
        t.dma(SP, lambda: SP.dma_start(tl[:, :, :], sums.rearrange("(g p e) c -> p g e c", p=TP, e=P)[:, :, P - 1, :]))
        heads_in.pool_dma(G, [lambda g=g: G.indirect_dma_start(out=hd[:, g, :], out_offset=None, in_=base,
                   element_offset=skip, in_offset=bass.IndirectOffsetOnAxis(ap=q.head_idx[:, g:g + 1], axis=0)) for g in range(TG)])
        def groups(w, to_psum, from_psum):
            for g0 in range(0, TG, 2 * w):
                sets = [range(g, min(g + w, TG)) for g in (g0, g0 + w) if g < TG]
                t.step(TE, *[m for x, gs in enumerate(sets) for g in gs for m in to_psum(ps[x], g, g - gs[0])])
                for x, gs in enumerate(sets):
                    t.step(V, *[m for g in gs for m in from_psum(ps[x], g, g - gs[0])])

        groups(2, lambda p, g, y: [lambda j=j: TE.transpose(p[:, 2 * y + j, 0:TP], tl[:, g, j * P:(j + 1) * P], q.ident[:TP, :TP])
                                   for j in range(2)],
               lambda p, g, y: [lambda: V.tensor_copy(tT[:, :, g * TP:(g + 1) * TP], p[:, 2 * y:2 * y + 2, 0:TP])])
        t.step(V, lambda: V.memset(cb[:, :, 0:1], 0.0))
        if gat:
            dT, mT, al, gm = (sb(c, f"{n}_{name}", [H, T]) for n in ("dT", "mT", "al", "gm"))
            cd, cm = (sb(c, f"{n}_{name}", [H, 1 + T]) for n in ("cd", "cm"))
            gB = sb(c, "gB_" + name, [P, 2, T])
            hs = sb(c, "hs_" + name, [H, D])
            groups(2, lambda p, g, y: [lambda j=j: TE.transpose(p[:H, 2 * y + j, 0:TP], tl[:, g, D + j * H:D + (j + 1) * H], q.ident[:TP, :TP])
                                       for j in range(2)],
                   lambda p, g, y: [lambda: V.tensor_copy(dT[:, g * TP:(g + 1) * TP], p[:H, 2 * y, 0:TP]),
                                    lambda: V.tensor_copy(mT[:, g * TP:(g + 1) * TP], p[:H, 2 * y + 1, 0:TP])])
            t.step(V, lambda: V.tensor_scalar(gm[:, :], q.whole[:H, :], BIG, -BIG, ALU.mult, ALU.add),
                   lambda: V.memset(cd[:, 0:1], 0.0), lambda: V.memset(cm[:, 0:1], -BIG))
            t.step(V, lambda: V.tensor_tensor_scan(cm[:, 1:], gm[:, :], mT[:, :], -BIG, ALU.add, ALU.max))
            t.step(V, lambda: V.tensor_tensor(al[:, :], mT[:, :], cm[:, 1:], ALU.subtract),
                   lambda: V.tensor_tensor(gm[:, :], cm[:, 0:T], cm[:, 1:], ALU.subtract))
            t.step(V, lambda: V.tensor_scalar(gm[:, :], gm[:, :], 0.0, None, ALU.min))
            t.step(S, lambda: S.activation(al[:, :], al[:, :], ACT.Exp), lambda: S.activation(gm[:, :], gm[:, :], ACT.Exp))
            t.step(V, lambda: V.tensor_tensor(gm[:, :], gm[:, :], q.whole[:H, :], ALU.mult))
            t.step(V, lambda: V.tensor_tensor(dT[:, :], dT[:, :], al[:, :], ALU.mult))
            t.step(V, lambda: V.tensor_tensor_scan(cd[:, 1:], gm[:, :], dT[:, :], 0.0, ALU.mult, ALU.add))
            t.step(V, lambda: V.tensor_copy(hs[:, :].rearrange("h (k c) -> h k c", c=C), bc(q.ident[:H, :H], 2, [H, H, C])))
            pf = pb(c, "pf_" + name, [P, 6, 512])
            made = Signal(q.sem("spread_" + name), per=2)
            used = Signal(q.sem("spread_used_" + name), per=1, ahead=3)
            t.wait(TE)
            t.wait(V)
            used.prime(V)
            chunks = [(j, x, slice(x * CK, (x + 1) * CK)) for j in range(2) for x in range(4)]
            for n, (j, x, xs) in enumerate(chunks):
                used.wait(TE, n, back=2)
                for k, factor in enumerate((al, gm)):
                    TE.matmul(pf[:, 2 * (n % 3) + k, 0:CK], hs[:, j * P:(j + 1) * P], factor[:, xs],
                              start=True, stop=True).then_inc(made.sem, 1)
            for n, (j, x, xs) in enumerate(chunks):
                made.wait(V, n)
                V.tensor_tensor(tT[:, j, xs], tT[:, j, xs], pf[:, 2 * (n % 3), 0:CK], ALU.mult)
                V.tensor_copy(gB[:, j, xs], pf[:, 2 * (n % 3) + 1, 0:CK]).then_inc(used.sem, 1)
            used.wait(V, len(chunks) - 1)
            t.step(V, *[lambda j=j: V.tensor_tensor_scan(cb[:, j, 1:], gB[:, j, :], tT[:, j, :], 0.0, ALU.mult, ALU.add)
                        for j in range(2)])
        else:
            t.step(V, *[lambda j=j: V.tensor_tensor_scan(cb[:, j, 1:], q.whole[:, :], tT[:, j, :], 0.0, ALU.mult, ALU.add)
                        for j in range(2)])
        xs = lambda g: slice(g * TP, (g + 1) * TP)
        groups(2, lambda p, g, y: [lambda j=j: TE.transpose(p[:TP, 2 * y + j, :], cb[:, j, xs(g)], q.ident[:, :]) for j in range(2)],
               lambda p, g, y: [lambda: V.tensor_copy(cp[:, g, 0:D].rearrange("p (j c) -> p j c", j=2), p[:TP, 2 * y:2 * y + 2, :])])
        if gat:
            groups(2, lambda p, g, y: [lambda j=j, m=m: TE.transpose(p[:TP, 2 * y + j, 0:H], m[:, xs(g)], q.ident[:H, :H])
                                       for j, m in enumerate((cd, cm))],
                   lambda p, g, y: [lambda: V.tensor_copy(cp[:, g, D:GR].rearrange("p (j c) -> p j c", j=2), p[:TP, 2 * y:2 * y + 2, 0:H])])
        heads_in.wait(V)
        if gat:
            mx = sb(c, "mx_" + name, [TP, TG, H])
            heads = lambda x: x[:, :, 0:D].rearrange("p g (h c) -> p g h c", c=C)
            t.step(V, lambda: V.tensor_tensor(mx[:, :, :], hd[:, :, D + H:GR], cp[:, :, D + H:GR], ALU.max))
            for x in (hd, cp):
                t.step(V, lambda x=x: V.tensor_tensor(x[:, :, D + H:GR], x[:, :, D + H:GR], mx[:, :, :], ALU.subtract))
                t.step(S, lambda x=x: S.activation(x[:, :, D + H:GR], x[:, :, D + H:GR], ACT.Exp))
                t.step(V, *[lambda x=x, g=g: V.tensor_tensor(heads(x)[:, g, :, :], heads(x)[:, g, :, :],
                                                             bc(x[:, g, D + H:GR], 2, [TP, H, C]), ALU.mult) for g in range(TG)],
                       lambda x=x: V.tensor_tensor(x[:, :, D:D + H], x[:, :, D:D + H], x[:, :, D + H:GR], ALU.mult))
        t.step(V, lambda: V.tensor_tensor(hd[:, :, :], hd[:, :, :], cp[:, :, :], ALU.add))
        t.pool_dma(G, [lambda g=g: G.indirect_dma_start(out=base, element_offset=skip, out_offset=bass.IndirectOffsetOnAxis(ap=q.fix_idx[:, g:g + 1], axis=0),
                                                    in_=hd[:, g, :], in_offset=None, bounds_check=EP - 1, oob_is_err=False)
                   for g in range(TG)])
        t.end(nc)


def node_rows(t, q, base, skip, i, ixn, rows, beside=()):
    V, G = q.V, q.G
    t.step(V, lambda: V.tensor_copy(ixn[:, :], q.row_idx[:, bass.ds(i * NB, NB)]))
    t.pool_dma(G, [lambda k=k: G.indirect_dma_start(out=rows[:, k, :], out_offset=None, in_=base, element_offset=skip,
               in_offset=bass.IndirectOffsetOnAxis(ap=ixn[:, k:k + 1], axis=0)) for k in range(NB)], q.SP, beside)


def layer0_update(nc, q):
    V, S, G, TE, SP, a, sb, pb = q.V, q.S, q.G, q.TE, q.SP, q.a, q.sb, q.pb
    chains = [Turns(q.sem(f"t_upd{k}"), q.sem(f"t_upd{k}_pool")) for k in range(K)]
    t0 = chains[0]
    with ExitStack() as c:
        wl = sb(c, "wl", [P, 2, C])
        ws = sb(c, "ws", [P, 2, C])
        wc = sb(c, "wc", [C, 9])
        gmm = sb(c, "gmm", [C, 3])
        bst = sb(c, "bst", [C, FULL + 1, 6])
        ss = sb(c, "ss", [C, 3, FULL + 1])
        mv = sb(c, "mv_u", [C, 2])

        def chain(t):
            ixn = sb(c, "ixn", [P, NB], I32)
            rows = sb(c, "rows", [P, NB, D])
            gT = sb(c, "gT", [P, 2, W])
            sq = sb(c, "sq", [C, 3, W])
            a0, a0s, pp, rr, vv = (sb(c, n, [C, W]) for n in ("a0", "a0s", "pp", "rr", "vv"))
            bh = sb(c, "bh", [P, 4, W])
            oT = sb(c, "oT", [C, 4, W])
            banks = [pb(c, "bank", [P, 2, W]) for _ in range(2)]
            pG = [b[:, 0, :] for b in banks]
            pA = pO = [banks[pl % 2][:C, pl // 2, :] for pl in range(4)]

            def body(i, width=W):
                node_rows(t, q, q.sums0_x, q.spare, i, ixn, rows,
                          [lambda: SP.dma_start(bh[C:P, :, :], q.hT_d[:, :, bass.ds(i * W, W)])])
                t.step(V, lambda: V.tensor_tensor(rows[:, :, :], rows[:, :, :], bc(q.some[:, bass.ds(i * NB, NB)], 2, [P, NB, D]), ALU.mult))
                t.step(TE, *[lambda j=j, k=k: TE.transpose(pG[j][:, k * P:(k + 1) * P], rows[:, k, j * P:(j + 1) * P], q.ident[:, :])
                             for j in range(2) for k in range(NB)])
                t.step(S, *[lambda j=j: S.activation(gT[:, j, :], pG[j], ACT.Copy) for j in range(2)])
                t.step(TE, *[lambda pl=pl: TE.matmul(pA[pl], wl[C * (pl % 2):C * (pl % 2) + C, min(pl, 1), :],
                                                     gT[C * (pl % 2):C * (pl % 2) + C, pl // 2, :], start=True, stop=True) for pl in range(4)])
                t.step(S, lambda: S.activation(a0[:, :], pA[0], ACT.Copy),
                       lambda: S.activation(a0s[:, :], pA[0], ACT.Square),
                       *[lambda x=x: S.activation(sq[:, x, :], pA[1 + x], ACT.Square) for x in range(3)])
                tt = lambda o, x, y, op: t.step(V, lambda: V.tensor_tensor(o, x, y, op))
                stt = lambda o, x, w, y: lambda: V.scalar_tensor_tensor(o, x, wc[:, w:w + 1], y, ALU.mult, ALU.add)
                t.step(V, lambda: V.tensor_scalar(pp[:, :], a0s[:, :], wc[:, 3:4], wc[:, 0:1], ALU.mult, ALU.add),
                       lambda: V.tensor_scalar(rr[:, :], a0s[:, :], wc[:, 7:8], wc[:, 5:6], ALU.mult, ALU.add),
                       lambda: V.tensor_tensor(vv[:, :], sq[:, 0, :], sq[:, 1, :], ALU.add))
                t.step(V, stt(pp[:, :], a0[:, :], 1, pp[:, :]), stt(rr[:, :], a0[:, :], 6, rr[:, :]),
                       lambda: V.tensor_tensor(vv[:, :], vv[:, :], sq[:, 2, :], ALU.add))
                t.step(V, stt(pp[:, :], vv[:, :], 4, pp[:, :]), stt(rr[:, :], vv[:, :], 8, rr[:, :]))
                tt(pp[:, :], pp[:, :], a0[:, :], ALU.mult)
                t.step(V, stt(bh[0:C, 0, :], vv[:, :], 2, pp[:, :]),
                       *[lambda x=x: V.tensor_tensor(bh[0:C, 1 + x, :], rr[:, :], pA[1 + x], ALU.mult) for x in range(3)])
                t.step(TE, *[lambda pl=pl: TE.matmul(pO[pl], ws[:, min(pl, 1), :], bh[:, pl, :], start=True, stop=True) for pl in range(4)])
                if width:
                    t.step(V, lambda: V.bn_stats(bst[:, bass.ds(i, 1), :].rearrange("p a b -> p (a b)"), pO[0][:, 0:width]))
                    t.step(S, *[lambda x=x: S.activation(sq[:, x, 0:width], pO[1 + x][:, 0:width], ACT.Square,
                                                         accum_out=ss[:, x, bass.ds(i, 1)]) for x in range(3)])
                t.step(S, *[lambda pl=pl: S.activation(oT[:, pl, :], pO[pl], ACT.Copy) for pl in range(4)])
                t.dma(SP, lambda: SP.dma_start(q.oT_d[:, :, bass.ds(i * W, W)], oT[:, :, :]))
            return body

        bodies = [chain(t) for t in chains]
        t0.dma(SP, *[lambda h=h, n=n: SP.dma_start(wl[h * C:(h + 1) * C, n, :], a[f"L0_gnn_W_lin{n}"]) for h in range(2) for n in range(2)],
               *[lambda h=h, n=n, v=v: SP.dma_start(ws[h * C:(h + 1) * C, n, :], a[f"L0_gnn_{v}{n}"]) for h, v in enumerate(("WB", "Wsc")) for n in range(2)],
               lambda: SP.dma_start(wc[:, 0:5], a["L0_gnn_Wc0"]), lambda: SP.dma_start(wc[:, 5:9], a["L0_gnn_Wc1"]),
               *[lambda k=k, n=n: SP.dma_start(gmm[:, k:k + 1], a["L0_gnn_" + n].unsqueeze(1)) for k, n in enumerate(("gamma0", "beta0", "gamma1"))])
        t0.end(nc)
        chains_loop(nc, chains, FULL // K, bodies)
        for g0 in range(FULL, NG, K):
            side_by_side([queued(t, lambda g: bodies[g - g0](g, LAST if g == FULL else 0), g0 + k) for k, t in enumerate(chains)])
        for t in chains:
            t.end(nc)
        t = t0
        t.step(V, lambda: V.bn_aggr(mv[:, :], bst[:, :, :].rearrange("p a b -> p (a b)")))
        t.step(V, lambda: V.tensor_reduce(q.stat[:, 3:4], ss[:, :, :].rearrange("p a b -> p (a b)"), mybir.AxisListType.X, ALU.add))
        t.step(S, lambda: S.activation(q.stat[:, 0:1], mv[:, 1:2], ACT.Sqrt, bias=q.eps_c[:C, 0:1]),
               lambda: S.activation(q.stat[:, 2:3], q.stat[:, 3:4], ACT.Sqrt, scale=1.0 / (3.0 * N), bias=q.eps_c[:C, 0:1]))
        t.step(V, lambda: V.reciprocal(q.stat[:, 0:1], q.stat[:, 0:1]), lambda: V.reciprocal(q.stat[:, 2:3], q.stat[:, 2:3]))
        t.step(V, lambda: V.tensor_tensor(q.stat[:, 0:3:2], q.stat[:, 0:3:2], gmm[:, 0:3:2], ALU.mult))
        t.step(V, lambda: V.tensor_tensor(q.stat[:, 1:2], mv[:, 0:1], q.stat[:, 0:1], ALU.mult))
        t.step(V, lambda: V.tensor_tensor(q.stat[:, 1:2], gmm[:, 1:2], q.stat[:, 1:2], ALU.subtract))
        t.end(nc)


class Features:

    @staticmethod
    def weights(t, q, c, n):
        V, SP, a = q.V, q.SP, q.a
        w = q.sb(c, "we", [P, 2, D + 2 * H])
        alr = q.sb(c, "alr", [P, 2, D])
        wt = q.sb(c, "wt", [P, 2, D])
        t.dma(SP, lambda: SP.dma_start(w[:, :, 0:D], a[f"L1_gnn_W{n}"].rearrange("(j p) c -> p j c", p=P)),
              *[lambda k=k, v=v: SP.dma_start(alr[:, k, :], a[f"L1_gnn_{v}{n}"].rearrange("h c -> (h c)").partition_broadcast(P))
                for k, v in enumerate(("al", "ar"))])
        for k in range(2):
            t.step(V, lambda k=k: V.tensor_tensor(wt[:, :, :], w[:, :, 0:D], bc(alr[:, k, :], 1, [P, 2, D]), ALU.mult))
            t.step(V, lambda k=k: V.tensor_reduce(w[:, :, D + k * H:D + (k + 1) * H],
                                                  wt[:, :, :].rearrange("p j (h c) -> p j h c", c=C), mybir.AxisListType.X, ALU.add))
        return w

    def __init__(self, t, q, c, w, banks):
        self.t, self.q, self.w = t, q, w
        self.hT = q.sb(c, "hT_p", [P, 2, W])
        self.f = q.sb(c, "f_p", [P, NB, D + H])
        self.er = q.sb(c, "er_p", [P, NB, H])
        self.ix = q.sb(c, "ix_p", [P, NB], I32)
        self.pZ = [b[:, 0:W] for b in banks]
        self.pF = [b[:, 0:D + 2 * H] for b in banks]

    def emit(self, i, z, func):
        t, q = self.t, self.q
        V, S, TE, SP = q.V, q.S, q.TE, q.SP
        t.step(TE, *[lambda j=j, k=k: TE.transpose(self.pZ[j][:, k * P:(k + 1) * P], z[:, k, j * P:(j + 1) * P], q.ident[:, :])
                     for j in range(2) for k in range(NB)])
        t.step(S, *[lambda j=j: S.activation(self.hT[:, j, :], self.pZ[j], func) for j in range(2)])
        t.step(TE, *[lambda j=j, k=k: TE.matmul(self.pF[k], self.hT[:, j, k * P:(k + 1) * P], self.w[:, j, :],
                                                start=j == 0, stop=j == 1) for k in range(NB) for j in range(2)])
        t.step(S, *[lambda k=k: S.activation(self.f[:, k, :], self.pF[k][:, 0:D + H], ACT.Copy) for k in range(NB)],
               *[lambda k=k: S.activation(self.er[:, k, :], self.pF[k][:, D + H:], ACT.Copy) for k in range(NB)])
        rows = lambda x: x.rearrange("(i k p) d -> i p k d", k=NB, p=P)[i, :, :, :]
        t.step(V, lambda: V.tensor_copy(self.ix[:, :], q.first_idx[:, bass.ds(i * NB, NB)]))
        t.pool_dma(q.G, [lambda k=k: q.G.indirect_dma_start(
            out=q.er_start, out_offset=bass.IndirectOffsetOnAxis(ap=self.ix[:, k:k + 1], axis=0),
            in_=self.er[:, k, :], in_offset=None, bounds_check=EP - 1, oob_is_err=False) for k in range(NB)],
            SP, [lambda: SP.dma_start(rows(q.table1), self.f[:, :, :]), lambda: SP.dma_start(rows(q.er_d), self.er[:, :, :])])


def layer0_norm_and_gat_nodes(nc, q):
    V, S, G, TE, SP, a, sb, pb = q.V, q.S, q.G, q.TE, q.SP, q.a, q.sb, q.pb
    chains = [Turns(q.sem(f"t_n1_{k}"), q.sem(f"t_n1_{k}_pool")) for k in range(K)]
    rows = lambda y, i: y.rearrange("(i k p) d -> i p k d", k=NB, p=P)[i, :, :, :]
    with ExitStack() as c:
        w = Features.weights(chains[0], q, c, 1)
        chains[0].end(nc)

        def chain(t):
            oT = sb(c, "oT_n", [C, 4, W])
            x, z = sb(c, "x_n", [P, NB, D]), sb(c, "z_n", [P, NB, D])
            st, mv, rs = sb(c, "st_n", [P, NB, 6]), sb(c, "mv_n", [P, NB, 2]), sb(c, "rs_n", [P, NB])
            banks = [pb(c, "bank", [P, 4 * P]) for _ in range(NB)]
            pN = banks[0][:, :].rearrange("p (k a c) -> p k a c", k=NB, c=C)
            ft = Features(t, q, c, w, banks)

            def body(i):
                t.dma(SP, lambda: SP.dma_start(oT[:, :, :], q.oT_d[:, :, bass.ds(i * W, W)]),
                      lambda: SP.dma_start(x[:, :, :], rows(a["x"], i)))
                t.step(S, lambda: S.activation(oT[:, 0, :], oT[:, 0, :], ACT.Identity, scale=q.stat[:, 0:1], bias=q.stat[:, 1:2]),
                       lambda: S.activation(oT[:, 1:4, :], oT[:, 1:4, :], ACT.Copy, scale=q.stat[:, 2:3]))
                t.step(TE, *[lambda k=k, pl=pl: TE.transpose(pN[:, k, pl, :], oT[:, pl, k * P:(k + 1) * P], q.ident[:C, :C])
                             for k in range(NB) for pl in range(4)])
                t.step(V, *[lambda k=k: V.tensor_tensor(x[:, k, 0:C], x[:, k, 0:C], pN[:, k, 0, :], ALU.add) for k in range(NB)],
                       *[lambda k=k: V.tensor_tensor(x[:, k, C:D].rearrange("p (c x) -> p x c", x=3),
                                                     x[:, k, C:D].rearrange("p (c x) -> p x c", x=3),
                                                     pN[:, k, 1:4, :], ALU.add) for k in range(NB)])
                t.dma(SP, lambda: SP.dma_start(rows(q.x1_d, i), x[:, :, :]))
                norm_rows(t, V, S, q, x, z, st, mv, rs)
                ft.emit(i, z, ACT.Relu)
            return body

        chains_loop(nc, chains, NG // K, [chain(t) for t in chains])
        for t in chains:
            t.end(nc)


def spread_er(nc, q, n):
    V, S, G, TE, SP, a, sb, pb = q.V, q.S, q.G, q.TE, q.SP, q.a, q.sb, q.pb
    t = Turns(q.sem(f"t_er{n}"), q.sem(f"t_er{n}_pool"))
    with ExitStack() as c:
        ch, held = sb(c, "ch", [P, CH, H]), sb(c, "held", [P, H, CH])
        ini = sb(c, "ini", [P, H])
        t.pool_dma(G, [lambda: G.indirect_dma_start(out=ini[:, :], out_offset=None, in_=q.er_d,
                                              in_offset=bass.IndirectOffsetOnAxis(ap=q.chunk_node[:, 0:1], axis=0))])
        t.dma(SP, lambda: SP.dma_start(ch[:, :, :].rearrange("p e h -> p (e h)"), q.er_start.rearrange("(p e) h -> p (e h)", p=P)))
        t.step(V, *[lambda h=h: V.tensor_tensor_scan(held[:, h, :], q.samep[:, :], ch[:, :, h], ini[:, h:h + 1], ALU.mult, ALU.add)
                    for h in range(H)])
        t.dma(SP, lambda: SP.dma_start(q.er_edge.rearrange("h (p e) -> p h e", p=P), held[:, :, :]))
        t.end(nc)


def gat_edges(nc, q, n):
    a, sb, pb = q.a, q.sb, q.pb
    FR = D + H
    NQ = SBT // 4
    with ExitStack() as c:
        er = sb(c, f"er_g{n}", [P, SB, P])
        ix = sb(c, f"ix_g{n}", [P, 2, SBT], I32)
        gb = sb(c, f"gb_g{n}", [P, 2, SBT, FR])
        elc = sb(c, f"elc{n}", [P, H, SBT])
        fs, mm_, ee, ww = (sb(c, f"{x}{n}", [P, P]) for x in ("fs", "mm_", "ee", "ww"))
        mT = sb(c, f"mT_g{n}", [P, 2, SBT, H])
        sel = sb(c, f"sel_g{n}", [P, 2, 4, P])
        ost = sb(c, f"ost_g{n}", [P, 2, 4, GR])
        pE = pb(c, f"pE{n}", [P, P])
        pW = pb(c, f"pW{n}", [P, 2, P])
        po = [pb(c, f"po{k}_{n}", [P, 2, 512]) for k in range(2)]

        nm = lambda x: f"{x}_g{n}"
        s_er = q.sem(nm("er"))
        s_ix = [Signal(q.sem(nm(f"ix{p}")), inc=16) for p in range(2)]
        s_g = [Signal(q.sem(nm(f"g{p}")), per=SBT, inc=16) for p in range(2)]
        s_elc = Signal(q.sem(nm("elc")))
        s_elT = Signal(q.sem(nm("elT")))
        s_d = Signal(q.sem(nm("d")))
        s_w = Signal(q.sem(nm("w")))
        s_wT = Signal(q.sem(nm("wT")))
        s_we = Signal(q.sem(nm("we")))
        s_msg = Signal(q.sem(nm("msg")), per=NQ)
        s_sum = Signal(q.sem(nm("sum")), per=2 * NQ, ahead=2)
        s_ev = Signal(q.sem(nm("ev")), per=2 * NQ, ahead=1)
        s_st = [Signal(q.sem(nm(f"st{p}")), per=NQ // 2, inc=16, ahead=1) for p in range(2)]
        dv = Signal(q.sem(nm("dv")), per=6)
        out_v = q.sums1.rearrange("(b j p) c -> b p j c", j=4, p=P)

        def over(eng, body, first=None):
            if first:
                first()
            with eng.Fori(0, SB // 2) as i:
                for p in range(2):
                    body(i * 2 + p, i, p, False)
            body(SB - 1, SB // 2, 0, True)

        assert SB % 2 == 1
        PREP = (NQ - 2, NQ - 1)

        with nc.Block() as block:
            @block.sync
            def _(eng):
                for s in s_st:
                    s.prime(eng)
                view = q.er_edge.rearrange("h (s t e) -> h t s e", t=SBT, e=P)
                for h in range(H):
                    eng.dma_start(er[h * SBT:(h + 1) * SBT, :, :], view[h, :, :, :]).then_inc(s_er, 16)

                def indices(s, p):
                    eng.dma_start(ix[:, p, :].rearrange("p (g j) -> p g j", j=8),
                                  a["src_cols"].rearrange("(s g) p j -> s p g j", g=4)[s, :, :, :]).then_inc(s_ix[p].sem, 16)

                def body(s, i, p, last):
                    if not last:
                        s_sum.wait(eng, s, 1)
                        eng.nop(nofuse=True)
                        indices(i * 2 + (p + 2), p)
                    for k in range(1, NQ + 1):
                        s_ev.wait(eng, s, 2 * k)
                        eng.nop(nofuse=True)
                        eng.dma_start(out_v[s * NQ + (k - 1), :, :, :], ost[:, k % 2, :, :]).then_inc(s_st[k % 2].sem, 16)

                def first():
                    indices(0, 0)
                    indices(1, 1)

                over(eng, body, first)
                s_ix[1].wait(eng, SB // 2)
                for s in s_st:
                    s.wait(eng, SB - 1)

            @block.gpsimd
            def _(eng):
                def body(s, i, p, last):
                    s_ix[p].wait(eng, i)
                    for k in range(1, NQ + 1):
                        s_sum.wait(eng, s, 2 * k, back=2)
                        eng.nop(nofuse=True)
                        for j in range(4 * k - 4, 4 * k):
                            eng.indirect_dma_start(out=gb[:, p, j, :], out_offset=None, in_=q.table1[:, :],
                                                   in_offset=bass.IndirectOffsetOnAxis(ap=ix[:, p, j:j + 1], axis=0)).then_inc(s_g[p].sem, 16)
                over(eng, body)

            @block.tensor
            def _(eng):
                s_sum.prime(eng)

                def el_rows(s):
                    s_elc.wait(eng, s)
                    eng.transpose(pE[:, :], elc[:, :, :].rearrange("p h t -> p (h t)"), q.ident[:, :]).then_inc(s_elT.sem, 1)

                def weights_back(s):
                    s_w.wait(eng, s)
                    eng.transpose(pW[:, 0, :], ww[:, :], q.ident[:, :])
                    eng.transpose(pW[:, 1, :], mm_[:, :], q.ident[:, :]).then_inc(s_wT.sem, 1)

                def first():
                    el_rows(0)
                    weights_back(0)

                def body(s, i, p, last):
                    for k in range(1, NQ + 1):
                        s_msg.wait(eng, s, k)
                        for x in range(2):
                            s_ev.wait(eng, s, 2 * k + x - 3)
                            for j in range(2):
                                tl = 4 * (k - 1) + 2 * x + j
                                ins = eng.matmul(po[x][:, j, 0:FR], sel[:, k % 2, 2 * x + j, :], gb[:, p, tl, :], start=True, stop=True)
                            ins.then_inc(s_sum.sem, 1)
                        if k in PREP and not last:
                            (el_rows, weights_back)[PREP.index(k)](s + 1)
                over(eng, body, first)

            @block.scalar
            def _(eng):
                s_ev.prime(eng)

                def el_side_by_side(s, i, p):
                    s_g[p].wait(eng, i)
                    eng.activation(elc[:, :, :], gb[:, p, :, D:FR].rearrange("p t h -> p h t"), ACT.Copy).then_inc(s_elc.sem, 1)
                    s_d.wait(eng, s)
                    eng.activation(ww[:, :], ee[:, :], ACT.Exp).then_inc(s_w.sem, 1)

                def weights_in_place(s, i, p):
                    s_wT.wait(eng, s)
                    view = lambda k: pW[:, k, :].rearrange("p (h t) -> p t h", t=SBT)
                    eng.activation(gb[:, p, :, D:FR], view(0), ACT.Copy)
                    eng.activation(mT[:, p, :, :], view(1), ACT.Copy).then_inc(s_we.sem, 1)

                def first():
                    el_side_by_side(0, 0, 0)
                    weights_in_place(0, 0, 0)

                def body(s, i, p, last):
                    s_we.wait(eng, s)
                    for k in range(1, NQ + 1):
                        s_st[k % 2].wait(eng, s, (k + 1) // 2 - 1)
                        for x in range(2):
                            tl = 4 * (k - 1) + 2 * x
                            eng.activation(ost[:, k % 2, 2 * x:2 * x + 2, FR:GR], mT[:, p, tl:tl + 2, :], ACT.Copy)
                            s_sum.wait(eng, s, 2 * k + x - 1)
                            eng.activation(ost[:, k % 2, 2 * x:2 * x + 2, 0:FR], po[x][:, :, 0:FR], ACT.Copy).then_inc(s_ev.sem, 1)
                        if k in PREP and not last:
                            (el_side_by_side, weights_in_place)[PREP.index(k)](s + 1, i + p, 1 - p)
                over(eng, body, first)

            @block.vector
            def _(eng):
                eng.wait_ge(s_er, 16 * H)

                def weights(s):
                    er_s = er[:, bass.ds(s, 1), :].rearrange("p a e -> p (a e)")
                    f_m, b_m = (m[:, bass.ds(s, 1), :].rearrange("p a e -> p (a e)") for m in (q.start_f, q.start_b))
                    s_elT.wait(eng, s)
                    eng.tensor_tensor_scan(fs[:, :], f_m, pE[:, :], -BIG, ALU.add, ALU.max).then_inc(dv.sem, 1)
                    eng.tensor_tensor(ee[:, :], pE[:, :], er_s, ALU.add).then_inc(dv.sem, 1)
                    dv.wait(eng, s, 1)
                    eng.tensor_tensor_scan(mm_[:, ::-1], b_m, fs[:, ::-1], -BIG, ALU.add, ALU.max).then_inc(dv.sem, 1)
                    dv.wait(eng, s, 2)
                    eng.scalar_tensor_tensor(ee[:, :], ee[:, :], 0.2, ee[:, :], ALU.mult, ALU.max).then_inc(dv.sem, 1)
                    dv.wait(eng, s, 3)
                    eng.tensor_tensor(mm_[:, :], mm_[:, :], er_s, ALU.add).then_inc(dv.sem, 1)
                    dv.wait(eng, s, 5)
                    eng.scalar_tensor_tensor(mm_[:, :], mm_[:, :], 0.2, mm_[:, :], ALU.mult, ALU.max).then_inc(dv.sem, 1)
                    dv.wait(eng, s, 6)
                    eng.tensor_tensor(ee[:, :], ee[:, :], mm_[:, :], ALU.subtract).then_inc(s_d.sem, 1)

                def body(s, i, p, last):
                    s_we.wait(eng, s)
                    for k in range(1, NQ + 1):
                        tl = slice(4 * (k - 1), 4 * k)
                        s_sum.wait(eng, s, 2 * k - 4)
                        eng.tensor_tensor(sel[:, k % 2, :, :], bc(q.lastpos[:, bass.ds(s * SBT + 4 * (k - 1), 4)], 2, [P, 4, P]),
                                          bc(q.iota_f[:, :], 1, [P, 4, P]), ALU.is_equal)
                        f = gb[:, p, tl, 0:D].rearrange("p t (h c) -> p t h c", c=C)
                        eng.tensor_tensor(f, f, bc(gb[:, p, tl, D:FR], 3, [P, 4, H, C]), ALU.mult).then_inc(s_msg.sem, 1)
                        if k == PREP[0] and not last:
                            weights(s + 1)
                over(eng, body, lambda: weights(0))


def gat_output(nc, q, n):
    V, S, G, TE, SP, a, sb, pb = q.V, q.S, q.G, q.TE, q.SP, q.a, q.sb, q.pb
    chains = [Turns(q.sem(f"t_o{n}_{k}"), q.sem(f"t_o{n}_{k}_pool")) for k in range(K)]
    view = lambda y, i: y.rearrange("(i k p) d -> i p k d", k=NB, p=P)[i, :, :, :]
    with ExitStack() as c:
        bias = sb(c, "bias", [P, D])
        chains[0].dma(SP, lambda: SP.dma_start(bias[:, :], a[f"L1_gnn_b{n}"].partition_broadcast(P)))
        w = Features.weights(chains[0], q, c, 2) if n == 1 else None
        chains[0].end(nc)

        def chain(t):
            ixn = sb(c, "ixn", [P, NB], I32)
            rows = sb(c, "rows", [P, NB, GR])
            v, ex = sb(c, "v", [P, NB, D]), sb(c, "ex", [P, NB, D])
            ns, rd = sb(c, "ns", [P, NB]), sb(c, "rd", [P, NB, H])
            x1 = sb(c, "x1", [P, NB, D])
            if n == 1:
                ft = Features(t, q, c, w, [pb(c, "bank", [P, 4 * P]) for _ in range(NB)])

            def body(i):
                node_rows(t, q, q.sums1, 0, i, ixn, rows,
                          [lambda: SP.dma_start(x1[:, :, :], view(q.x1_d, i))] if n == 2 else [])
                some = q.some[:, bass.ds(i * NB, NB)]
                t.step(V, lambda: V.tensor_scalar(ns[:, :], some, -1.0, 1.0, ALU.mult, ALU.add))
                t.step(V, lambda: V.tensor_tensor(rd[:, :, :], rows[:, :, D:D + H], bc(ns[:, :], 2, [P, NB, H]), ALU.add))
                t.step(V, lambda: V.reciprocal(rd[:, :, :], rd[:, :, :]))
                t.step(V, lambda: V.tensor_tensor(rd[:, :, :], rd[:, :, :], bc(some, 2, [P, NB, H]), ALU.mult))
                t.step(V, *[lambda k=k: V.tensor_tensor(v[:, k, :].rearrange("p (h c) -> p h c", c=C),
                                                      rows[:, k, 0:D].rearrange("p (h c) -> p h c", c=C),
                                                      bc(rd[:, k, :], 2, [P, H, C]), ALU.mult) for k in range(NB)])
                t.step(V, lambda: V.tensor_tensor(v[:, :, :], v[:, :, :], bc(bias[:, :], 1, [P, NB, D]), ALU.add))
                t.step(V, lambda: V.tensor_scalar(ex[:, :, :], v[:, :, :], 0.0, None, ALU.min))
                t.step(S, lambda: S.activation(ex[:, :, :], ex[:, :, :], ACT.Exp))
                t.step(V, lambda: V.tensor_scalar(v[:, :, :], v[:, :, :], 0.0, -1.0, ALU.max, ALU.add))
                t.step(V, lambda: V.tensor_tensor(v[:, :, :], v[:, :, :], ex[:, :, :], ALU.add))
                if n == 1:
                    ft.emit(i, v, ACT.Copy)
                else:
                    t.step(V, lambda: V.tensor_tensor(v[:, :, :], v[:, :, :], x1[:, :, :], ALU.add))
                    t.dma(SP, lambda: SP.dma_start(view(q.out, i), v[:, :, :]))
            return body

        chains_loop(nc, chains, NG // K, [chain(t) for t in chains])
        for t in chains:
            t.end(nc)


def kernel(**inputs):
    import numpy as _np
    import concourse.bacc as _bacc
    from concourse import mybir as _mybir
    from concourse.bass_utils import run_bass_kernel_spmd as _run

    x = _np.asarray(inputs["x"])
    src, dst = _np.asarray(inputs["src"]), _np.asarray(inputs["dst"])
    pad = EP - E
    srcp = _np.concatenate([src, _np.zeros(pad + SPARE * 1024, src.dtype)])
    dstp = _np.concatenate([dst, _np.full(pad, N, dst.dtype)])
    rbf = _np.concatenate([_np.asarray(inputs["edge_attr_16"]), _np.zeros((pad + SPARE * 1024, R), _np.float32)])
    sh = _np.concatenate([_np.asarray(inputs["edge_attr_4"]), _np.zeros((pad + SPARE * 1024, 4), _np.float32)])
    arrays = {
        "x": _np.concatenate([x, _np.zeros((NP_ - N, D), x.dtype)]),
        "src_cols": srcp.reshape(EP // 1024 + SPARE, 8, P).transpose(0, 2, 1),
        "dst_rows": dstp.reshape(T, P),
        "dst_line": _np.concatenate([_np.full(1, -1, dst.dtype), dstp, _np.full(1, -2, dst.dtype)]),
        "rbf": rbf.reshape(EP // 1024 + SPARE, 2, HALF, R).transpose(0, 1, 3, 2).reshape(-1, 2 * R, HALF),
        "sh": sh.reshape(EP // 1024 + SPARE, 8, P, 4).transpose(0, 2, 1, 3).reshape(-1, P, 32),
    }
    for k, v in inputs.items():
        if k[:2] in ("L0", "L1"):
            arrays[k] = _np.asarray(v)
    arrays = {k: _np.ascontiguousarray(v) for k, v in arrays.items()}
    nc = _bacc.Bacc("TRN2", target_bir_lowering=False, num_devices=1)
    a = {k: nc.dram_tensor("in_" + k, v.shape, _mybir.dt.from_np(v.dtype), kind="ExternalInput").ap() for k, v in arrays.items()}
    out = nc.dram_tensor("out", (NP_, D), F32, kind="ExternalOutput").ap()
    program(nc, a, out)
    r = _run(nc, [{"in_" + k: v for k, v in arrays.items()}], core_ids=[0])
    return r.results[0]["out"][:N]
```
